# Optimizing a Trainium2 kernel written in Bass

```python
import numpy as np
import jax
import jax.numpy as jnp

def _softmax(x, axis=-1):
    return jax.nn.softmax(x, axis=axis)

def _gelu(x):
    return jax.nn.gelu(x, approximate=True)

def _silu(x):
    return jax.nn.silu(x)

def _sigmoid(x):
    return jax.nn.sigmoid(x)

def _layernorm(x, axis=-1, eps=1e-05):
    m = jnp.mean(x, axis=axis, keepdims=True)
    v = jnp.var(x, axis=axis, keepdims=True)
    return (x - m) / jnp.sqrt(v + eps)

def _scatter_add(tgt, idx, src, axis=0):
    return tgt.at[idx].add(src)

def _segment_sum(src, seg, n):
    return jax.ops.segment_sum(src, seg, n)
kernel_name = 'mk_hybrid_d1_jaxref_r4_faa3c6'

def setup_inputs(seed: int=0):
    np.random.seed(seed)
    _w = jnp.asarray

    def _L0_attn_a_setup():
        import jax, jax.numpy as jnp
        import numpy as np
        B, S, HID, NH = (8, 1024, 256, 16)
        D = HID // NH
        LN_EPS = 1e-05

        def _l2norm(a):
            n = jnp.sqrt(jnp.sum(a * a, axis=-1, keepdims=True))
            return a / jnp.maximum(n, 1e-12)
        key = jax.random.key(seed)
        ks = jax.random.split(key, 8)
        s = 0.02
        x = jax.random.normal(ks[0], (B, S, HID), jnp.float32)
        Wq = jax.random.normal(ks[1], (HID, NH * D), jnp.float32) * s
        Wk = jax.random.normal(ks[2], (HID, NH * D), jnp.float32) * s
        Wv = jax.random.normal(ks[3], (HID, NH * D), jnp.float32) * s
        Wbeta = jax.random.normal(ks[4], (HID, NH), jnp.float32) * s
        Wg = jax.random.normal(ks[5], (HID, NH * D), jnp.float32) * s
        Wout = jax.random.normal(ks[6], (NH * D, HID), jnp.float32) * s
        ln_g = jnp.ones((NH * D,), jnp.float32)
        ln_b = jnp.zeros((NH * D,), jnp.float32)
        return {'x': x, 'Wq': Wq, 'Wk': Wk, 'Wv': Wv, 'Wbeta': Wbeta, 'Wg': Wg, 'Wout': Wout, 'ln_g': ln_g, 'ln_b': ln_b}
    _L0_attn_a_in = _L0_attn_a_setup()

    def _L0_attn_b_setup():
        import jax, jax.numpy as jnp
        import numpy as np
        EMBED_DIM = 256
        key = jax.random.key(seed)
        ks = jax.random.split(key, 9)
        B, S, D = (4, 1024, EMBED_DIM)
        s = 1.0 / np.sqrt(D)
        inp = {'x': jax.random.normal(ks[0], (B, S, D), dtype=jnp.float32)}
        names = ['q', 'k', 'v', 'out']
        for i, n in enumerate(names):
            inp[f'w_{n}'] = jax.random.uniform(ks[1 + 2 * i], (D, D), jnp.float32, -s, s)
            inp[f'b_{n}'] = jax.random.uniform(ks[2 + 2 * i], (D,), jnp.float32, -s, s)
        return inp
    _L0_attn_b_in = _L0_attn_b_setup()

    def _L0_ffn_setup():
        import jax, jax.numpy as jnp
        import numpy as np
        from jax import lax
        T, B, I, M, O = (64, 64, 256, 256, 256)

        def _xavier(key, shape):
            fan_out, fan_in = shape
            limit = float(np.sqrt(6.0 / (fan_in + fan_out)))
            return jax.random.uniform(key, shape, jnp.float32, -limit, limit)
        key = jax.random.key(seed)
        ks = jax.random.split(key, 9)
        x = jax.random.normal(ks[0], (T, B, I), jnp.float32)
        return {'x': x, 'wf': _xavier(ks[1], (M, I)), 'uf': _xavier(ks[2], (M, M)), 'bf': jnp.zeros((M,), jnp.float32), 'wi': _xavier(ks[3], (M, I)), 'ui': _xavier(ks[4], (M, M)), 'bi': jnp.zeros((M,), jnp.float32), 'wc': _xavier(ks[5], (M, I)), 'uc': _xavier(ks[6], (M, M)), 'bc': jnp.zeros((M,), jnp.float32), 'wo': _xavier(ks[7], (O, I)), 'uo': _xavier(ks[8], (O, M)), 'bo': jnp.zeros((O,), jnp.float32), 'in_c': jnp.zeros((M,), jnp.float32)}
    _L0_ffn_in = _L0_ffn_setup()
    _d = {'L0_attn_a_x': _L0_attn_a_in['x'], 'L0_attn_a_Wq': _L0_attn_a_in['Wq'], 'L0_attn_a_Wk': _L0_attn_a_in['Wk'], 'L0_attn_a_Wv': _L0_attn_a_in['Wv'], 'L0_attn_a_Wbeta': _L0_attn_a_in['Wbeta'], 'L0_attn_a_Wg': _L0_attn_a_in['Wg'], 'L0_attn_a_Wout': _L0_attn_a_in['Wout'], 'L0_attn_a_ln_g': _L0_attn_a_in['ln_g'], 'L0_attn_a_ln_b': _L0_attn_a_in['ln_b'], 'L0_attn_b_w_q': _L0_attn_b_in['w_q'], 'L0_attn_b_b_q': _L0_attn_b_in['b_q'], 'L0_attn_b_w_k': _L0_attn_b_in['w_k'], 'L0_attn_b_b_k': _L0_attn_b_in['b_k'], 'L0_attn_b_w_v': _L0_attn_b_in['w_v'], 'L0_attn_b_b_v': _L0_attn_b_in['b_v'], 'L0_attn_b_w_out': _L0_attn_b_in['w_out'], 'L0_attn_b_b_out': _L0_attn_b_in['b_out'], 'L0_ffn_wf': _L0_ffn_in['wf'], 'L0_ffn_uf': _L0_ffn_in['uf'], 'L0_ffn_bf': _L0_ffn_in['bf'], 'L0_ffn_wi': _L0_ffn_in['wi'], 'L0_ffn_ui': _L0_ffn_in['ui'], 'L0_ffn_bi': _L0_ffn_in['bi'], 'L0_ffn_wc': _L0_ffn_in['wc'], 'L0_ffn_uc': _L0_ffn_in['uc'], 'L0_ffn_bc': _L0_ffn_in['bc'], 'L0_ffn_wo': _L0_ffn_in['wo'], 'L0_ffn_uo': _L0_ffn_in['uo'], 'L0_ffn_bo': _L0_ffn_in['bo'], 'L0_ffn_in_c': _L0_ffn_in['in_c']}
    _x0 = _d['L0_attn_a_x']
    _d['L0_attn_a_x'] = jax.random.normal(jax.random.fold_in(jax.random.key(seed), 1), (4, 1024, 256), dtype=_x0.dtype)
    del _x0
    return _d

def reference(L0_attn_a_x, L0_attn_a_Wq, L0_attn_a_Wk, L0_attn_a_Wv, L0_attn_a_Wbeta, L0_attn_a_Wg, L0_attn_a_Wout, L0_attn_a_ln_g, L0_attn_a_ln_b, L0_attn_b_w_q, L0_attn_b_b_q, L0_attn_b_w_k, L0_attn_b_b_k, L0_attn_b_w_v, L0_attn_b_b_v, L0_attn_b_w_out, L0_attn_b_b_out, L0_ffn_wf, L0_ffn_uf, L0_ffn_bf, L0_ffn_wi, L0_ffn_ui, L0_ffn_bi, L0_ffn_wc, L0_ffn_uc, L0_ffn_bc, L0_ffn_wo, L0_ffn_uo, L0_ffn_bo, L0_ffn_in_c):

    def _L0_attn_a_ref(x, Wq, Wk, Wv, Wbeta, Wg, Wout, ln_g, ln_b):
        import jax, jax.numpy as jnp
        import numpy as np
        B, S, HID, NH = (8, 1024, 256, 16)
        D = HID // NH
        LN_EPS = 1e-05

        def _l2norm(a):
            n = jnp.sqrt(jnp.sum(a * a, axis=-1, keepdims=True))
            return a / jnp.maximum(n, 1e-12)
        b, s, _ = x.shape
        nh = Wbeta.shape[1]
        d = Wq.shape[1] // nh
        q = _l2norm((x @ Wq).reshape(b, s, nh, d))
        k = _l2norm((x @ Wk).reshape(b, s, nh, d))
        v = (x @ Wv).reshape(b, s, nh, d)
        beta = jax.nn.sigmoid(x @ Wbeta)
        qT = jnp.moveaxis(q, 1, 0)
        kT = jnp.moveaxis(k, 1, 0)
        vT = jnp.moveaxis(v, 1, 0)
        bT = jnp.moveaxis(beta, 1, 0)
        state0 = jnp.zeros((b, nh, d, d), x.dtype)

        def step(state, inp):
            qt, kt, vt, bt = inp
            kk = kt[..., :, None] * kt[..., None, :]
            bb = bt[..., None, None]
            state = state * (1.0 - bb * kk) + bb * (vt[..., :, None] * kt[..., None, :])
            out_t = jnp.einsum('bhij,bhj->bhi', state, qt)
            return (state, out_t)
        _, outs = jax.lax.scan(step, state0, (qT, kT, vT, bT))
        out = jnp.moveaxis(outs, 0, 1).reshape(b, s, nh * d)
        mu = jnp.mean(out, axis=-1, keepdims=True)
        var = jnp.mean((out - mu) ** 2, axis=-1, keepdims=True)
        out = (out - mu) / jnp.sqrt(var + LN_EPS) * ln_g + ln_b
        out = out * jax.nn.silu(x @ Wg)
        return out @ Wout

    def _L0_attn_b_ref(x, w_q, b_q, w_k, b_k, w_v, b_v, w_out, b_out):
        import jax, jax.numpy as jnp
        import numpy as np
        EMBED_DIM = 256
        D = x.shape[-1]
        scaling = 1.0 / jnp.sqrt(jnp.asarray(D, x.dtype))
        q = jnp.einsum('bsd,ed->bse', x, w_q) + b_q
        k = jnp.einsum('bsd,ed->bse', x, w_k) + b_k
        v = jnp.einsum('bsd,ed->bse', x, w_v) + b_v
        scores = jnp.einsum('bqd,bkd->bqk', q, k) * scaling
        attn = jax.nn.softmax(scores, axis=-1)
        out = jnp.einsum('bqk,bkd->bqd', attn, v)
        return jnp.einsum('bsd,ed->bse', out, w_out) + b_out

    def _L0_ffn_ref(x, wf, uf, bf, wi, ui, bi, wc, uc, bc, wo, uo, bo, in_c):
        import jax, jax.numpy as jnp
        import numpy as np
        from jax import lax
        T, B, I, M, O = (64, 64, 256, 256, 256)

        def _xavier(key, shape):
            fan_out, fan_in = shape
            limit = float(np.sqrt(6.0 / (fan_in + fan_out)))
            return jax.random.uniform(key, shape, jnp.float32, -limit, limit)
        batch = x.shape[1]
        c0 = jnp.broadcast_to(in_c, (batch, in_c.shape[0]))

        def step(c, xt):
            ft = jax.nn.sigmoid(xt @ wf.T + c @ uf.T + bf)
            it = jax.nn.sigmoid(xt @ wi.T + c @ ui.T + bi)
            gt = jnp.tanh(xt @ wc.T + c @ uc.T + bc)
            c = ft * c + it * gt
            return (c, None)
        c_final, _ = lax.scan(step, c0, x)
        h = jnp.tanh(jnp.einsum('tbi,oi->tbo', x, wo) + c_final @ uo.T + bo)
        return h
    x = L0_attn_a_x
    x = x + _L0_attn_a_ref(_layernorm(x, axis=-1), L0_attn_a_Wq, L0_attn_a_Wk, L0_attn_a_Wv, L0_attn_a_Wbeta, L0_attn_a_Wg, L0_attn_a_Wout, L0_attn_a_ln_g, L0_attn_a_ln_b)
    x = x + _L0_ffn_ref(_layernorm(x, axis=-1), L0_ffn_wf, L0_ffn_uf, L0_ffn_bf, L0_ffn_wi, L0_ffn_ui, L0_ffn_bi, L0_ffn_wc, L0_ffn_uc, L0_ffn_bc, L0_ffn_wo, L0_ffn_uo, L0_ffn_bo, L0_ffn_in_c)
    x = x + _L0_attn_b_ref(_layernorm(x, axis=-1), L0_attn_b_w_q, L0_attn_b_b_q, L0_attn_b_w_k, L0_attn_b_b_k, L0_attn_b_w_v, L0_attn_b_b_v, L0_attn_b_w_out, L0_attn_b_b_out)
    x = x + _L0_ffn_ref(_layernorm(x, axis=-1), L0_ffn_wf, L0_ffn_uf, L0_ffn_bf, L0_ffn_wi, L0_ffn_ui, L0_ffn_bi, L0_ffn_wc, L0_ffn_uc, L0_ffn_bc, L0_ffn_wo, L0_ffn_uo, L0_ffn_bo, L0_ffn_in_c)
    return x

_drawn_inputs = setup_inputs


def setup_inputs(seed=0):
    import zlib

    import numpy as np

    out = dict(_drawn_inputs(seed))
    spreads = {'L0_attn_a_ln_g': (1.0, 0.6),
     'L0_attn_a_ln_b': (0.0, 0.8),
     'L0_ffn_bf': (0.0, 0.729),
     'L0_ffn_bi': (0.0, 0.531),
     'L0_ffn_bc': (0.0, 0.1),
     'L0_ffn_bo': (0.0, 0.1),
     'L0_ffn_in_c': (0.0, 0.333)}
    factors = {'L0_attn_a_Wbeta': 7.813,
     'L0_attn_b_w_q': 8.0,
     'L0_attn_b_b_q': 8.0,
     'L0_attn_b_w_k': 8.0,
     'L0_attn_b_b_k': 8.0,
     'L0_attn_b_w_v': 3.366,
     'L0_attn_b_b_v': 3.599}
    for name, (base, spread) in spreads.items():
        noise = np.random.default_rng([zlib.crc32(name.encode()), seed]).standard_normal(out[name].shape)
        drawn = base * np.exp(spread * noise) if base else spread * noise
        out[name] = jnp.asarray(drawn.astype(out[name].dtype))
    for name, factor in factors.items():
        out[name] = (out[name] * factor).astype(out[name].dtype)
    return out
```

```python
from contextlib import ExitStack

import concourse.bass as bass
from concourse import mybir

F32 = mybir.dt.float32
ALU = mybir.AluOpType
ACT = mybir.ActivationFunctionType
AX = mybir.AxisListType

B, S, HID, NH, D = 4, 1024, 256, 16, 16
P = 128
NC = S // P
KT = HID // P
TOK = B * P
HALF = 64
SUB = 32
NS = P // SUB
COL = SUB + 1
ND = D // 2 + 1
NI = D // 2
U = ND * NI
MIR = (ND - 2) * NI
PAIRS = U + MIR
V_, Q_, K_, KB_ = range(4)
NITEM = 2 * 4
SLOTS = 4
EPS = 1e-5
SCALE = 1.0 / 16.0
(LNG, LNB, BF, BI, BC, INC, BQ, BK, BV) = range(0, 18, 2)
DMA = 16


class LayerNorm:

    def __init__(self, sb, sem, name):
        self.stats = sb(f"{name}_stats", [P, B, 6])
        self.mv = sb(f"{name}_mv", [P, B, 2])
        self.rs = sb(f"{name}_rs", [P, B])
        self.last = sb(f"{name}_last", [P, 1])
        self.settled = sem(f"{name}_settled")
        self.stat_done = sem(f"{name}_stat_done")
        self.mv_done = sem(f"{name}_mv_done")
        self.var_done = sem(f"{name}_var_done")
        self.rstd_done = sem(f"{name}_rstd_done")
        self.norm_done = sem(f"{name}_norm_done")


def wait(e, sem, count):
    if not isinstance(count, int) or count > 0:
        e.wait_ge(sem, count)


def block_kernel(nc, x, wqkvg, wbeta, wout, cols, rows, wx, wc, wattn, ident_d, out):
    rs_d = nc.dram_tensor("scan_in_dram", [NC, 2, 4, B, HID, HALF], F32, kind="Internal").ap()
    os_d = nc.dram_tensor("scan_out_dram", [NC, 2, B, NH, D, P], F32, kind="Internal").ap()
    gs_d = nc.dram_tensor("gate_dram", [NC, P, KT * TOK], F32, kind="Internal").ap()
    x2_d = nc.dram_tensor("x2_dram", [B, S, HID], F32, kind="Internal").ap()
    vs_d = nc.dram_tensor("values_dram", [B, S, HID], F32, kind="Internal").ap()
    ks_d = nc.dram_tensor("keys_dram", [KT, P, B, S], F32, kind="Internal").ap()
    x_m = x.rearrange("b (m p) d -> m p b d", p=P)
    x2_m = x2_d.rearrange("b (m p) d -> m p b d", p=P)
    out_m = out.rearrange("b (m p) d -> m p b d", p=P)
    vs_m = vs_d.rearrange("b (m p) d -> m p b d", p=P)
    ks_m = ks_d.rearrange("k p b (m t) -> m k p b t", t=P)
    os_m = os_d.rearrange("m a b h i t -> m a (b h) i t")
    os_f = os_d.rearrange("m a b h i t -> m a (h i) b t")

    with ExitStack() as ctx:
        def sb(name, shape):
            return ctx.enter_context(nc.sbuf_tensor(name, shape, F32))

        def psum(name, shape):
            return ctx.enter_context(nc.psum_tensor(name, shape, F32))

        def sem(name):
            return ctx.enter_context(nc.semaphore(name))

        w_qkvg = sb("w_qkvg", [P, KT, 4 * HID])
        w_beta = sb("w_beta", [P, KT, NH])
        w_out = sb("w_out", [P, KT, HID])
        col = sb("col", [P, 18])
        hcol = sb("hcol", [P, 8])
        row = sb("row", [1, 2 * HID + P])
        w_x = sb("w_x", [P, KT, 4 * HID])
        w_c = sb("w_c", [P, KT, 4 * HID])
        w_g = sb("w_g", [P, KT, HID])
        w_vo = sb("w_vo", [P, KT, HID])
        q_bias = sb("q_bias", [P, 2 * KT])
        qk_const = sb("qk_const", [1, 1])
        y_bias = sb("y_bias", [1, HID])
        ident = sb("ident", [P, P])
        eps4 = sb("eps4", [P, B])
        mhalf = sb("mhalf", [P, P])
        c0 = sb("c0", [P, KT, P])
        xin = sb("xin", [P, B, HID])
        xnT = sb("xnT", [P, KT, TOK])
        qk = sb("qk", [P, B, 2 * HID])
        sq = sb("sq", [P, 2, 2 * HID])
        ss = sb("ss", [P, B * 2 * NH])
        rn = sb("rn", [P, B * 2 * NH])
        bt = sb("bt", [P, B * NH])
        beta = sb("beta", [P, B * NH])
        kb = sb("kb", [P, B, HID])
        stage = sb("stage", [P, SLOTS, TOK])
        gate = sb("gate", [P, KT, TOK])
        lay = sb("lay", [P, 2, 4, D, HALF])
        dec = sb("dec", [P, 2, U, COL])
        st = sb("st", [P, 2, PAIRS, COL])
        ob = sb("ob", [P, 2, D, HALF])
        oH = sb("oH", [P, 2, KT, TOK])
        nrm = sb("nrm", [P, B, HID])
        ogT = sb("ogT", [P, KT, TOK])
        gl = sb("gl", [P, KT, TOK])
        xr = sb("xr", [P, B, HID])
        n2T = sb("n2T", [P, KT, TOK])
        n3T = sb("n3T", [P, KT, TOK])
        gt = sb("gt", [P, 3, KT * P])
        c_init = sb("c_init", [P, KT])
        cc = sb("cc", [P, KT, P])
        hh = sb("hh", [P, 2, 2 * HID])
        keys = lay[:, :, :, :, :].rearrange("p a b c d -> p (a b c d)").rearrange("p (k b s) -> p k b s", k=KT, b=B)
        vals = st[:, :, :, :].rearrange("p a b c -> p (a b c)")[:, 0:B * NC * HID].rearrange(
            "p (b j d) -> p b j d", b=B, j=NC)
        flat = dec[:, :, :, :].rearrange("p a b c -> p (a b c)")
        prob = flat[:, 0:S]
        probT = flat[:, S:2 * S].rearrange("p (j q) -> p j q", j=NC)
        qT = flat[:, 2 * S:3 * S].rearrange("p (k t) -> p k t", k=KT)
        xq = flat[:, 3 * S:4 * S].rearrange("p (k t) -> p k t", k=KT)
        ao = flat[:, 4 * S:4 * S + HID]
        aoT = flat[:, 4 * S + HID:4 * S + 2 * HID].rearrange("p (k t) -> p k t", k=KT)
        w_raw = oH[:, :, :, :].rearrange("p a b c -> p (a b c)").rearrange("p (w k n) -> p w k n", w=4, k=KT)
        mx = sb("mx", [P, 8])
        rq = sb("rq", [P, B])

        PB = psum("PB", [P, 2, 512])
        QB = psum("QB", [P, 2, 512])
        FB = psum("FB", [P, 2, 512])
        JB = psum("JB", [P, 2, 512])

        ln_x = LayerNorm(sb, sem, "ln_x")
        ln_o = LayerNorm(sb, sem, "ln_o")
        ln_2 = LayerNorm(sb, sem, "ln_2")
        ln_3 = LayerNorm(sb, sem, "ln_3")

        w_loaded = sem("w_loaded")
        const_set = sem("const_set")
        dve_const = sem("dve_const")
        x_loaded = sem("x_loaded")
        xT_done = sem("xT_done")
        xT_copied = sem("xT_copied")
        qk_mm = sem("qk_mm")
        sq_done = sem("sq_done")
        qk_copied = sem("qk_copied")
        ss_done = sem("ss_done")
        ssmax_done = sem("ssmax_done")
        rn_done = sem("rn_done")
        beta_mm = sem("beta_mm")
        bt_done = sem("bt_done")
        beta_done = sem("beta_done")
        v_mm = sem("v_mm")
        g_mm = sem("g_mm")
        tg_done = sem("tg_done")
        gate_done = sem("gate_done")
        gate_spilled = sem("gate_spilled")
        qkn_done = sem("qkn_done")
        kb_done = sem("kb_done")
        turn_done = sem("turn_done")
        staged = sem("staged")
        spilled = [sem(f"spilled{i}") for i in range(SLOTS)]
        lay_loaded = [sem(f"lay_loaded{i}") for i in range(2)]
        kk_done = sem("kk_done")
        dec_done = sem("dec_done")
        inp_done = sem("inp_done")
        scan_done = sem("scan_done")
        carried = sem("carried")
        prod_done = sem("prod_done")
        sum_done = sem("sum_done")
        sum_copied = sem("sum_copied")
        ob_spilled = [sem(f"ob_spilled{i}") for i in range(2)]
        o_loaded = sem("o_loaded")
        gl_loaded = sem("gl_loaded")
        xr_loaded = sem("xr_loaded")
        osum_done = sem("osum_done")
        oT_done = sem("oT_done")
        onT_done = sem("onT_done")
        og_done = sem("og_done")
        gated = sem("gated")
        y_mm = sem("y_mm")
        x1_done = sem("x1_done")
        n2t_done = sem("n2t_done")
        n2T_copied = sem("n2T_copied")
        cell_mm = sem("cell_mm")
        cell_act = sem("cell_act")
        cell_h = sem("cell_h")
        c_done = sem("c_done")
        h_mm = sem("h_mm")
        h_act = sem("h_act")
        x2_done = sem("x2_done")
        x2_stored = sem("x2_stored")
        v_stored = sem("v_stored")
        n3t_done = sem("n3t_done")
        n3T_copied = sem("n3T_copied")
        k_stored = sem("k_stored")
        wb_mm = sem("wb_mm")
        wb_done = sem("wb_done")
        keys_loaded = sem("keys_loaded")
        vals_loaded = sem("vals_loaded")
        xq_loaded = sem("xq_loaded")
        q_mm = sem("q_mm")
        q_copied = sem("q_copied")
        rq_mm = sem("rq_mm")
        rq_done = sem("rq_done")
        score_mm = sem("score_mm")
        max_done = sem("max_done")
        bias_step = sem("bias_step")
        bias_done = sem("bias_done")
        exp_done = sem("exp_done")
        pt_mm = sem("pt_mm")
        pt_act = sem("pt_act")
        pt_dve = sem("pt_dve")
        pv_mm = sem("pv_mm")
        recip_done = sem("recip_done")
        ao_done = sem("ao_done")
        aot_mm = sem("aot_mm")
        aot_copied = sem("aot_copied")
        ya_mm = sem("ya_mm")
        x3_done = sem("x3_done")

        NW = 10

        block = ctx.enter_context(nc.Block())

        @block.sync
        def _(sp):
            def load_weights():
                for dst, src in ((ident[:, :], ident_d), (col[:, :], cols), (row[:, :], rows),
                                 (w_qkvg[:, :, :], wqkvg.rearrange("(k p) n -> p k n", p=P)),
                                 (w_beta[:, :, :], wbeta.rearrange("(k p) n -> p k n", p=P)),
                                 (w_out[:, :, :], wout.rearrange("(k p) n -> p k n", p=P)),
                                 (w_x[:, :, :], wx.rearrange("(k p) n -> p k n", p=P)),
                                 (w_c[:, :, :], wc.rearrange("(k p) n -> p k n", p=P))):
                    sp.dma_start(dst, src).then_inc(w_loaded, DMA)
                for k in range(KT):
                    sp.dma_start(w_raw[:, :, k, :], wattn.rearrange("w (k p) n -> k p w n", p=P)[k]).then_inc(w_loaded, DMA)

            def after(sem, count):
                if not isinstance(count, int):
                    sp.wait_ge(w_loaded, NW * DMA)
                wait(sp, sem, count)

            def load_x(m):
                after(xT_done, 2 * m)
                sp.dma_start(xin[:, :, :], x_m[m]).then_inc(x_loaded, DMA)

            def spill_gate(m):
                for ft in range(KT):
                    after(gate_done, 2 * m + ft + 1)
                    sp.dma_start(gs_d[m, :, ft * TOK:(ft + 1) * TOK], gate[:, ft, :]).then_inc(gate_spilled, DMA)

            def spill_item(m, j):
                after(staged, NITEM * m + j + 1)
                for hf in range(2):
                    dst = rs_d[m, hf, j // 2].rearrange("b f t -> f b t")[(j % 2) * P:(j % 2 + 1) * P]
                    src = stage[:, j % SLOTS, :].rearrange("p (b s t) -> p s b t", b=B, s=2)[:, hf]
                    sp.dma_start(dst, src).then_inc(spilled[j % SLOTS], DMA)

            def load_lay(m, hf):
                for s in range(SLOTS):
                    after(spilled[s], 4 * DMA * (m + 1))
                after(prod_done, 2 * NS * (m - 1) + 4 * hf + 4)
                src = rs_d[m, hf].rearrange("w b (h i) t -> (b h) w (i t)", h=NH)
                dst = lay[:, hf].rearrange("p w i t -> p w (i t)")
                n = D * HALF
                sp.dma_start(dst[0:64], src).then_inc(lay_loaded[hf], DMA)
                sp.dma_start(dst[64:128, :, 0:n // 2], src[:, :, n // 2:n]).then_inc(lay_loaded[hf], DMA)
                sp.dma_start(dst[64:128, :, n // 2:n], src[:, :, 0:n // 2]).then_inc(lay_loaded[hf], DMA)

            def spill_sums(m, hf):
                after(sum_copied, NS * m + 2 * hf + 2)
                t = slice(hf * HALF, (hf + 1) * HALF)
                sp.dma_start(os_m[m, 0][:, :, t], ob[0:64, hf]).then_inc(ob_spilled[hf], DMA)
                sp.dma_start(os_m[m, 1][:, 8:16, t], ob[64:128, hf, 0:8]).then_inc(ob_spilled[hf], DMA)
                sp.dma_start(os_m[m, 1][:, 0:8, t], ob[64:128, hf, 8:16]).then_inc(ob_spilled[hf], DMA)

            def load_post(m):
                for hf in range(2):
                    after(ob_spilled[hf], 3 * DMA * (m + 1))
                after(oT_done, 2 * m)
                if isinstance(m, int) and m == 0:
                    after(wb_mm, 5)
                for a in range(2):
                    for ft in range(KT):
                        sp.dma_start(oH[:, a, ft, :].rearrange("p (b t) -> p b t", b=B),
                                     os_f[m, a][ft * P:(ft + 1) * P]).then_inc(o_loaded, DMA)
                after(gate_spilled, 2 * DMA * (m + 1))
                after(gated, 2 * m)
                sp.dma_start(gl[:, :, :].rearrange("p k t -> p (k t)"), gs_d[m]).then_inc(gl_loaded, DMA)
                load_xr(m, x_m[m], ln_3.norm_done, 4 * m)

            def load_xr(M, src, norms, count):
                after(x2_stored, DMA * M)
                after(norms, count)
                sp.dma_start(xr[:, :, :], src).then_inc(xr_loaded, DMA)

            def store_x(M, dst):
                after(x2_done, 2 * (M + 1))
                sp.dma_start(dst, xr[:, :, :]).then_inc(x2_stored, DMA)

            def spill_kv(m):
                after(ln_3.norm_done, 4 * (m + 1))
                sp.dma_start(vs_m[m], nrm[:, :, :]).then_inc(v_stored, DMA)
                for ft in range(KT):
                    after(n3T_copied, 2 * m + ft + 1)
                    sp.dma_start(ks_m[m, ft], n3T[:, ft, :].rearrange("p (b t) -> p b t", b=B)).then_inc(k_stored, DMA)

            def chunk_a(m):
                load_x(m)
                spill_gate(m)
                for j in range(NITEM):
                    spill_item(m, j)
                load_lay(m, 0)
                load_lay(m, 1)
                spill_sums(m, 0)
                spill_sums(m, 1)
                load_post(m)
                store_x(m, x2_m[m])
                spill_kv(m)

            def chunk_b(c):
                after(rq_mm, c)
                for k in range(KT):
                    sp.dma_start(xq[:, k, :].rearrange("p (b t) -> p b t", b=B), ks_m[c, k]).then_inc(xq_loaded, DMA)
                load_xr(NC + c, x2_m[c], ln_3.norm_done, 4 * NC)
                store_x(NC + c, out_m[c])

            load_weights()
            chunk_a(0)
            with sp.Fori(1, NC) as m:
                chunk_a(m)
            sp.wait_ge(k_stored, 2 * DMA * NC)
            sp.wait_ge(v_stored, DMA * NC)
            sp.wait_ge(x2_stored, DMA * NC)
            sp.wait_ge(prod_done, 2 * NS * NC)
            sp.wait_ge(sum_done, NS * NC)
            for b in range(B):
                for k in range(KT):
                    sp.dma_start(keys[:, k, b, :], ks_d[k, :, b, :]).then_inc(keys_loaded, DMA)
                sp.dma_start(vals[:, b], vs_d[b].rearrange("(j p) d -> p j d", p=P)).then_inc(vals_loaded, DMA)
            chunk_b(0)
            with sp.Fori(1, NC) as c:
                chunk_b(c)
            sp.wait_ge(x2_stored, 2 * DMA * NC)

        @block.gpsimd
        def _(gp):
            def consts():
                gp.memset(eps4[:, :], EPS).then_inc(const_set, 1)
                gp.memset(mhalf[:, :], -0.5).then_inc(const_set, 1)
                gp.memset(dec[:, :, :, 0:1], 0.0).then_inc(const_set, 1)
                gp.memset(st[:, 0, :, 0:1], 0.0).then_inc(const_set, 1)
                gp.memset(ob[:, :, D - 1, :], 0.0).then_inc(const_set, 1)
                gp.wait_ge(const_set, 5)

            def rstd(L, M):
                gp.wait_ge(L.mv_done, 4 * (M + 1))
                gp.tensor_tensor(L.rs[:, :], L.mv[:, :, 1], eps4[:, :], ALU.add).then_inc(L.var_done, 1)
                gp.wait_ge(L.var_done, M + 1)
                gp.tensor_tensor(L.rs[:, :], L.rs[:, :], mhalf[:, 0:B], ALU.pow).then_inc(L.rstd_done, 1)

            def head_norms(m):
                gp.wait_ge(ssmax_done, m + 1)
                gp.tensor_tensor(rn[:, :], rn[:, :], mhalf[:, :], ALU.pow).then_inc(rn_done, 1)

            def kk(m, s):
                hf, par, t = s // 2, s % 2, (s % 2) * SUB
                gp.wait_ge(lay_loaded[hf], 3 * DMA * (m + 1))
                wait(gp, scan_done, 2 * NS * m + 2 * s - 2)
                a, b_ = pair_views(lay, hf, K_, t), shifted_views(lay, hf, KB_, t)
                gp.tensor_tensor(pairs_out(dec, par, 0, ND), a(0, ND), b_(0, ND), ALU.mult).then_inc(kk_done, 1)

            def add_halves(m):
                gp.wait_ge(o_loaded, 4 * DMA * (m + 1))
                gp.tensor_tensor(oH[:, 0], oH[:, 0], oH[:, 1], ALU.add).then_inc(osum_done, 1)

            def gating(m):
                gp.wait_ge(gl_loaded, DMA * (m + 1))
                for ft in range(KT):
                    gp.wait_ge(og_done, 2 * m + ft + 1)
                    gp.tensor_tensor(ogT[:, ft], ogT[:, ft], gl[:, ft], ALU.mult).then_inc(gated, 1)

            def add_mlp(M):
                for j in range(2):
                    gp.wait_ge(h_act, 2 * M + j + 1)
                    v = xr[:, 2 * j:2 * j + 2, :].rearrange("p b d -> p (b d)")
                    gp.tensor_tensor(v, v, hh[:, j, :], ALU.add).then_inc(x2_done, 1)

            def chunk_a(m):
                rstd(ln_x, m)
                head_norms(m)
                for s in range(NS):
                    kk(m, s)
                add_halves(m)
                rstd(ln_o, m)
                gating(m)
                rstd(ln_2, m)
                add_mlp(m)
                rstd(ln_3, m)

            def chunk_b(c):
                rstd(ln_2, NC + c)
                add_mlp(NC + c)

            consts()
            chunk_a(0)
            with gp.Fori(1, NC) as m:
                chunk_a(m)
            with gp.Fori(0, NC) as c:
                chunk_b(c)

        @block.scalar
        def _(act):
            def copy(dst, src, scale=1.0, bias=0.0):
                return act.activation(dst, src, ACT.Identity, scale=scale, bias=bias)

            def pre(m):
                for ft in range(KT):
                    act.wait_ge(xT_done, 2 * m + ft + 1)
                    wait(act, g_mm, 2 * m)
                    copy(xnT[:, ft, :], PB[:, ft, :]).then_inc(xT_copied, 1)
                for b in range(B):
                    act.wait_ge(qk_mm, 4 * m + b + 1)
                    wait(act, ss_done, 4 * m + b - 1)
                    act.activation(sq[:, b % 2, :], PB[:, b % 2, :], ACT.Square).then_inc(sq_done, 1)
                    wait(act, turn_done, 6 * m)
                    copy(qk[:, b, :], PB[:, b % 2, :]).then_inc(qk_copied, 1)
                act.wait_ge(beta_mm, m + 1)
                wait(act, beta_done, m)
                act.activation(bt[:, :], PB[:, 0, 0:B * NH], ACT.Tanh, scale=0.5).then_inc(bt_done, 1)
                for ft in range(KT):
                    act.wait_ge(v_mm, 2 * m + ft + 1)
                    to_stage(m, ft, PB[:, 1 - ft, :])
                for ft in range(KT):
                    act.wait_ge(g_mm, 2 * m + ft + 1)
                    wait(act, gate_spilled, 2 * DMA * m)
                    act.activation(gate[:, ft, :], PB[:, 1 - ft, :], ACT.Tanh, scale=0.5).then_inc(tg_done, 1)
                for j in range(6):
                    act.wait_ge(turn_done, 6 * m + j + 1)
                    to_stage(m, 2 + j, PB[:, (j + 1) % 2, :])

            def to_stage(m, j, src):
                wait(act, spilled[j % SLOTS], 4 * DMA * m + 2 * DMA * (j // SLOTS))
                copy(stage[:, j % SLOTS, :], src).then_inc(staged, 1)

            def decay(m, s):
                act.wait_ge(kk_done, NS * m + s + 1)
                v = dec[:, s % 2, :, 1:COL]
                copy(v, v, scale=-1.0, bias=1.0).then_inc(dec_done, 1)

            def sums(m, s):
                act.wait_ge(sum_done, NS * m + s + 1)
                hf, t = s // 2, (s % 2) * SUB
                wait(act, ob_spilled[hf], 3 * DMA * m)
                copy(ob[:, hf, 0:D - 1, t:t + SUB],
                     JB[:, s % 2, 0:(D - 1) * SUB].rearrange("p (i t) -> p i t", t=SUB)).then_inc(sum_copied, 1)

            def scale_o(m):
                for ft in range(KT):
                    act.wait_ge(onT_done, 2 * m + ft + 1)
                    wait(act, y_mm, 2 * m)
                    copy(ogT[:, ft, :], QB[:, ft, :], scale=hcol[:, ft:ft + 1],
                         bias=hcol[:, 2 + ft:3 + ft]).then_inc(og_done, 1)

            def mlp(M):
                for ft in range(KT):
                    act.wait_ge(n2t_done, 2 * M + ft + 1)
                    wait(act, h_mm, 2 * M)
                    copy(n2T[:, ft, :], QB[:, ft, :]).then_inc(n2T_copied, 1)
                for b in range(B):
                    wait(act, c_done, 4 * M + b)
                    for g in range(3):
                        if g != 1:
                            act.wait_ge(cell_mm, 8 * M + 2 * b + (g // 2) + 1)
                        for mt in range(KT):
                            n = g * KT + mt
                            bias = hcol[:, 4 + n:5 + n] if g < 2 else col[:, BC + mt:BC + mt + 1]
                            act.activation(gt[:, g, mt * P:(mt + 1) * P], FB[:, n // 4, (n % 4) * P:(n % 4 + 1) * P],
                                           ACT.Tanh, scale=0.5 if g < 2 else 1.0, bias=bias).then_inc(cell_act, 1)
                for j in range(2):
                    act.wait_ge(h_mm, 2 * M + j + 1)
                    wait(act, x2_done, 2 * M)
                    act.activation(hh[:, j, :], QB[:, j, :], ACT.Tanh).then_inc(h_act, 1)

            def keys_out(m):
                for ft in range(KT):
                    act.wait_ge(n3t_done, 2 * m + ft + 1)
                    wait(act, k_stored, 2 * DMA * m)
                    copy(n3T[:, ft, :], QB[:, ft, :]).then_inc(n3T_copied, 1)

            def attn_weights():
                act.wait_ge(wb_mm, 5)
                copy(w_g[:, :, :], JB[:, 0, :].rearrange("p (k n) -> p k n", k=KT)).then_inc(wb_done, 1)
                copy(w_vo[:, :, :], JB[:, 1, :].rearrange("p (k n) -> p k n", k=KT)).then_inc(wb_done, 1)
                copy(q_bias[:, :], QB[:, 0, 0:2 * KT]).then_inc(wb_done, 1)
                copy(qk_const[:, :], QB[0:1, 0, 16:17]).then_inc(wb_done, 1)

            def chunk_a(m):
                pre(m)
                if isinstance(m, int):
                    attn_weights()
                for s in range(NS):
                    decay(m, s)
                    if s:
                        sums(m, s - 1)
                sums(m, NS - 1)
                scale_o(m)
                mlp(m)
                keys_out(m)

            def attend(c, b):
                act.wait_ge(bias_done, 4 * c + b + 1)
                wait(act, pt_mm, 2 * (4 * c + b))
                act.activation(prob, JB[:, :, :].rearrange("p a n -> p (a n)"), ACT.Exp, scale=SCALE,
                               bias=mx[:, 2:3], accum_out=mx[:, 3:4]).then_inc(exp_done, 1)
                act.wait_ge(pt_mm, 2 * (4 * c + b) + 1)
                wait(act, pv_mm, 4 * c + b)
                copy(probT[:, 0:4, :], PB[:, 0, :].rearrange("p (j q) -> p j q", j=4)).then_inc(pt_act, 1)
                act.wait_ge(aot_mm, 4 * c + b + 1)
                wait(act, ya_mm, 4 * c + b)
                copy(aoT[:, :, :], QB[:, 1, 0:HID].rearrange("p (k t) -> p k t", k=KT)).then_inc(aot_copied, 1)

            def chunk_b(c):
                for et in range(KT):
                    act.wait_ge(q_mm, 2 * c + et + 1)
                    wait(act, score_mm, 4 * c)
                    copy(qT[:, et, :], PB[:, et, :], bias=q_bias[:, et:et + 1]).then_inc(q_copied, 1)
                for b in range(B):
                    attend(c, b)
                mlp(NC + c)

            act.wait_ge(dve_const, 6)
            chunk_a(0)
            with act.Fori(1, NC) as m:
                chunk_a(m)
            chunk_b(0)
            with act.Fori(1, NC) as c:
                chunk_b(c)

        @block.tensor
        def _(pe):
            def mm(dst, lhsT, rhs, start, stop):
                return pe.matmul(dst, lhsT, rhs, start=start, stop=stop, skip_group_check=True)

            def turn_tiles(bank, src, ft):
                for b in range(B):
                    i = pe.transpose(bank[:, b * P:(b + 1) * P], src[:, b, ft * P:(ft + 1) * P], ident[:, :])
                return i

            def pre(m):
                pe.wait_ge(ln_x.norm_done, 4 * (m + 1))
                for ft in range(KT):
                    wait(pe, staged, NITEM * m - ft)
                    turn_tiles(PB[:, ft, :], xin, ft).then_inc(xT_done, 1)
                pe.wait_ge(xT_copied, 2 * (m + 1))
                for b in range(B):
                    if b >= 2:
                        pe.wait_ge(qk_copied, 4 * m + b - 1)
                    for k in range(KT):
                        i = mm(PB[:, b % 2, :], xnT[:, k, b * P:(b + 1) * P], w_qkvg[:, k, 0:2 * HID],
                               k == 0, k == KT - 1)
                    i.then_inc(qk_mm, 1)
                pe.wait_ge(qk_copied, 4 * m + 3)
                for b in range(B):
                    for k in range(KT):
                        i = mm(PB[:, 0, b * NH:(b + 1) * NH], xnT[:, k, b * P:(b + 1) * P], w_beta[:, k, :],
                               b == 0 and k == 0, k == KT - 1)
                i.then_inc(beta_mm, 1)
                for n, done in ((2, v_mm), (3, g_mm)):
                    for ft in range(KT):
                        if n == 2 and ft == 0:
                            pe.wait_ge(qk_copied, 4 * m + 4)
                        elif n == 2:
                            pe.wait_ge(bt_done, m + 1)
                        else:
                            pe.wait_ge(staged, NITEM * m + ft + 1)
                        for k in range(KT):
                            w = w_qkvg[:, k, n * HID + ft * P:n * HID + (ft + 1) * P]
                            i = mm(PB[:, 1 - ft, :], w, xnT[:, k, :], k == 0, k == KT - 1)
                        i.then_inc(done, 1)
                pe.wait_ge(qkn_done, m + 1)
                for j in range(6):
                    if j < 2:
                        pe.wait_ge(gate_done, 2 * m + j + 1)
                    else:
                        pe.wait_ge(staged, NITEM * m + j + 1)
                    if j == 4:
                        pe.wait_ge(kb_done, m + 1)
                    src = (qk[:, :, 0:HID], qk[:, :, HID:2 * HID], kb[:, :, :])[j // 2]
                    turn_tiles(PB[:, (j + 1) % 2, :], src, j % 2).then_inc(turn_done, 1)

            def attn_weights():
                for d in range(KT):
                    for k in range(KT):
                        i = mm(JB[:, 0, d * HID:(d + 1) * HID], w_raw[:, 0, k, d * P:(d + 1) * P], w_raw[:, 1, k, :],
                               d == 0 and k == 0, k == KT - 1)
                i.then_inc(wb_mm, 1)
                for d in range(KT):
                    for k in range(KT):
                        i = mm(JB[:, 1, d * HID:(d + 1) * HID], w_raw[:, 2, k, d * P:(d + 1) * P], w_raw[:, 3, k, :],
                               d == 0 and k == 0, k == KT - 1)
                i.then_inc(wb_mm, 1)
                for w, bias, at in ((1, BQ, 0), (0, BK, 2)):
                    for d in range(KT):
                        for k in range(KT):
                            i = mm(QB[:, 0, at + d:at + d + 1], w_raw[:, w, k, d * P:(d + 1) * P],
                                   col[:, bias + k:bias + k + 1], at + d + k == 0, k == KT - 1)
                i.then_inc(wb_mm, 1)
                for k in range(KT):
                    i = mm(QB[0:1, 0, 16:17], col[:, BQ + k:BQ + k + 1], col[:, BK + k:BK + k + 1], False, k == KT - 1)
                i.then_inc(wb_mm, 1)
                for k in range(KT):
                    i = mm(QB[0:1, 1, 0:HID], col[:, BV + k:BV + k + 1], w_raw[:, 3, k, :], k == 0, k == KT - 1)
                i.then_inc(wb_mm, 1)

            def sum_j(m, s):
                pe.wait_ge(prod_done, 2 * NS * m + 2 * s + 2)
                wait(pe, sum_copied, NS * m + s - 1)
                if isinstance(m, int) and m == 0 and s < 2:
                    pe.wait_ge(wb_done, 5)
                par = s % 2
                order = [(0, 0)] + [(1, d) for d in range(ND - 2, 0, -1)] + [(0, d) for d in range(1, ND)]
                for n, (mirror, d) in enumerate(order):
                    at = U + (d - 1) * NI if mirror else d * NI
                    lo = d if mirror else 0
                    i = mm(JB[:, par, lo * SUB:(lo + NI) * SUB], ident[:, :], st[:, par, at:at + NI, 1:COL],
                           n == 0, n == len(order) - 1)
                i.then_inc(sum_done, 1)

            def post(m):
                pe.wait_ge(osum_done, m + 1)
                wait(pe, n3T_copied, 2 * m)
                for j in range(2):
                    for b in (2 * j, 2 * j + 1):
                        for ft in range(KT):
                            i = pe.transpose(QB[:, j, (b % 2) * HID + ft * P:(b % 2) * HID + (ft + 1) * P],
                                             oH[:, 0, ft, b * P:(b + 1) * P], ident[:, :])
                    i.then_inc(oT_done, 1)
                pe.wait_ge(ln_o.norm_done, 4 * (m + 1))
                for ft in range(KT):
                    turn_tiles(QB[:, ft, :], nrm, ft).then_inc(onT_done, 1)
                pe.wait_ge(gated, 2 * (m + 1))
                for j in range(2):
                    for b in (2 * j, 2 * j + 1):
                        for k in range(KT):
                            i = mm(QB[:, j, (b % 2) * HID:(b % 2 + 1) * HID], ogT[:, k, b * P:(b + 1) * P],
                                   w_out[:, k, :], b % 2 == 0 and k == 0, k == KT - 1)
                    i.then_inc(y_mm, 1)

            def mlp(M):
                pe.wait_ge(ln_2.norm_done, 4 * (M + 1))
                for ft in range(KT):
                    turn_tiles(QB[:, ft, :], nrm, ft).then_inc(n2t_done, 1)
                pe.wait_ge(n2T_copied, 2 * (M + 1))
                for b in range(B):
                    wait(pe, cell_act, 24 * M + 6 * b)
                    for n in range(3 * KT):
                        for k in range(KT):
                            mm(FB[:, n // 4, (n % 4) * P:(n % 4 + 1) * P], w_x[:, k, n * P:(n + 1) * P],
                               n2T[:, k, b * P:(b + 1) * P], n % 4 == 0 and k == 0, False)
                    if b:
                        pe.wait_ge(c_done, 4 * M + b)
                    cell = cc if b else c0
                    for n in range(3 * KT):
                        for k in range(KT):
                            i = mm(FB[:, n // 4, (n % 4) * P:(n % 4 + 1) * P], w_c[:, k, n * P:(n + 1) * P],
                                   cell[:, k, :], False, k == KT - 1)
                        if n in (3, 5):
                            i.then_inc(cell_mm, 1)
                pe.wait_ge(c_done, 4 * (M + 1))
                for j in range(2):
                    for b in (2 * j, 2 * j + 1):
                        dst = QB[:, j, (b % 2) * HID:(b % 2 + 1) * HID]
                        for k in range(KT):
                            mm(dst, n2T[:, k, b * P:(b + 1) * P], w_x[:, k, 3 * HID:4 * HID], b % 2 == 0 and k == 0, False)
                        for k in range(KT):
                            mm(dst, cc[:, k, :], w_c[:, k, 3 * HID:4 * HID], False, False)
                        i = mm(dst, row[:, 2 * HID:2 * HID + P], row[:, 0:HID], False, True)
                    i.then_inc(h_mm, 1)

            def keys_out(m):
                pe.wait_ge(ln_3.norm_done, 4 * (m + 1))
                pe.wait_ge(h_act, 2 * (m + 1))
                for ft in range(KT):
                    turn_tiles(QB[:, ft, :], nrm, ft).then_inc(n3t_done, 1)

            def chunk_a(m):
                pre(m)
                if isinstance(m, int):
                    attn_weights()
                for s in range(NS):
                    sum_j(m, s)
                post(m)
                mlp(m)
                keys_out(m)

            def attend(c, b):
                n = 4 * c + b
                wait(pe, exp_done, n)
                for j in range(2):
                    for k in range(KT):
                        i = mm(JB[:, j, :], qT[:, k, b * P:(b + 1) * P], keys[:, k, b, j * 512:(j + 1) * 512],
                               k == 0, k == KT - 1)
                i.then_inc(score_mm, 1)
                pe.wait_ge(exp_done, n + 1)
                for j in range(2):
                    wait(pe, (pt_act, pt_dve)[j], n)
                    if j == 0:
                        pe.wait_ge(q_copied, 2 * (c + 1))
                        pe.wait_ge(rq_done, c + 1)
                    for t in range(4):
                        i = pe.transpose(PB[:, j, t * P:(t + 1) * P], prob[:, (4 * j + t) * P:(4 * j + t + 1) * P],
                                         ident[:, :])
                    i.then_inc(pt_mm, 1)
                pe.wait_ge(pt_act, n + 1)
                pe.wait_ge(pt_dve, n + 1)
                wait(pe, x3_done, n)
                for t in range(NC):
                    i = mm(QB[:, 0, 0:HID], probT[:, t, :], vals[:, b, t, :], t == 0, t == NC - 1)
                i.then_inc(pv_mm, 1)
                pe.wait_ge(ao_done, n + 1)
                for k in range(KT):
                    i = pe.transpose(QB[:, 1, k * P:(k + 1) * P], ao[:, k * P:(k + 1) * P], ident[:, :])
                i.then_inc(aot_mm, 1)
                pe.wait_ge(aot_copied, n + 1)
                for k in range(KT):
                    mm(QB[:, 0, HID:2 * HID], aoT[:, k, :], w_vo[:, k, :], k == 0, False)
                mm(QB[:, 0, HID:2 * HID], row[:, 2 * HID:2 * HID + P], y_bias[:, :], False, True).then_inc(ya_mm, 1)

            def chunk_b(c):
                pe.wait_ge(xq_loaded, 2 * DMA * (c + 1))
                wait(pe, pt_act, 4 * c)
                wait(pe, pt_dve, 4 * c)
                for et in range(KT):
                    for k in range(KT):
                        i = mm(PB[:, et, :], w_g[:, k, et * P:(et + 1) * P], xq[:, k, :], k == 0, k == KT - 1)
                    i.then_inc(q_mm, 1)
                pe.wait_ge(q_copied, 2 * c + 1)
                for b in range(B):
                    for k in range(KT):
                        mm(PB[:, 0, b:b + 1], xq[:, k, b * P:(b + 1) * P], q_bias[:, 2 + k:3 + k], b == 0 and k == 0, False)
                    i = mm(PB[:, 0, b:b + 1], row[:, 2 * HID:2 * HID + P], qk_const[:, :], False, True)
                i.then_inc(rq_mm, 1)
                pe.wait_ge(q_copied, 2 * (c + 1))
                for b in range(B):
                    attend(c, b)
                mlp(NC + c)

            pe.wait_ge(w_loaded, NW * DMA)
            pe.wait_ge(dve_const, 6)
            chunk_a(0)
            with pe.Fori(1, NC) as m:
                chunk_a(m)
            pe.wait_ge(keys_loaded, 2 * B * DMA)
            pe.wait_ge(vals_loaded, B * DMA)
            chunk_b(0)
            with pe.Fori(1, NC) as c:
                chunk_b(c)

        @block.vector
        def _(dve):
            def norm_stats(L, M, src, ready):
                wait(dve, L.norm_done, 4 * M)
                for b in range(B):
                    ready(b)
                    dve.bn_stats(L.stats[:, b, :], src(b)).then_inc(L.stat_done, 1)
                dve.wait_ge(L.stat_done, 4 * (M + 1))
                wait(dve, L.settled, M)
                dve.tensor_copy(L.last[:, :], L.stats[:, B - 1, 0:1]).then_inc(L.settled, 1)
                for b in range(B):
                    dve.bn_aggr(L.mv[:, b, :], L.stats[:, b, :]).then_inc(L.mv_done, 1)

            def norm_apply(L, M, src, dst):
                dve.wait_ge(L.rstd_done, M + 1)
                dve.wait_ge(L.mv_done, 4 * (M + 1))
                for b in range(B):
                    dve.tensor_scalar(dst(b), src(b), L.mv[:, b, 0:1], L.rs[:, b:b + 1],
                                      ALU.subtract, ALU.mult).then_inc(L.norm_done, 1)

            def tile(t):
                return lambda b: t[:, b, :]

            def consts():
                dve.wait_ge(w_loaded, NW * DMA)
                dve.tensor_scalar(hcol[:, 0:4], col[:, LNG:LNG + 4], 0.5, None, ALU.mult).then_inc(dve_const, 1)
                dve.tensor_scalar(hcol[:, 4:8], col[:, BF:BF + 4], 0.5, None, ALU.mult).then_inc(dve_const, 1)
                dve.tensor_scalar(w_c[:, :, :], w_c[:, :, :], 0.5, None, ALU.mult).then_inc(dve_const, 1)
                dve.tensor_scalar(c_init[:, :], col[:, INC:INC + 2], 2.0, None, ALU.mult).then_inc(dve_const, 1)
                dve.wait_ge(dve_const, 4)
                dve.wait_ge(const_set, 5)
                for k in range(KT):
                    dve.tensor_scalar(c0[:, k, :], mhalf[:, :], 0.0, c_init[:, k:k + 1], ALU.mult, ALU.add).then_inc(dve_const, 1)
                dve.wait_ge(dve_const, 6)

            def pre(m):
                norm_stats(ln_x, m, tile(xin), lambda b: dve.wait_ge(x_loaded, DMA * (m + 1)))
                norm_apply(ln_x, m, tile(xin), tile(xin))
                for b in range(B):
                    dve.wait_ge(sq_done, 4 * m + b + 1)
                    wait(dve, ssmax_done, m)
                    dve.tensor_reduce(ss[:, b * 32:(b + 1) * 32], sq[:, b % 2, :].rearrange("p (h i) -> p h i", i=D),
                                      AX.X, ALU.add).then_inc(ss_done, 1)
                dve.wait_ge(ss_done, 4 * (m + 1))
                wait(dve, qkn_done, m)
                dve.tensor_scalar(rn[:, :], ss[:, :], 1e-24, None, ALU.max).then_inc(ssmax_done, 1)
                dve.wait_ge(bt_done, m + 1)
                wait(dve, kb_done, m)
                dve.tensor_scalar(beta[:, :], bt[:, :], 0.5, 0.5, ALU.mult, ALU.add).then_inc(beta_done, 1)
                for ft in range(KT):
                    dve.wait_ge(tg_done, 2 * m + ft + 1)
                    dve.scalar_tensor_tensor(out=gate[:, ft, :], in0=gate[:, ft, :], scalar=1.0, in1=PB[:, 1 - ft, :],
                                             op0=ALU.add, op1=ALU.mult).then_inc(gate_done, 1)
                dve.wait_ge(rn_done, m + 1)
                dve.wait_ge(qk_copied, 4 * (m + 1))
                v = qk[:, :, :].rearrange("p b (h i) -> p (b h) i", i=D)
                dve.tensor_tensor(v, v, rn[:, :].unsqueeze(2).broadcast_to([P, B * 2 * NH, D]),
                                  ALU.mult).then_inc(qkn_done, 1)
                dve.wait_ge(qkn_done, m + 1)
                dve.wait_ge(beta_done, m + 1)
                wait(dve, turn_done, 6 * m)
                dve.tensor_tensor(kb[:, :, :].rearrange("p b (h i) -> p b h i", i=D),
                                  qk[:, :, HID:2 * HID].rearrange("p b (h i) -> p b h i", i=D),
                                  beta[:, :].rearrange("p (b h) -> p b h", b=B).unsqueeze(3).broadcast_to([P, B, NH, D]),
                                  ALU.mult).then_inc(kb_done, 1)

            def scan(m, s):
                hf, par, t = s // 2, s % 2, (s % 2) * SUB
                n = NS * m + s
                v, v_sh = pair_views(lay, hf, V_, t), shifted_views(lay, hf, V_, t)
                b_, b_sh = pair_views(lay, hf, KB_, t), shifted_views(lay, hf, KB_, t)
                q, q_sh = pair_views(lay, hf, Q_, t), shifted_views(lay, hf, Q_, t)
                up = pairs_out(st, par, 0, ND)
                mi = pairs_out(st, par, U, ND - 2)
                dve.wait_ge(lay_loaded[hf], 3 * DMA * (m + 1))
                wait(dve, sum_done, n - 1)
                dve.tensor_tensor(up, v(0, ND), b_sh(0, ND), ALU.mult).then_inc(inp_done, 1)
                dve.tensor_tensor(mi, v_sh(1, ND - 1), b_(1, ND - 1), ALU.mult).then_inc(inp_done, 1)
                dve.wait_ge(dec_done, n + 1)
                dve.wait_ge(inp_done, 2 * n + 2)
                wait(dve, carried, n)
                a1 = dec[:, par, :, :].rearrange("p r t -> p (r t)")
                a2 = dec[:, par, NI:NI + MIR, :].rearrange("p r t -> p (r t)")
                s1 = st[:, par, 0:U, :].rearrange("p r t -> p (r t)")
                s2 = st[:, par, U:PAIRS, :].rearrange("p r t -> p (r t)")
                dve.tensor_tensor_scan(s1, a1, s1, 0.0, ALU.mult, ALU.add).then_inc(scan_done, 1)
                dve.tensor_tensor_scan(s2, a2, s2, 0.0, ALU.mult, ALU.add).then_inc(scan_done, 1)
                dve.wait_ge(scan_done, 2 * n + 2)
                dve.tensor_copy(st[:, 1 - par, :, 0:1], st[:, par, :, SUB:COL]).then_inc(carried, 1)
                dve.wait_ge(carried, n + 1)
                dve.tensor_tensor(up, up, q_sh(0, ND), ALU.mult).then_inc(prod_done, 1)
                dve.tensor_tensor(mi, mi, q(1, ND - 1), ALU.mult).then_inc(prod_done, 1)

            def post(m):
                def src(b):
                    return QB[:, b // 2, (b % 2) * HID:(b % 2 + 1) * HID]

                norm_stats(ln_o, m, src, lambda b: dve.wait_ge(oT_done, 2 * m + b // 2 + 1))
                wait(dve, n3t_done, 2 * m)
                wait(dve, v_stored, DMA * m)
                norm_apply(ln_o, m, src, tile(nrm))
                dve.wait_ge(xr_loaded, DMA * (m + 1))
                for j in range(2):
                    dve.wait_ge(y_mm, 2 * m + j + 1)
                    v = xr[:, 2 * j:2 * j + 2, :].rearrange("p b d -> p (b d)")
                    dve.tensor_tensor(v, v, QB[:, j, :], ALU.add).then_inc(x1_done, 1)

            def mlp_norm(M, ready, free):
                norm_stats(ln_2, M, tile(xr), ready)
                free()
                norm_apply(ln_2, M, tile(xr), tile(nrm))

            def mlp(M):
                for b in range(B):
                    cell = cc if b else c0
                    dve.wait_ge(cell_act, 24 * M + 6 * b + 6)
                    wait(dve, c_done, 4 * M + b)
                    c_in = cell[:, :, :].rearrange("p k t -> p (k t)")
                    dve.scalar_tensor_tensor(out=gt[:, 0, :], in0=gt[:, 0, :], scalar=1.0, in1=c_in,
                                             op0=ALU.add, op1=ALU.mult).then_inc(cell_h, 1)
                    dve.scalar_tensor_tensor(out=gt[:, 1, :], in0=gt[:, 1, :], scalar=1.0, in1=gt[:, 2, :],
                                             op0=ALU.add, op1=ALU.mult).then_inc(cell_h, 1)
                    dve.wait_ge(cell_h, 8 * M + 2 * b + 2)
                    if b == 0:
                        wait(dve, h_mm, 2 * M)
                    dve.scalar_tensor_tensor(out=cc[:, :, :].rearrange("p k t -> p (k t)"), in0=gt[:, 0, :], scalar=0.5,
                                             in1=gt[:, 1, :], op0=ALU.mult, op1=ALU.add).then_inc(c_done, 1)

            def keys_norm(m):
                norm_stats(ln_3, m, tile(xr), lambda b: dve.wait_ge(x2_done, 2 * m + b // 2 + 1))
                dve.wait_ge(n2t_done, 2 * (m + 1))
                norm_apply(ln_3, m, tile(xr), tile(nrm))

            def chunk_a(m):
                pre(m)
                if isinstance(m, int):
                    dve.wait_ge(wb_mm, 5)
                    dve.tensor_tensor(y_bias[:, :], row[:, HID:2 * HID], QB[0:1, 1, 0:HID], ALU.add).then_inc(wb_done, 1)
                for s in range(NS):
                    scan(m, s)
                post(m)
                mlp_norm(m, lambda b: dve.wait_ge(x1_done, 2 * m + b // 2 + 1),
                         lambda: dve.wait_ge(onT_done, 2 * (m + 1)))
                mlp(m)
                keys_norm(m)

            def attend(c, b):
                n = 4 * c + b
                dve.wait_ge(score_mm, n + 1)
                wait(dve, exp_done, n)
                dve.tensor_reduce(mx[:, 0:1], JB[:, :, :], AX.XY, ALU.max).then_inc(max_done, 1)
                dve.wait_ge(max_done, n + 1)
                dve.tensor_tensor(mx[:, 1:2], mx[:, 0:1], rq[:, b:b + 1], ALU.add).then_inc(bias_step, 1)
                dve.wait_ge(bias_step, 2 * n + 1)
                dve.tensor_tensor(mx[:, 1:2], rq[:, b:b + 1], mx[:, 1:2], ALU.subtract).then_inc(bias_step, 1)
                dve.wait_ge(bias_step, 2 * n + 2)
                dve.tensor_scalar(mx[:, 2:3], mx[:, 1:2], SCALE, None, ALU.mult).then_inc(bias_done, 1)
                dve.wait_ge(pt_mm, 2 * n + 2)
                wait(dve, pv_mm, n)
                dve.tensor_copy(probT[:, 4:8, :], PB[:, 1, :].rearrange("p (j q) -> p j q", j=4)).then_inc(pt_dve, 1)
                dve.wait_ge(exp_done, n + 1)
                dve.reciprocal(mx[:, 4:5], mx[:, 3:4]).then_inc(recip_done, 1)
                dve.wait_ge(recip_done, n + 1)
                dve.wait_ge(pv_mm, n + 1)
                wait(dve, aot_mm, n)
                dve.tensor_scalar(ao, QB[:, 0, 0:HID], mx[:, 4:5], None, ALU.mult).then_inc(ao_done, 1)
                dve.wait_ge(ya_mm, n + 1)
                dve.tensor_tensor(xr[:, b, :], xr[:, b, :], QB[:, 0, HID:2 * HID], ALU.add).then_inc(x3_done, 1)

            def chunk_b(c):
                dve.wait_ge(rq_mm, c + 1)
                wait(dve, bias_done, 4 * c)
                dve.tensor_copy(rq[:, :], PB[:, 0, 0:B]).then_inc(rq_done, 1)
                dve.wait_ge(rq_done, c + 1)
                dve.wait_ge(xr_loaded, DMA * (NC + c + 1))
                for b in range(B):
                    attend(c, b)
                mlp_norm(NC + c, lambda b: dve.wait_ge(x3_done, 4 * c + b + 1),
                         lambda: (dve.wait_ge(n2t_done, 2 * (NC + c)), dve.wait_ge(n3t_done, 2 * NC),
                                  dve.wait_ge(v_stored, DMA * NC)))
                mlp(NC + c)

            consts()
            chunk_a(0)
            with dve.Fori(1, NC) as m:
                chunk_a(m)
            chunk_b(0)
            with dve.Fori(1, NC) as c:
                chunk_b(c)


def _lay_view(lay, hf, w, t, pattern, first):
    base = lay[:, hf, w, first:first + 1, t:t + SUB]
    return bass.AP(base.tensor, base.offset, [list(base.ap[0])] + pattern)


def pair_views(lay, hf, w, t):
    return lambda d0, nd: _lay_view(lay, hf, w, t, [[0, nd if d0 == 0 else nd - d0], [HALF, NI], [1, SUB]], 0)


def shifted_views(lay, hf, w, t):
    return lambda d0, nd: _lay_view(lay, hf, w, t, [[HALF, nd if d0 == 0 else nd - d0], [HALF, NI], [1, SUB]], d0)


def pairs_out(buf, par, at, nd):
    return buf[:, par, at:at + nd * NI, 1:COL].rearrange("p (d i) t -> p d i t", i=NI)


def kernel(**inputs):
    import numpy as np
    import concourse.bacc as bacc
    from concourse.bass_utils import run_bass_kernel_spmd

    f = {k: np.asarray(v) for k, v in inputs.items()}
    a = lambda n: f["L0_attn_a_" + n]
    b = lambda n: f["L0_attn_b_" + n]
    w = lambda n: f["L0_ffn_" + n]
    cols = [a("ln_g"), a("ln_b"), w("bf"), w("bi"), w("bc"), w("in_c"), b("b_q"), b("b_k"), b("b_v")]
    arrays = {
        "x": a("x"),
        "wqkvg": np.concatenate([a("Wq"), a("Wk"), a("Wv"), a("Wg")], axis=1),
        "wbeta": a("Wbeta"),
        "wout": a("Wout"),
        "cols": np.concatenate([v.reshape(KT, P).T for v in cols], axis=1),
        "rows": np.concatenate([w("bo"), b("b_out"), np.ones(P, np.float32)])[None, :],
        "wx": np.concatenate([w("wf").T, w("wi").T, w("wc").T, w("wo").T], axis=1),
        "wc": np.concatenate([w("uf").T, w("ui").T, w("uc").T, w("uo").T], axis=1),
        "wattn": np.stack([b("w_q"), b("w_k"), b("w_v"), b("w_out").T]),
        "ident": np.eye(P, dtype=np.float32),
    }
    arrays = {k: np.ascontiguousarray(v) for k, v in arrays.items()}
    nc = bacc.Bacc("TRN2", target_bir_lowering=False, num_devices=1)
    args = [nc.dram_tensor("in_" + k, v.shape, mybir.dt.from_np(v.dtype), kind="ExternalInput").ap() for k, v in arrays.items()]
    out = nc.dram_tensor("out", (B, S, HID), F32, kind="ExternalOutput").ap()
    block_kernel(nc, *args, out)
    r = run_bass_kernel_spmd(nc, [{"in_" + k: v for k, v in arrays.items()}], core_ids=[0])
    return r.results[0]["out"]
```

```python
from contextlib import ExitStack

import concourse.bass as bass
from concourse import mybir

F32 = mybir.dt.float32
ALU = mybir.AluOpType
ACT = mybir.ActivationFunctionType
AX = mybir.AxisListType

B, S, HID, NH, D = 4, 1024, 256, 16, 16
P = 128
NC = S // P
KT = HID // P
TOK = B * P
HALF = 64
SUB = 32
NS = P // SUB
COL = SUB + 1
ND = D // 2 + 1
NI = D // 2
U = ND * NI
MIR = (ND - 2) * NI
PAIRS = U + MIR
V_, Q_, K_, KB_ = range(4)
NITEM = 2 * 4
SLOTS = 4
EPS = 1e-5
SCALE = 1.0 / 16.0
(LNG, LNB, BF, BI, BC, INC, BQ, BK, BV) = range(0, 18, 2)
DMA = 16
PARTS = 4


class LayerNorm:

    def __init__(self, sb, sem, name):
        self.stats = sb(f"{name}_stats", [P, B, 6])
        self.mv = sb(f"{name}_mv", [P, B, 2])
        self.rs = sb(f"{name}_rs", [P, B])
        self.last = sb(f"{name}_last", [P, 1])
        self.settled = sem(f"{name}_settled")
        self.stat_done = sem(f"{name}_stat_done")
        self.mv_done = sem(f"{name}_mv_done")
        self.var_done = sem(f"{name}_var_done")
        self.rstd_done = sem(f"{name}_rstd_done")
        self.norm_done = sem(f"{name}_norm_done")


def wait(e, sem, count):
    if not isinstance(count, int) or count > 0:
        e.wait_ge(sem, count)


def block_kernel(nc, x, wqkvg, wbeta, wout, cols, rows, wx, wc, wattn, ident_d, out):
    rs_d = nc.dram_tensor("scan_in_dram", [NC, 2, 4, B, HID, HALF], F32, kind="Internal").ap()
    os_d = nc.dram_tensor("scan_out_dram", [NC, 2, B, NH, D, P], F32, kind="Internal").ap()
    gs_d = nc.dram_tensor("gate_dram", [NC, P, KT * TOK], F32, kind="Internal").ap()
    x2_d = nc.dram_tensor("x2_dram", [B, S, HID], F32, kind="Internal").ap()
    vs_d = nc.dram_tensor("values_dram", [B, S, HID], F32, kind="Internal").ap()
    ks_d = nc.dram_tensor("keys_dram", [KT, P, B, S], F32, kind="Internal").ap()
    x_m = x.rearrange("b (m p) d -> m p b d", p=P)
    x2_m = x2_d.rearrange("b (m p) d -> m p b d", p=P)
    out_m = out.rearrange("b (m p) d -> m p b d", p=P)
    vs_m = vs_d.rearrange("b (m p) d -> m p b d", p=P)
    ks_m = ks_d.rearrange("k p b (m t) -> m k p b t", t=P)
    os_m = os_d.rearrange("m a b h i t -> m a (b h) i t")
    os_f = os_d.rearrange("m a b h i t -> m a (h i) b t")

    with ExitStack() as ctx:
        def sb(name, shape):
            return ctx.enter_context(nc.sbuf_tensor(name, shape, F32))

        def psum(name, shape):
            return ctx.enter_context(nc.psum_tensor(name, shape, F32))

        def sem(name):
            return ctx.enter_context(nc.semaphore(name))

        w_qkvg = sb("w_qkvg", [P, KT, 4 * HID])
        w_beta = sb("w_beta", [P, KT, NH])
        w_out = sb("w_out", [P, KT, HID])
        col = sb("col", [P, 18])
        hcol = sb("hcol", [P, 8])
        row = sb("row", [1, 2 * HID + P])
        w_x = sb("w_x", [P, KT, 4 * HID])
        w_c = sb("w_c", [P, KT, 4 * HID])
        w_g = sb("w_g", [P, KT, HID])
        w_vo = sb("w_vo", [P, KT, HID])
        q_bias = sb("q_bias", [P, 2 * KT])
        qk_const = sb("qk_const", [1, 1])
        y_bias = sb("y_bias", [1, HID])
        ident = sb("ident", [P, P])
        eps4 = sb("eps4", [P, B])
        mhalf = sb("mhalf", [P, P])
        c0 = sb("c0", [P, KT, P])
        xin = sb("xin", [P, B, HID])
        xnT = sb("xnT", [P, KT, TOK])
        qk = sb("qk", [P, B, 2 * HID])
        sq = sb("sq", [P, 2, 2 * HID])
        ss = sb("ss", [P, B * 2 * NH])
        rn = sb("rn", [P, B * 2 * NH])
        bt = sb("bt", [P, B * NH])
        beta = sb("beta", [P, B * NH])
        kb = sb("kb", [P, B, HID])
        stage = sb("stage", [P, SLOTS, TOK])
        gate = sb("gate", [P, KT, TOK])
        lay = sb("lay", [P, 2, 4, D, HALF])
        dec = sb("dec", [P, 2, U, COL])
        st = sb("st", [P, 2, PAIRS, COL])
        ob = sb("ob", [P, 2, D, HALF])
        oH = sb("oH", [P, 2, KT, TOK])
        nrm = sb("nrm", [P, B, HID])
        ogT = sb("ogT", [P, KT, TOK])
        gl = sb("gl", [P, KT, TOK])
        xr = sb("xr", [P, B, HID])
        n2T = sb("n2T", [P, KT, TOK])
        n3T = sb("n3T", [P, KT, TOK])
        gt = sb("gt", [P, 3, KT * P])
        c_init = sb("c_init", [P, KT])
        cc = sb("cc", [P, KT, P])
        hh = sb("hh", [P, 2, 2 * HID])
        keys = lay[:, :, :, :, :].rearrange("p a b c d -> p (a b c d)").rearrange("p (k b s) -> p k b s", k=KT, b=B)
        vals = st[:, :, :, :].rearrange("p a b c -> p (a b c)")[:, 0:B * NC * HID].rearrange(
            "p (b j d) -> p b j d", b=B, j=NC)
        flat = dec[:, :, :, :].rearrange("p a b c -> p (a b c)")
        prob = flat[:, 0:S]
        probT = flat[:, S:2 * S].rearrange("p (j q) -> p j q", j=NC)
        qT = flat[:, 2 * S:3 * S].rearrange("p (k t) -> p k t", k=KT)
        xq = flat[:, 3 * S:4 * S].rearrange("p (k t) -> p k t", k=KT)
        ao = flat[:, 4 * S:4 * S + HID]
        aoT = flat[:, 4 * S + HID:4 * S + 2 * HID].rearrange("p (k t) -> p k t", k=KT)
        w_raw = oH[:, :, :, :].rearrange("p a b c -> p (a b c)").rearrange("p (w k n) -> p w k n", w=4, k=KT)
        xa = xin
        mx = sb("mx", [P, 2, 8])
        rq = sb("rq", [P, B])

        PB = psum("PB", [P, 2, 512])
        QB = psum("QB", [P, 2, 512])
        FB = psum("FB", [P, 2, 512])
        JB = psum("JB", [P, 2, 512])

        ln_x = LayerNorm(sb, sem, "ln_x")
        ln_o = LayerNorm(sb, sem, "ln_o")
        ln_2 = LayerNorm(sb, sem, "ln_2")
        ln_3 = LayerNorm(sb, sem, "ln_3")

        w_loaded = sem("w_loaded")
        const_set = sem("const_set")
        dve_const = sem("dve_const")
        x_loaded = sem("x_loaded")
        xT_done = sem("xT_done")
        xT_copied = sem("xT_copied")
        qk_mm = sem("qk_mm")
        sq_done = sem("sq_done")
        qk_copied = sem("qk_copied")
        ss_done = sem("ss_done")
        ssmax_done = sem("ssmax_done")
        norm_sqrt = sem("norm_sqrt")
        rn_done = sem("rn_done")
        n3T_free = sem("n3T_free")
        beta_mm = sem("beta_mm")
        bt_done = sem("bt_done")
        beta_done = sem("beta_done")
        v_mm = sem("v_mm")
        g_mm = sem("g_mm")
        tg_done = sem("tg_done")
        gate_done = sem("gate_done")
        gate_spilled = sem("gate_spilled")
        qkn_done = sem("qkn_done")
        kb_done = sem("kb_done")
        turn_done = sem("turn_done")
        staged = sem("staged")
        spilled = [sem(f"spilled{i}") for i in range(SLOTS)]
        lay_loaded = [sem(f"lay_loaded{i}") for i in range(2)]
        kk_done = sem("kk_done")
        dec_done = sem("dec_done")
        inp_done = sem("inp_done")
        scan_done = sem("scan_done")
        carried = sem("carried")
        prod_done = sem("prod_done")
        sum_done = sem("sum_done")
        sum_copied = sem("sum_copied")
        ob_spilled = [sem(f"ob_spilled{i}") for i in range(2)]
        o_loaded = sem("o_loaded")
        gl_loaded = sem("gl_loaded")
        xr_loaded = sem("xr_loaded")
        osum_done = sem("osum_done")
        oT_done = sem("oT_done")
        onT_done = sem("onT_done")
        og_done = sem("og_done")
        gated = sem("gated")
        y_mm = sem("y_mm")
        x1_done = sem("x1_done")
        n2t_done = sem("n2t_done")
        n2T_copied = sem("n2T_copied")
        cell_mm = sem("cell_mm")
        cell_act = sem("cell_act")
        cell_h = sem("cell_h")
        c_done = sem("c_done")
        h_mm = sem("h_mm")
        h_act = sem("h_act")
        x2_done = sem("x2_done")
        x2_stored = sem("x2_stored")
        v_stored = sem("v_stored")
        n3t_done = sem("n3t_done")
        n3T_copied = sem("n3T_copied")
        
        wb_mm = sem("wb_mm")
        wb_done = sem("wb_done")
        keys_loaded = [sem(f"keys_loaded{i}") for i in range(B)]
        vals_loaded = [sem(f"vals_loaded{i}") for i in range(B)]
        xq_loaded = sem("xq_loaded")
        xa_loaded = sem("xa_loaded")
        xa_copied = sem("xa_copied")
        q_mm = sem("q_mm")
        q_copied = sem("q_copied")
        rq_mm = sem("rq_mm")
        rq_done = sem("rq_done")
        score_mm = sem("score_mm")
        max_done = sem("max_done")
        bias_step = sem("bias_step")
        bias_done = sem("bias_done")
        exp_done = sem("exp_done")
        pt_mm = sem("pt_mm")
        pt_act = sem("pt_act")
        pt_dve = sem("pt_dve")
        pv_mm = sem("pv_mm")
        recip_done = sem("recip_done")
        ao_done = sem("ao_done")
        aot_mm = sem("aot_mm")
        aot_copied = sem("aot_copied")
        ya_mm = sem("ya_mm")
        x3_done = sem("x3_done")

        def stages(i, steady=False):
            def stage(lag):
                def call(step, *args):
                    if steady or 0 <= i - lag < NC:
                        step(i - lag, *args)
                return call
            return stage(-1), stage(0), stage(1), stage(2)

        def mlp_before(c):
            return lambda step, *args: step(NC + c - 1, *args)

        def no_mlp(step, *args):
            pass

        def rounds(e, one):
            for i in (-1, 0, 1):
                one(i, *stages(i))
            with e.Fori(2, NC - 1) as i:
                one(i, *stages(i, steady=True))
            for i in (NC - 1, NC, NC + 1):
                one(i, *stages(i))

        NW = 10

        block = ctx.enter_context(nc.Block())

        @block.sync
        def _(sp):
            def load_weights():
                for dst, src in ((ident[:, :], ident_d), (col[:, :], cols), (row[:, :], rows),
                                 (w_qkvg[:, :, :], wqkvg.rearrange("(k p) n -> p k n", p=P)),
                                 (w_beta[:, :, :], wbeta.rearrange("(k p) n -> p k n", p=P)),
                                 (w_out[:, :, :], wout.rearrange("(k p) n -> p k n", p=P)),
                                 (w_x[:, :, :], wx.rearrange("(k p) n -> p k n", p=P)),
                                 (w_c[:, :, :], wc.rearrange("(k p) n -> p k n", p=P))):
                    sp.dma_start(dst, src).then_inc(w_loaded, DMA)
                for k in range(KT):
                    sp.dma_start(w_raw[:, :, k, :], wattn.rearrange("w (k p) n -> k p w n", p=P)[k]).then_inc(w_loaded, DMA)

            def after(*waits):
                waits = [(w, n if isinstance(n, int) else sp.snap(n)) for w, n in waits]
                if not all(isinstance(n, int) for _, n in waits):
                    sp.wait_ge(w_loaded, NW * DMA)
                for w, n in waits:
                    wait(sp, w, n)

            def load_x(m):
                after((xT_done, 2 * m))
                sp.dma_start(xin[:, :, :], x_m[m]).then_inc(x_loaded, DMA)

            def spill_gate(m):
                for ft in range(KT):
                    after((gate_done, 2 * m + ft + 1))
                    sp.dma_start(gs_d[m, :, ft * TOK:(ft + 1) * TOK], gate[:, ft, :]).then_inc(gate_spilled, DMA)

            def spill_item(m, j):
                after((staged, NITEM * m + j + 1))
                for hf in range(2):
                    dst = rs_d[m, hf, j // 2].rearrange("b f t -> f b t")[(j % 2) * P:(j % 2 + 1) * P]
                    src = stage[:, j % SLOTS, :].rearrange("p (b s t) -> p s b t", b=B, s=2)[:, hf]
                    sp.dma_start(dst, src).then_inc(spilled[j % SLOTS], DMA)

            def load_lay(m, hf):
                after(*((sp_, 4 * DMA * (m + 1)) for sp_ in spilled))
                src = rs_d[m, hf].rearrange("w b (h i) t -> (b h) w (i t)", h=NH)
                dst = lay[:, hf].rearrange("p w i t -> p w (i t)")
                n = D * HALF
                sp.dma_start(dst[0:64], src).then_inc(lay_loaded[hf], DMA)
                sp.dma_start(dst[64:128, :, 0:n // 2], src[:, :, n // 2:n]).then_inc(lay_loaded[hf], DMA)
                sp.dma_start(dst[64:128, :, n // 2:n], src[:, :, 0:n // 2]).then_inc(lay_loaded[hf], DMA)

            def spill_sums(m, hf):
                after((sum_copied, NS * m + 2 * hf + 2))
                t = slice(hf * HALF, (hf + 1) * HALF)
                sp.dma_start(os_m[m, 0][:, :, t], ob[0:64, hf]).then_inc(ob_spilled[hf], DMA)
                sp.dma_start(os_m[m, 1][:, 8:16, t], ob[64:128, hf, 0:8]).then_inc(ob_spilled[hf], DMA)
                sp.dma_start(os_m[m, 1][:, 0:8, t], ob[64:128, hf, 8:16]).then_inc(ob_spilled[hf], DMA)

            def load_o(m):
                after(*((ob_spilled[hf], 3 * DMA * (m + 1)) for hf in range(2)))
                if isinstance(m, int) and m == 0:
                    sp.wait_ge(wb_mm, 5)
                for a in (1, 0):
                    for ft in range(KT):
                        sp.dma_start(oH[:, a, ft, :].rearrange("p (b t) -> p b t", b=B),
                                     os_f[m, a][ft * P:(ft + 1) * P]).then_inc(o_loaded, DMA)

            def load_gate(m):
                after((gate_spilled, 2 * DMA * (m + 1)))
                sp.dma_start(gl[:, :, :].rearrange("p k t -> p (k t)"), gs_d[m]).then_inc(gl_loaded, DMA)

            def load_xa(m):
                after((x2_stored, DMA * m))
                sp.dma_start(xr[:, :, :], x_m[m]).then_inc(xr_loaded, DMA)

            def store_xa(m):
                store_x(m, x2_m[m])

            def store_x(M, dst):
                after((x2_done, 2 * (M + 1)))
                sp.dma_start(dst, xr[:, :, :]).then_inc(x2_stored, DMA)

            def store_v(m):
                after((ln_3.norm_done, 4 * (m + 1)))
                sp.dma_start(vs_m[m], nrm[:, :, :]).then_inc(v_stored, DMA)

            def store_k(m):
                for ft in range(KT):
                    after((n3T_copied, 2 * m + ft + 1))
                    sp.dma_start(ks_m[m, ft], n3T[:, ft, :].rearrange("p (b t) -> p b t", b=B)).then_inc(n3T_free, DMA)

            def one(i, pre, main, post, keys_):
                pre(load_x)
                post(spill_sums, 1)
                main(load_lay, 1)
                keys_(store_v)
                keys_(store_k)
                post(load_gate)
                post(load_o)
                post(load_xa)
                pre(spill_item, 0)
                pre(spill_item, 1)
                pre(spill_gate)
                main(spill_sums, 0)
                pre(spill_item, 2)
                pre(spill_item, 3)
                pre(spill_item, 4)
                pre(spill_item, 5)
                pre(spill_item, 6)
                pre(spill_item, 7)
                pre(load_lay, 0)
                post(store_xa)

            def load_queries(c):
                after((rq_mm, c))
                for k in range(KT):
                    sp.dma_start(xq[:, k, :].rearrange("p (b t) -> p b t", b=B), ks_m[c, k]).then_inc(xq_loaded, DMA)

            def load_x2(c):
                first = isinstance(c, int) and c == 0
                after((ln_2.norm_done, 0 if first else 4 * (NC + c)), (xa_copied, c))
                sp.dma_start(xa[:, :, :], x2_m[c]).then_inc(xa_loaded, DMA)

            def store_out(c):
                store_x(NC + c, out_m[c])

            load_weights()
            rounds(sp, one)
            sp.wait_ge(n3T_free, 2 * DMA * (NC + 1))
            sp.wait_ge(v_stored, DMA * NC)
            sp.wait_ge(x2_stored, DMA * NC)
            sp.wait_ge(prod_done, 2 * NS * NC)
            sp.wait_ge(sum_done, NS * NC)
            load_queries(0)
            for b in range(B):
                for k in range(KT):
                    sp.dma_start(keys[:, k, b, :], ks_d[k, :, b, :]).then_inc(keys_loaded[b], DMA)
                sp.dma_start(vals[:, b], vs_d[b].rearrange("(j p) d -> p j d", p=P)).then_inc(vals_loaded[b], DMA)
            load_x2(0)
            load_queries(1)
            with sp.Fori(1, NC - 1) as c:
                load_x2(c)
                load_queries(c + 1)
                store_out(c - 1)
            load_x2(NC - 1)
            store_out(NC - 2)
            store_out(NC - 1)
            sp.wait_ge(x2_stored, 2 * DMA * NC)

        @block.gpsimd
        def _(gp):
            def consts():
                gp.memset(eps4[:, :], EPS).then_inc(const_set, 1)
                gp.memset(mhalf[:, :], -0.5).then_inc(const_set, 1)
                gp.memset(dec[:, :, :, 0:1], 0.0).then_inc(const_set, 1)
                gp.memset(st[:, 0, :, 0:1], 0.0).then_inc(const_set, 1)
                gp.memset(ob[:, :, D - 1, :], 0.0).then_inc(const_set, 1)
                gp.memset(n3T[:, :, 0:1], 0.0).then_inc(n3T_free, 2 * DMA)
                gp.wait_ge(const_set, 5)

            def rstd(L, M):
                gp.wait_ge(L.mv_done, 4 * (M + 1))
                gp.tensor_tensor(L.rs[:, :], L.mv[:, :, 1], eps4[:, :], ALU.add).then_inc(L.var_done, 1)
                gp.wait_ge(L.var_done, M + 1)
                gp.tensor_tensor(L.rs[:, :], L.rs[:, :], mhalf[:, 0:B], ALU.pow).then_inc(L.rstd_done, 1)

            def kk(m, s):
                hf, par, t = s // 2, s % 2, (s % 2) * SUB
                gp.wait_ge(lay_loaded[hf], 3 * DMA * (m + 1))
                wait(gp, scan_done, 2 * NS * m + 2 * s - 2)
                a, b_ = pair_views(lay, hf, K_, t), shifted_views(lay, hf, KB_, t)
                gp.tensor_tensor(pairs_out(dec, par, 0, ND), a(0, ND), b_(0, ND), ALU.mult).then_inc(kk_done, 1)

            def add_halves(m):
                gp.wait_ge(o_loaded, 4 * DMA * (m + 1))
                gp.tensor_tensor(oH[:, 0], oH[:, 0], oH[:, 1], ALU.add).then_inc(osum_done, 1)

            def gating(m):
                gp.wait_ge(gl_loaded, DMA * (m + 1))
                for ft in range(KT):
                    gp.wait_ge(og_done, 2 * m + ft + 1)
                    gp.tensor_tensor(ogT[:, ft], ogT[:, ft], gl[:, ft], ALU.mult).then_inc(gated, 1)

            def add_mlp(M):
                for j in range(2):
                    gp.wait_ge(h_act, 2 * M + j + 1)
                    v = xr[:, 2 * j:2 * j + 2, :].rearrange("p b d -> p (b d)")
                    gp.tensor_tensor(v, v, hh[:, j, :], ALU.add).then_inc(x2_done, 1)

            def norm_x(m):
                rstd(ln_x, m)

            def norm_o(m):
                rstd(ln_o, m)

            def norm_2(M):
                rstd(ln_2, M)

            def norm_3(m):
                rstd(ln_3, m)

            def chunk_b(c):
                rstd(ln_2, NC + c)
                gp.wait_ge(xa_copied, c + 1)
                add_mlp(NC + c)

            def one(i, pre, main, post, keys_):
                pre(norm_x)
                keys_(norm_3)
                main(kk, 1)
                post(add_halves)
                post(norm_o)
                main(kk, 2)
                post(gating)
                post(norm_2)
                main(kk, 3)
                pre(kk, 0)
                post(add_mlp)

            consts()
            rounds(gp, one)
            chunk_b(0)
            with gp.Fori(1, NC) as c:
                chunk_b(c)

        @block.scalar
        def _(act):
            def copy(dst, src, scale=1.0, bias=0.0):
                return act.activation(dst, src, ACT.Identity, scale=scale, bias=bias)

            def copy_xT(m):
                for ft in range(KT):
                    act.wait_ge(xT_done, 2 * m + ft + 1)
                    wait(act, g_mm, 2 * m)
                    copy(xnT[:, ft, :], PB[:, ft, :]).then_inc(xT_copied, 1)

            def copy_qk(m, b):
                act.wait_ge(qk_mm, 4 * m + b + 1)
                wait(act, ss_done, 4 * m + b - 1)
                act.activation(sq[:, b % 2, :], PB[:, b % 2, :], ACT.Square).then_inc(sq_done, 1)
                wait(act, turn_done, 6 * m)
                copy(qk[:, b, :], PB[:, b % 2, :]).then_inc(qk_copied, 1)

            def beta_tanh(m):
                act.wait_ge(beta_mm, m + 1)
                wait(act, beta_done, m)
                act.activation(bt[:, :], PB[:, 0, 0:B * NH], ACT.Tanh, scale=0.5).then_inc(bt_done, 1)

            def copy_v(m, ft):
                act.wait_ge(v_mm, 2 * m + ft + 1)
                to_stage(m, ft, PB[:, 1 - ft, :])

            def gate_tanh(m, ft):
                act.wait_ge(g_mm, 2 * m + ft + 1)
                wait(act, gate_spilled, 2 * DMA * m)
                act.activation(gate[:, ft, :], PB[:, 1 - ft, :], ACT.Tanh, scale=0.5).then_inc(tg_done, 1)

            def head_norms(m):
                act.wait_ge(ssmax_done, m + 1)
                act.activation(rn[:, :], rn[:, :], ACT.Sqrt).then_inc(norm_sqrt, 1)

            def copy_turned(m, j):
                act.wait_ge(turn_done, 6 * m + j + 1)
                to_stage(m, 2 + j, PB[:, (j + 1) % 2, :])

            def to_stage(m, j, src):
                wait(act, spilled[j % SLOTS], 4 * DMA * m + 2 * DMA * (j // SLOTS))
                copy(stage[:, j % SLOTS, :], src).then_inc(staged, 1)

            def decay(m, s):
                act.wait_ge(kk_done, NS * m + s + 1)
                v = dec[:, s % 2, :, 1:COL]
                copy(v, v, scale=-1.0, bias=1.0).then_inc(dec_done, 1)

            def sums(m, s):
                act.wait_ge(sum_done, NS * m + s + 1)
                hf, t = s // 2, (s % 2) * SUB
                wait(act, ob_spilled[hf], 3 * DMA * m)
                copy(ob[:, hf, 0:D - 1, t:t + SUB],
                     JB[:, s % 2, 0:(D - 1) * SUB].rearrange("p (i t) -> p i t", t=SUB)).then_inc(sum_copied, 1)

            def scale_o(m):
                for ft in range(KT):
                    act.wait_ge(onT_done, 2 * m + ft + 1)
                    wait(act, y_mm, 2 * m)
                    copy(ogT[:, ft, :], QB[:, ft, :], scale=hcol[:, ft:ft + 1],
                         bias=hcol[:, 2 + ft:3 + ft]).then_inc(og_done, 1)

            def copy_n2T(M):
                for ft in range(KT):
                    act.wait_ge(n2t_done, 2 * M + ft + 1)
                    wait(act, h_mm, 2 * M)
                    copy(n2T[:, ft, :], QB[:, ft, :]).then_inc(n2T_copied, 1)

            def cell(M, b):
                wait(act, c_done, 4 * M + b)
                for g in range(3):
                    if g != 1:
                        act.wait_ge(cell_mm, 8 * M + 2 * b + (g // 2) + 1)
                    for mt in range(KT):
                        n = g * KT + mt
                        bias = hcol[:, 4 + n:5 + n] if g < 2 else col[:, BC + mt:BC + mt + 1]
                        act.activation(gt[:, g, mt * P:(mt + 1) * P], FB[:, n // 4, (n % 4) * P:(n % 4 + 1) * P],
                                       ACT.Tanh, scale=0.5 if g < 2 else 1.0, bias=bias).then_inc(cell_act, 1)

            def h_tanh(M):
                for j in range(2):
                    act.wait_ge(h_mm, 2 * M + j + 1)
                    wait(act, x2_done, 2 * M)
                    act.activation(hh[:, j, :], QB[:, j, :], ACT.Tanh).then_inc(h_act, 1)

            def keys_out(m):
                for ft in range(KT):
                    act.wait_ge(n3t_done, 2 * m + ft + 1)
                    act.wait_ge(n3T_free, 2 * DMA * (m + 1))
                    copy(n3T[:, ft, :], QB[:, ft, :]).then_inc(n3T_copied, 1)

            def attn_weights():
                act.wait_ge(wb_mm, 5)
                copy(w_g[:, :, :], JB[:, 0, :].rearrange("p (k n) -> p k n", k=KT)).then_inc(wb_done, 1)
                copy(w_vo[:, :, :], JB[:, 1, :].rearrange("p (k n) -> p k n", k=KT)).then_inc(wb_done, 1)
                copy(q_bias[:, :], QB[:, 0, 0:2 * KT]).then_inc(wb_done, 1)
                copy(qk_const[:, :], QB[0:1, 0, 16:17]).then_inc(wb_done, 1)

            def one(i, pre, main, post, keys_):
                pre(copy_xT)
                pre(copy_qk, 0)
                pre(copy_qk, 1)
                pre(copy_qk, 2)
                pre(copy_qk, 3)
                pre(beta_tanh)
                main(decay, 1)
                keys_(keys_out)
                pre(head_norms)
                pre(copy_v, 0)
                pre(copy_v, 1)
                main(sums, 0)
                pre(gate_tanh, 0)
                pre(gate_tanh, 1)
                main(decay, 2)
                post(scale_o)
                pre(copy_turned, 0)
                pre(copy_turned, 1)
                main(sums, 1)
                pre(copy_turned, 2)
                pre(copy_turned, 3)
                pre(copy_turned, 4)
                pre(copy_turned, 5)
                post(copy_n2T)
                main(decay, 3)
                post(cell, 0)
                post(cell, 1)
                main(sums, 2)
                post(cell, 2)
                post(cell, 3)
                pre(decay, 0)
                post(h_tanh)
                main(sums, 3)
                if isinstance(i, int) and i == -1:
                    attn_weights()

            def softmax(c, b):
                n = 4 * c + b
                act.wait_ge(bias_done, n + 1)
                wait(act, pt_mm, 2 * n)
                act.activation(prob, JB[:, :, :].rearrange("p a n -> p (a n)"), ACT.Exp, scale=SCALE,
                               bias=mx[:, b % 2, 2:3], accum_out=mx[:, b % 2, 3:4]).then_inc(exp_done, 1)

            def copy_prob(c, b):
                n = 4 * c + b
                act.wait_ge(pt_mm, 2 * n + 1)
                wait(act, pv_mm, n)
                copy(probT[:, 0:4, :], PB[:, 0, :].rearrange("p (j q) -> p j q", j=4)).then_inc(pt_act, 1)

            def copy_ao(c, b):
                n = 4 * c + b
                act.wait_ge(aot_mm, n + 1)
                wait(act, ya_mm, n)
                copy(aoT[:, :, :], QB[:, 1, 0:HID].rearrange("p (k t) -> p k t", k=KT)).then_inc(aot_copied, 1)

            def copy_q(c):
                for et in range(KT):
                    act.wait_ge(q_mm, 2 * c + et + 1)
                    wait(act, score_mm, 4 * c)
                    copy(qT[:, et, :], PB[:, et, :], bias=q_bias[:, et:et + 1]).then_inc(q_copied, 1)

            def copy_xa(M):
                act.wait_ge(x3_done, 4 * (M - NC + 1))
                act.wait_ge(x2_stored, DMA * M)
                copy(xr[:, :, :], xa[:, :, :]).then_inc(xa_copied, 1)

            def chunk_b(c, mlp_of, last=False):
                mlp_of(copy_xa)
                copy_prob(c, 0)
                softmax(c, 1)
                mlp_of(copy_n2T)
                copy_ao(c, 0)
                mlp_of(cell, 0)
                copy_prob(c, 1)
                softmax(c, 2)
                mlp_of(cell, 1)
                copy_ao(c, 1)
                copy_prob(c, 2)
                softmax(c, 3)
                mlp_of(cell, 2)
                copy_ao(c, 2)
                mlp_of(cell, 3)
                copy_prob(c, 3)
                if not last:
                    copy_q(c + 1)
                    softmax(c + 1, 0)
                mlp_of(h_tanh)
                copy_ao(c, 3)

            act.wait_ge(dve_const, 6)
            rounds(act, one)
            copy_q(0)
            softmax(0, 0)
            chunk_b(0, no_mlp)
            with act.Fori(1, NC - 1) as c:
                chunk_b(c, mlp_before(c))
            chunk_b(NC - 1, mlp_before(NC - 1), last=True)
            copy_xa(2 * NC - 1)
            copy_n2T(2 * NC - 1)
            for b in range(B):
                cell(2 * NC - 1, b)
            h_tanh(2 * NC - 1)

        @block.tensor
        def _(pe):
            def mm(dst, lhsT, rhs, start, stop):
                return pe.matmul(dst, lhsT, rhs, start=start, stop=stop, skip_group_check=True)

            def turn_tiles(bank, src, ft):
                for b in range(B):
                    i = pe.transpose(bank[:, b * P:(b + 1) * P], src[:, b, ft * P:(ft + 1) * P], ident[:, :])
                return i

            def turn_x(m):
                pe.wait_ge(ln_x.norm_done, 4 * (m + 1))
                for ft in range(KT):
                    wait(pe, staged, NITEM * m - ft)
                    turn_tiles(PB[:, ft, :], xin, ft).then_inc(xT_done, 1)

            def project_qk(m):
                pe.wait_ge(xT_copied, 2 * (m + 1))
                for b in range(B):
                    if b >= 2:
                        pe.wait_ge(qk_copied, 4 * m + b - 1)
                    for k in range(KT):
                        i = mm(PB[:, b % 2, :], xnT[:, k, b * P:(b + 1) * P], w_qkvg[:, k, 0:2 * HID],
                               k == 0, k == KT - 1)
                    i.then_inc(qk_mm, 1)
                pe.wait_ge(qk_copied, 4 * m + 3)
                for b in range(B):
                    for k in range(KT):
                        i = mm(PB[:, 0, b * NH:(b + 1) * NH], xnT[:, k, b * P:(b + 1) * P], w_beta[:, k, :],
                               b == 0 and k == 0, k == KT - 1)
                i.then_inc(beta_mm, 1)

            def project_t(m, n, ft, done):
                if n == 2 and ft == 0:
                    pe.wait_ge(qk_copied, 4 * m + 4)
                elif n == 2:
                    pe.wait_ge(bt_done, m + 1)
                else:
                    pe.wait_ge(staged, NITEM * m + ft + 1)
                for k in range(KT):
                    w = w_qkvg[:, k, n * HID + ft * P:n * HID + (ft + 1) * P]
                    i = mm(PB[:, 1 - ft, :], w, xnT[:, k, :], k == 0, k == KT - 1)
                i.then_inc(done, 1)

            def project_v(m, ft):
                project_t(m, 2, ft, v_mm)

            def project_g(m, ft):
                project_t(m, 3, ft, g_mm)

            def turn_qk(m, j):
                if j < 2:
                    pe.wait_ge(qkn_done, m + 1)
                    pe.wait_ge(gate_done, 2 * m + j + 1)
                else:
                    pe.wait_ge(staged, NITEM * m + j + 1)
                if j == 4:
                    pe.wait_ge(kb_done, m + 1)
                src = (qk[:, :, 0:HID], qk[:, :, HID:2 * HID], kb[:, :, :])[j // 2]
                turn_tiles(PB[:, (j + 1) % 2, :], src, j % 2).then_inc(turn_done, 1)

            def attn_weights():
                for d in range(KT):
                    for k in range(KT):
                        i = mm(JB[:, 0, d * HID:(d + 1) * HID], w_raw[:, 0, k, d * P:(d + 1) * P], w_raw[:, 1, k, :],
                               d == 0 and k == 0, k == KT - 1)
                i.then_inc(wb_mm, 1)
                for d in range(KT):
                    for k in range(KT):
                        i = mm(JB[:, 1, d * HID:(d + 1) * HID], w_raw[:, 2, k, d * P:(d + 1) * P], w_raw[:, 3, k, :],
                               d == 0 and k == 0, k == KT - 1)
                i.then_inc(wb_mm, 1)
                for w, bias, at in ((1, BQ, 0), (0, BK, 2)):
                    for d in range(KT):
                        for k in range(KT):
                            i = mm(QB[:, 0, at + d:at + d + 1], w_raw[:, w, k, d * P:(d + 1) * P],
                                   col[:, bias + k:bias + k + 1], at + d + k == 0, k == KT - 1)
                i.then_inc(wb_mm, 1)
                for k in range(KT):
                    i = mm(QB[0:1, 0, 16:17], col[:, BQ + k:BQ + k + 1], col[:, BK + k:BK + k + 1], False, k == KT - 1)
                i.then_inc(wb_mm, 1)
                for k in range(KT):
                    i = mm(QB[0:1, 1, 0:HID], col[:, BV + k:BV + k + 1], w_raw[:, 3, k, :], k == 0, k == KT - 1)
                i.then_inc(wb_mm, 1)

            def sum_j(m, s, part=None):
                if not part:
                    pe.wait_ge(prod_done, 2 * NS * m + 2 * s + 2)
                    wait(pe, sum_copied, NS * m + s - 1)
                    if isinstance(m, int) and m == 0 and s < 2:
                        pe.wait_ge(wb_done, 5)
                par = s % 2
                order = [(0, 0)] + [(1, d) for d in range(ND - 2, 0, -1)] + [(0, d) for d in range(1, ND)]
                for n, (mirror, d) in enumerate(order):
                    if part is not None and n * PARTS // len(order) != part:
                        continue
                    at = U + (d - 1) * NI if mirror else d * NI
                    lo = d if mirror else 0
                    i = mm(JB[:, par, lo * SUB:(lo + NI) * SUB], ident[:, :], st[:, par, at:at + NI, 1:COL],
                           n == 0, n == len(order) - 1)
                if part is None or part == PARTS - 1:
                    i.then_inc(sum_done, 1)

            def turn_o(m):
                pe.wait_ge(osum_done, m + 1)
                if isinstance(m, int) and m == 0:
                    pe.wait_ge(wb_done, 5)
                for j in range(2):
                    wait(pe, n3T_copied, 2 * m)
                    for b in (2 * j, 2 * j + 1):
                        for ft in range(KT):
                            i = pe.transpose(QB[:, j, (b % 2) * HID + ft * P:(b % 2) * HID + (ft + 1) * P],
                                             oH[:, 0, ft, b * P:(b + 1) * P], ident[:, :])
                    i.then_inc(oT_done, 1)

            def turn_on(m):
                pe.wait_ge(ln_o.norm_done, 4 * (m + 1))
                for ft in range(KT):
                    turn_tiles(QB[:, ft, :], nrm, ft).then_inc(onT_done, 1)

            def project_o(m):
                pe.wait_ge(gated, 2 * (m + 1))
                for j in range(2):
                    for b in (2 * j, 2 * j + 1):
                        for k in range(KT):
                            i = mm(QB[:, j, (b % 2) * HID:(b % 2 + 1) * HID], ogT[:, k, b * P:(b + 1) * P],
                                   w_out[:, k, :], b % 2 == 0 and k == 0, k == KT - 1)
                    i.then_inc(y_mm, 1)

            def turn_n2(M):
                pe.wait_ge(ln_2.norm_done, 4 * (M + 1))
                for ft in range(KT):
                    turn_tiles(QB[:, ft, :], nrm, ft).then_inc(n2t_done, 1)

            def cell_x(M, b):
                pe.wait_ge(n2T_copied, 2 * (M + 1))
                wait(pe, cell_act, 24 * M + 6 * b)
                for n in range(3 * KT):
                    for k in range(KT):
                        mm(FB[:, n // 4, (n % 4) * P:(n % 4 + 1) * P], w_x[:, k, n * P:(n + 1) * P],
                           n2T[:, k, b * P:(b + 1) * P], n % 4 == 0 and k == 0, False)

            def cell_c(M, b):
                if b:
                    pe.wait_ge(c_done, 4 * M + b)
                cell = cc if b else c0
                for n in range(3 * KT):
                    for k in range(KT):
                        i = mm(FB[:, n // 4, (n % 4) * P:(n % 4 + 1) * P], w_c[:, k, n * P:(n + 1) * P],
                               cell[:, k, :], False, k == KT - 1)
                    if n in (3, 5):
                        i.then_inc(cell_mm, 1)

            def hidden(M):
                pe.wait_ge(c_done, 4 * (M + 1))
                for j in range(2):
                    for b in (2 * j, 2 * j + 1):
                        dst = QB[:, j, (b % 2) * HID:(b % 2 + 1) * HID]
                        for k in range(KT):
                            mm(dst, n2T[:, k, b * P:(b + 1) * P], w_x[:, k, 3 * HID:4 * HID], b % 2 == 0 and k == 0, False)
                        for k in range(KT):
                            mm(dst, cc[:, k, :], w_c[:, k, 3 * HID:4 * HID], False, False)
                        i = mm(dst, row[:, 2 * HID:2 * HID + P], row[:, 0:HID], False, True)
                    i.then_inc(h_mm, 1)

            def keys_out(m):
                pe.wait_ge(ln_3.norm_done, 4 * (m + 1))
                pe.wait_ge(h_act, 2 * (m + 1))
                for ft in range(KT):
                    turn_tiles(QB[:, ft, :], nrm, ft).then_inc(n3t_done, 1)

            def one(i, pre, main, post, keys_):
                pre(turn_x)
                pre(project_qk)
                keys_(keys_out)
                pre(project_v, 0)
                pre(project_v, 1)
                post(turn_o)
                main(sum_j, 0)
                pre(project_g, 0)
                pre(project_g, 1)
                post(turn_on)
                post(project_o)
                main(sum_j, 1)
                pre(turn_qk, 0)
                pre(turn_qk, 1)
                pre(turn_qk, 2)
                pre(turn_qk, 3)
                pre(turn_qk, 4)
                pre(turn_qk, 5)
                post(turn_n2)
                post(cell_x, 0)
                post(cell_c, 0)
                main(sum_j, 2, 0)
                post(cell_x, 1)
                main(sum_j, 2, 1)
                post(cell_c, 1)
                main(sum_j, 2, 2)
                post(cell_x, 2)
                main(sum_j, 2, 3)
                post(cell_c, 2)
                post(cell_x, 3)
                post(cell_c, 3)
                post(hidden)
                main(sum_j, 3)
                if isinstance(i, int) and i == -1:
                    attn_weights()

            def score(c, b):
                n = 4 * c + b
                wait(pe, exp_done, n)
                if isinstance(c, int) and c == 0:
                    pe.wait_ge(keys_loaded[b], 2 * DMA)
                if b == 0:
                    pe.wait_ge(q_copied, 2 * (c + 1))
                for j in range(2):
                    for k in range(KT):
                        i = mm(JB[:, j, :], qT[:, k, b * P:(b + 1) * P], keys[:, k, b, j * 512:(j + 1) * 512],
                               k == 0, k == KT - 1)
                i.then_inc(score_mm, 1)

            def turn_prob(c, b):
                n = 4 * c + b
                pe.wait_ge(exp_done, n + 1)
                for j in range(2):
                    wait(pe, (pt_act, pt_dve)[j], n)
                    if b == 0:
                        pe.wait_ge(q_copied, 2 * (c + 1))
                        pe.wait_ge(rq_done, c + 1)
                    for t in range(4):
                        i = pe.transpose(PB[:, j, t * P:(t + 1) * P], prob[:, (4 * j + t) * P:(4 * j + t + 1) * P],
                                         ident[:, :])
                    i.then_inc(pt_mm, 1)

            def attend(c, b):
                n = 4 * c + b
                pe.wait_ge(pt_act, n + 1)
                pe.wait_ge(pt_dve, n + 1)
                wait(pe, x3_done, n)
                if isinstance(c, int) and c == 0:
                    pe.wait_ge(vals_loaded[b], DMA)
                if not (isinstance(c, int) and c == 0):
                    if b == 0:
                        pe.wait_ge(n2T_copied, 2 * (NC + c))
                    if b == B - 1:
                        pe.wait_ge(h_act, 2 * (NC + c))
                for t in range(NC):
                    i = mm(QB[:, 0, 0:HID], probT[:, t, :], vals[:, b, t, :], t == 0, t == NC - 1)
                i.then_inc(pv_mm, 1)

            def turn_ao(c, b):
                n = 4 * c + b
                pe.wait_ge(ao_done, n + 1)
                for k in range(KT):
                    i = pe.transpose(QB[:, 1, k * P:(k + 1) * P], ao[:, k * P:(k + 1) * P], ident[:, :])
                i.then_inc(aot_mm, 1)

            def project_y(c, b):
                n = 4 * c + b
                pe.wait_ge(aot_copied, n + 1)
                for k in range(KT):
                    mm(QB[:, 0, HID:2 * HID], aoT[:, k, :], w_vo[:, k, :], k == 0, False)
                mm(QB[:, 0, HID:2 * HID], row[:, 2 * HID:2 * HID + P], y_bias[:, :], False, True).then_inc(ya_mm, 1)

            def queries(c):
                pe.wait_ge(xq_loaded, 2 * DMA * (c + 1))
                wait(pe, pt_act, 4 * c)
                wait(pe, pt_dve, 4 * c)
                for et in range(KT):
                    for k in range(KT):
                        i = mm(PB[:, et, :], w_g[:, k, et * P:(et + 1) * P], xq[:, k, :], k == 0, k == KT - 1)
                    i.then_inc(q_mm, 1)
                pe.wait_ge(q_copied, 2 * c + 1)
                for b in range(B):
                    for k in range(KT):
                        mm(PB[:, 0, b:b + 1], xq[:, k, b * P:(b + 1) * P], q_bias[:, 2 + k:3 + k], b == 0 and k == 0, False)
                    i = mm(PB[:, 0, b:b + 1], row[:, 2 * HID:2 * HID + P], qk_const[:, :], False, True)
                i.then_inc(rq_mm, 1)

            def chunk_b(c, mlp_of, last=False):
                turn_prob(c, 0)
                score(c, 1)
                wait(pe, x3_done, 4 * c)
                mlp_of(turn_n2)
                attend(c, 0)
                mlp_of(cell_x, 0)
                turn_ao(c, 0)
                mlp_of(cell_c, 0)
                project_y(c, 0)
                turn_prob(c, 1)
                score(c, 2)
                mlp_of(cell_x, 1)
                attend(c, 1)
                mlp_of(cell_c, 1)
                turn_ao(c, 1)
                project_y(c, 1)
                turn_prob(c, 2)
                score(c, 3)
                mlp_of(cell_x, 2)
                attend(c, 2)
                mlp_of(cell_c, 2)
                turn_ao(c, 2)
                project_y(c, 2)
                turn_prob(c, 3)
                mlp_of(cell_x, 3)
                mlp_of(cell_c, 3)
                if not last:
                    queries(c + 1)
                    score(c + 1, 0)
                pe.wait_ge(x3_done, 4 * c + 3)
                mlp_of(hidden)
                attend(c, 3)
                turn_ao(c, 3)
                project_y(c, 3)

            pe.wait_ge(w_loaded, NW * DMA)
            pe.wait_ge(dve_const, 6)
            rounds(pe, one)
            pe.wait_ge(staged, NITEM * NC)
            pe.wait_ge(sum_copied, NS * NC)
            pe.wait_ge(n3T_copied, 2 * NC)
            queries(0)
            score(0, 0)
            chunk_b(0, no_mlp)
            with pe.Fori(1, NC - 1) as c:
                chunk_b(c, mlp_before(c))
            chunk_b(NC - 1, mlp_before(NC - 1), last=True)
            pe.wait_ge(x3_done, 4 * NC)
            turn_n2(2 * NC - 1)
            for b in range(B):
                cell_x(2 * NC - 1, b)
                cell_c(2 * NC - 1, b)
            hidden(2 * NC - 1)

        @block.vector
        def _(dve):
            def norm_stats(L, M, src, ready, lag=0):
                if isinstance(M, int) or not lag:
                    wait(dve, L.norm_done, 4 * M)
                else:
                    dve.wait_ge(prod_done, 2 * NS * (M + lag))
                for b in range(B):
                    ready(b)
                    dve.bn_stats(L.stats[:, b, :], src(b)).then_inc(L.stat_done, 1)
                dve.wait_ge(L.stat_done, 4 * (M + 1))
                if isinstance(M, int) or not lag:
                    wait(dve, L.settled, M)
                dve.tensor_copy(L.last[:, :], L.stats[:, B - 1, 0:1]).then_inc(L.settled, 1)
                for b in range(B):
                    dve.bn_aggr(L.mv[:, b, :], L.stats[:, b, :]).then_inc(L.mv_done, 1)

            def norm_apply(L, M, src, dst):
                dve.wait_ge(L.rstd_done, M + 1)
                dve.wait_ge(L.mv_done, 4 * (M + 1))
                for b in range(B):
                    dve.tensor_scalar(dst(b), src(b), L.mv[:, b, 0:1], L.rs[:, b:b + 1],
                                      ALU.subtract, ALU.mult).then_inc(L.norm_done, 1)

            def tile(t):
                return lambda b: t[:, b, :]

            def consts():
                dve.wait_ge(w_loaded, NW * DMA)
                dve.tensor_scalar(hcol[:, 0:4], col[:, LNG:LNG + 4], 0.5, None, ALU.mult).then_inc(dve_const, 1)
                dve.tensor_scalar(hcol[:, 4:8], col[:, BF:BF + 4], 0.5, None, ALU.mult).then_inc(dve_const, 1)
                dve.tensor_scalar(w_c[:, :, :], w_c[:, :, :], 0.5, None, ALU.mult).then_inc(dve_const, 1)
                dve.tensor_scalar(c_init[:, :], col[:, INC:INC + 2], 2.0, None, ALU.mult).then_inc(dve_const, 1)
                dve.wait_ge(dve_const, 4)
                dve.wait_ge(const_set, 5)
                for k in range(KT):
                    dve.tensor_scalar(c0[:, k, :], mhalf[:, :], 0.0, c_init[:, k:k + 1], ALU.mult, ALU.add).then_inc(dve_const, 1)
                dve.wait_ge(dve_const, 6)

            def x_stats(m):
                norm_stats(ln_x, m, tile(xin), lambda b: dve.wait_ge(x_loaded, DMA * (m + 1)))

            def x_norm(m):
                norm_apply(ln_x, m, tile(xin), tile(xin))

            def square_sums(m, b):
                dve.wait_ge(sq_done, 4 * m + b + 1)
                wait(dve, ssmax_done, m)
                dve.tensor_reduce(ss[:, b * 32:(b + 1) * 32], sq[:, b % 2, :].rearrange("p (h i) -> p h i", i=D),
                                  AX.X, ALU.add).then_inc(ss_done, 1)

            def head_guard(m):
                dve.wait_ge(ss_done, 4 * (m + 1))
                wait(dve, qkn_done, m)
                dve.tensor_scalar(rn[:, :], ss[:, :], 1e-24, None, ALU.max).then_inc(ssmax_done, 1)

            def make_beta(m):
                dve.wait_ge(bt_done, m + 1)
                wait(dve, kb_done, m)
                dve.tensor_scalar(beta[:, :], bt[:, :], 0.5, 0.5, ALU.mult, ALU.add).then_inc(beta_done, 1)

            def make_gate(m, ft):
                dve.wait_ge(tg_done, 2 * m + ft + 1)
                dve.scalar_tensor_tensor(out=gate[:, ft, :], in0=gate[:, ft, :], scalar=1.0, in1=PB[:, 1 - ft, :],
                                         op0=ALU.add, op1=ALU.mult).then_inc(gate_done, 1)

            def head_recip(m):
                dve.wait_ge(norm_sqrt, m + 1)
                dve.reciprocal(rn[:, :], rn[:, :]).then_inc(rn_done, 1)

            def scale_qk(m):
                dve.wait_ge(rn_done, m + 1)
                dve.wait_ge(qk_copied, 4 * (m + 1))
                v = qk[:, :, :].rearrange("p b (h i) -> p (b h) i", i=D)
                dve.tensor_tensor(v, v, rn[:, :].unsqueeze(2).broadcast_to([P, B * 2 * NH, D]),
                                  ALU.mult).then_inc(qkn_done, 1)

            def scale_kb(m):
                dve.wait_ge(qkn_done, m + 1)
                dve.wait_ge(beta_done, m + 1)
                wait(dve, turn_done, 6 * m)
                dve.tensor_tensor(kb[:, :, :].rearrange("p b (h i) -> p b h i", i=D),
                                  qk[:, :, HID:2 * HID].rearrange("p b (h i) -> p b h i", i=D),
                                  beta[:, :].rearrange("p (b h) -> p b h", b=B).unsqueeze(3).broadcast_to([P, B, NH, D]),
                                  ALU.mult).then_inc(kb_done, 1)

            def views(w, s):
                return pair_views(lay, s // 2, w, (s % 2) * SUB), shifted_views(lay, s // 2, w, (s % 2) * SUB)

            def inputs(m, s, mirror):
                v, v_sh = views(V_, s)
                b_, b_sh = views(KB_, s)
                if not mirror:
                    dve.wait_ge(lay_loaded[s // 2], 3 * DMA * (m + 1))
                    wait(dve, sum_done, NS * m + s - 1)
                    dve.tensor_tensor(pairs_out(st, s % 2, 0, ND), v(0, ND), b_sh(0, ND), ALU.mult).then_inc(inp_done, 1)
                else:
                    dve.tensor_tensor(pairs_out(st, s % 2, U, ND - 2), v_sh(1, ND - 1), b_(1, ND - 1),
                                      ALU.mult).then_inc(inp_done, 1)

            def scan(m, s, mirror):
                n, par = NS * m + s, s % 2
                if not mirror:
                    dve.wait_ge(dec_done, n + 1)
                    dve.wait_ge(inp_done, 2 * n + 2)
                    wait(dve, carried, n)
                a = dec[:, par, NI:NI + MIR, :] if mirror else dec[:, par, :, :]
                v = st[:, par, U:PAIRS, :] if mirror else st[:, par, 0:U, :]
                a, v = a.rearrange("p r t -> p (r t)"), v.rearrange("p r t -> p (r t)")
                dve.tensor_tensor_scan(v, a, v, 0.0, ALU.mult, ALU.add).then_inc(scan_done, 1)

            def carry(m, s):
                n, par = NS * m + s, s % 2
                dve.wait_ge(scan_done, 2 * n + 2)
                dve.tensor_copy(st[:, 1 - par, :, 0:1], st[:, par, :, SUB:COL]).then_inc(carried, 1)

            def outputs(m, s, mirror):
                q, q_sh = views(Q_, s)
                if not mirror:
                    dve.wait_ge(carried, NS * m + s + 1)
                    v = pairs_out(st, s % 2, 0, ND)
                    dve.tensor_tensor(v, v, q_sh(0, ND), ALU.mult).then_inc(prod_done, 1)
                else:
                    v = pairs_out(st, s % 2, U, ND - 2)
                    dve.tensor_tensor(v, v, q(1, ND - 1), ALU.mult).then_inc(prod_done, 1)

            def o_tile(b):
                return QB[:, b // 2, (b % 2) * HID:(b % 2 + 1) * HID]

            def o_stats(m):
                norm_stats(ln_o, m, o_tile, lambda b: dve.wait_ge(oT_done, 2 * m + b // 2 + 1))

            def o_norm(m):
                wait(dve, n3t_done, 2 * m)
                wait(dve, v_stored, DMA * m)
                norm_apply(ln_o, m, o_tile, tile(nrm))

            def add_y(m):
                dve.wait_ge(xr_loaded, DMA * (m + 1))
                for j in range(2):
                    dve.wait_ge(y_mm, 2 * m + j + 1)
                    v = xr[:, 2 * j:2 * j + 2, :].rearrange("p b d -> p (b d)")
                    dve.tensor_tensor(v, v, QB[:, j, :], ALU.add).then_inc(x1_done, 1)

            def n2_stats(m):
                norm_stats(ln_2, m, tile(xr), lambda b: dve.wait_ge(x1_done, 2 * m + b // 2 + 1))

            def n2_norm(m):
                dve.wait_ge(onT_done, 2 * (m + 1))
                norm_apply(ln_2, m, tile(xr), tile(nrm))

            def cell(M, b):
                before = cc if b else c0
                dve.wait_ge(cell_act, 24 * M + 6 * b + 6)
                wait(dve, c_done, 4 * M + b)
                c_in = before[:, :, :].rearrange("p k t -> p (k t)")
                dve.scalar_tensor_tensor(out=gt[:, 0, :], in0=gt[:, 0, :], scalar=1.0, in1=c_in,
                                         op0=ALU.add, op1=ALU.mult).then_inc(cell_h, 1)
                dve.scalar_tensor_tensor(out=gt[:, 1, :], in0=gt[:, 1, :], scalar=1.0, in1=gt[:, 2, :],
                                         op0=ALU.add, op1=ALU.mult).then_inc(cell_h, 1)
                dve.wait_ge(cell_h, 8 * M + 2 * b + 2)
                if b == 0:
                    wait(dve, h_mm, 2 * M)
                dve.scalar_tensor_tensor(out=cc[:, :, :].rearrange("p k t -> p (k t)"), in0=gt[:, 0, :], scalar=0.5,
                                         in1=gt[:, 1, :], op0=ALU.mult, op1=ALU.add).then_inc(c_done, 1)

            def n3_stats(m):
                norm_stats(ln_3, m, tile(xr), lambda b: dve.wait_ge(x2_done, 2 * m + b // 2 + 1), lag=2)

            def n3_norm(m):
                dve.wait_ge(n2t_done, 2 * (m + 1))
                norm_apply(ln_3, m, tile(xr), tile(nrm))

            def one(i, pre, main, post, keys_):
                pre(x_stats)
                main(inputs, 0, False)
                main(inputs, 0, True)
                pre(x_norm)
                keys_(n3_stats)
                main(scan, 0, False)
                main(scan, 0, True)
                main(carry, 0)
                keys_(n3_norm)
                main(outputs, 0, False)
                main(outputs, 0, True)
                pre(square_sums, 0)
                pre(square_sums, 1)
                main(inputs, 1, False)
                pre(square_sums, 2)
                pre(square_sums, 3)
                pre(head_guard)
                pre(make_beta)
                main(inputs, 1, True)
                post(o_stats)
                main(scan, 1, False)
                main(scan, 1, True)
                main(carry, 1)
                post(o_norm)
                pre(head_recip)
                main(outputs, 1, False)
                main(outputs, 1, True)
                pre(make_gate, 0)
                pre(make_gate, 1)
                pre(scale_qk)
                main(inputs, 2, False)
                main(inputs, 2, True)
                pre(scale_kb)
                post(add_y)
                post(n2_stats)
                main(scan, 2, False)
                main(scan, 2, True)
                main(carry, 2)
                post(n2_norm)
                main(outputs, 2, False)
                main(outputs, 2, True)
                main(inputs, 3, False)
                post(cell, 0)
                main(inputs, 3, True)
                post(cell, 1)
                main(scan, 3, False)
                post(cell, 2)
                main(scan, 3, True)
                main(carry, 3)
                main(outputs, 3, False)
                post(cell, 3)
                main(outputs, 3, True)
                if isinstance(i, int) and i == -1:
                    dve.wait_ge(wb_mm, 5)
                    dve.tensor_tensor(y_bias[:, :], row[:, HID:2 * HID], QB[0:1, 1, 0:HID], ALU.add).then_inc(wb_done, 1)

            def row_max(c, b):
                n = 4 * c + b
                m_ = mx[:, b % 2, :]
                dve.wait_ge(score_mm, n + 1)
                wait(dve, recip_done, n - 1)
                dve.tensor_reduce(m_[:, 0:1], JB[:, :, :], AX.XY, ALU.max).then_inc(max_done, 1)
                dve.wait_ge(max_done, n + 1)
                dve.tensor_tensor(m_[:, 1:2], m_[:, 0:1], rq[:, b:b + 1], ALU.add).then_inc(bias_step, 1)
                dve.wait_ge(bias_step, 2 * n + 1)
                dve.tensor_tensor(m_[:, 1:2], rq[:, b:b + 1], m_[:, 1:2], ALU.subtract).then_inc(bias_step, 1)
                dve.wait_ge(bias_step, 2 * n + 2)
                dve.tensor_scalar(m_[:, 2:3], m_[:, 1:2], SCALE, None, ALU.mult).then_inc(bias_done, 1)

            def copy_prob(c, b):
                n = 4 * c + b
                dve.wait_ge(pt_mm, 2 * n + 2)
                wait(dve, pv_mm, n)
                dve.tensor_copy(probT[:, 4:8, :], PB[:, 1, :].rearrange("p (j q) -> p j q", j=4)).then_inc(pt_dve, 1)

            def scale_ao(c, b):
                n = 4 * c + b
                dve.wait_ge(exp_done, n + 1)
                dve.reciprocal(mx[:, b % 2, 4:5], mx[:, b % 2, 3:4]).then_inc(recip_done, 1)
                dve.wait_ge(recip_done, n + 1)
                dve.wait_ge(pv_mm, n + 1)
                wait(dve, aot_mm, n)
                dve.tensor_scalar(ao, QB[:, 0, 0:HID], mx[:, b % 2, 4:5], None, ALU.mult).then_inc(ao_done, 1)

            def add_ya(c, b):
                n = 4 * c + b
                dve.wait_ge(xa_loaded, DMA * (c + 1))
                dve.wait_ge(ya_mm, n + 1)
                dve.tensor_tensor(xa[:, b, :], xa[:, b, :], QB[:, 0, HID:2 * HID], ALU.add).then_inc(x3_done, 1)

            def copy_rq(c):
                dve.wait_ge(rq_mm, c + 1)
                wait(dve, bias_done, 4 * c)
                dve.tensor_copy(rq[:, :], PB[:, 0, 0:B]).then_inc(rq_done, 1)
                dve.wait_ge(rq_done, c + 1)

            def xa_stats(M):
                norm_stats(ln_2, M, tile(xa), lambda b: dve.wait_ge(x3_done, 4 * (M - NC) + b + 1))

            def xa_norm(M):
                dve.wait_ge(n2t_done, 2 * M)
                if isinstance(M, int) and M == NC:
                    dve.wait_ge(n3t_done, 2 * NC)
                    dve.wait_ge(v_stored, DMA * NC)
                norm_apply(ln_2, M, tile(xa), tile(nrm))

            def chunk_b(c, mlp_of, last=False):
                mlp_of(xa_stats)
                copy_prob(c, 0)
                mlp_of(xa_norm)
                row_max(c, 1)
                scale_ao(c, 0)
                add_ya(c, 0)
                mlp_of(cell, 0)
                copy_prob(c, 1)
                row_max(c, 2)
                scale_ao(c, 1)
                mlp_of(cell, 1)
                add_ya(c, 1)
                copy_prob(c, 2)
                row_max(c, 3)
                scale_ao(c, 2)
                add_ya(c, 2)
                mlp_of(cell, 2)
                copy_prob(c, 3)
                mlp_of(cell, 3)
                if not last:
                    copy_rq(c + 1)
                    row_max(c + 1, 0)
                scale_ao(c, 3)
                add_ya(c, 3)

            consts()
            rounds(dve, one)
            copy_rq(0)
            row_max(0, 0)
            chunk_b(0, no_mlp)
            with dve.Fori(1, NC - 1) as c:
                chunk_b(c, mlp_before(c))
            chunk_b(NC - 1, mlp_before(NC - 1), last=True)
            xa_stats(2 * NC - 1)
            xa_norm(2 * NC - 1)
            for b in range(B):
                cell(2 * NC - 1, b)


def _lay_view(lay, hf, w, t, pattern, first):
    base = lay[:, hf, w, first:first + 1, t:t + SUB]
    return bass.AP(base.tensor, base.offset, [list(base.ap[0])] + pattern)


def pair_views(lay, hf, w, t):
    return lambda d0, nd: _lay_view(lay, hf, w, t, [[0, nd if d0 == 0 else nd - d0], [HALF, NI], [1, SUB]], 0)


def shifted_views(lay, hf, w, t):
    return lambda d0, nd: _lay_view(lay, hf, w, t, [[HALF, nd if d0 == 0 else nd - d0], [HALF, NI], [1, SUB]], d0)


def pairs_out(buf, par, at, nd):
    return buf[:, par, at:at + nd * NI, 1:COL].rearrange("p (d i) t -> p d i t", i=NI)


def kernel(**inputs):
    import numpy as np
    import concourse.bacc as bacc
    from concourse.bass_utils import run_bass_kernel_spmd

    f = {k: np.asarray(v) for k, v in inputs.items()}
    a = lambda n: f["L0_attn_a_" + n]
    b = lambda n: f["L0_attn_b_" + n]
    w = lambda n: f["L0_ffn_" + n]
    cols = [a("ln_g"), a("ln_b"), w("bf"), w("bi"), w("bc"), w("in_c"), b("b_q"), b("b_k"), b("b_v")]
    arrays = {
        "x": a("x"),
        "wqkvg": np.concatenate([a("Wq"), a("Wk"), a("Wv"), a("Wg")], axis=1),
        "wbeta": a("Wbeta"),
        "wout": a("Wout"),
        "cols": np.concatenate([v.reshape(KT, P).T for v in cols], axis=1),
        "rows": np.concatenate([w("bo"), b("b_out"), np.ones(P, np.float32)])[None, :],
        "wx": np.concatenate([w("wf").T, w("wi").T, w("wc").T, w("wo").T], axis=1),
        "wc": np.concatenate([w("uf").T, w("ui").T, w("uc").T, w("uo").T], axis=1),
        "wattn": np.stack([b("w_q"), b("w_k"), b("w_v"), b("w_out").T]),
        "ident": np.eye(P, dtype=np.float32),
    }
    arrays = {k: np.ascontiguousarray(v) for k, v in arrays.items()}
    nc = bacc.Bacc("TRN2", target_bir_lowering=False, num_devices=1)
    args = [nc.dram_tensor("in_" + k, v.shape, mybir.dt.from_np(v.dtype), kind="ExternalInput").ap() for k, v in arrays.items()]
    out = nc.dram_tensor("out", (B, S, HID), F32, kind="ExternalOutput").ap()
    block_kernel(nc, *args, out)
    r = run_bass_kernel_spmd(nc, [{"in_" + k: v for k, v in arrays.items()}], core_ids=[0])
    return r.results[0]["out"]
```

```python
from contextlib import ExitStack

import concourse.bass as bass
from concourse import mybir

F32 = mybir.dt.float32
F32R = mybir.dt.float32r
ALU = mybir.AluOpType
ACT = mybir.ActivationFunctionType
AX = mybir.AxisListType

B, S, HID, NH, D = 4, 1024, 256, 16, 16
P = 128
NC = S // P
KT = HID // P
TOK = B * P
HALF = 64
SUB = 32
NS = P // SUB
COL = SUB + 1
ND = D // 2 + 1
NI = D // 2
U = ND * NI
MIR = (ND - 2) * NI
PAIRS = U + MIR
V_, Q_, K_, KB_ = range(4)
NITEM = 2 * 4
SLOTS = 4
EPS = 1e-5
SCALE = 1.0 / 16.0
(LNG, LNB, BF, BI, BC, INC, BQ, BK, BV) = range(0, 18, 2)
DMA = 16
PARTS = (0, 3, 6, 8, 10)


class LayerNorm:

    def __init__(self, sb, sem, name):
        self.stats = sb(f"{name}_stats", [P, B, 6])
        self.mv = sb(f"{name}_mv", [P, B, 2])
        self.rs = sb(f"{name}_rs", [P, B])
        self.shift = sb(f"{name}_shift", [P, B])
        self.last = sb(f"{name}_last", [P, 1])
        self.settled = sem(f"{name}_settled")
        self.stat_done = sem(f"{name}_stat_done")
        self.mv_done = sem(f"{name}_mv_done")
        self.var_done = sem(f"{name}_var_done")
        self.rstd_done = sem(f"{name}_rstd_done")
        self.neg_done = sem(f"{name}_neg_done")
        self.shift_done = sem(f"{name}_shift_done")
        self.norm_done = sem(f"{name}_norm_done")


def wait(e, sem, count):
    if not isinstance(count, int) or count > 0:
        e.wait_ge(sem, count)


def block_kernel(nc, x, wqkvg, wbeta, wout, cols, rows, wx, wc, wattn, ident_d, out):
    rs_d = nc.dram_tensor("scan_in_dram", [NC, 2, 4, B, HID, HALF], F32, kind="Internal").ap()
    os_d = nc.dram_tensor("scan_out_dram", [NC, 2, B, NH, D, P], F32, kind="Internal").ap()
    gs_d = nc.dram_tensor("gate_dram", [NC, P, KT * TOK], F32, kind="Internal").ap()
    x2_d = nc.dram_tensor("x2_dram", [B, S, HID], F32, kind="Internal").ap()
    vs_d = nc.dram_tensor("values_dram", [B, S, HID], F32, kind="Internal").ap()
    ks_d = nc.dram_tensor("keys_dram", [KT, P, B, S], F32, kind="Internal").ap()
    x_m = x.rearrange("b (m p) d -> m p b d", p=P)
    x2_m = x2_d.rearrange("b (m p) d -> m p b d", p=P)
    out_m = out.rearrange("b (m p) d -> m p b d", p=P)
    vs_m = vs_d.rearrange("b (m p) d -> m p b d", p=P)
    ks_m = ks_d.rearrange("k p b (m t) -> m k p b t", t=P)
    os_m = os_d.rearrange("m a b h i t -> m a (b h) i t")
    os_f = os_d.rearrange("m a b h i t -> m a (h i) b t")

    with ExitStack() as ctx:
        stage_a = ExitStack()

        def sb(name, shape, dtype=F32):
            return ctx.enter_context(nc.sbuf_tensor(name, shape, dtype))

        def sb_a(name, shape):
            return stage_a.enter_context(nc.sbuf_tensor(name, shape, F32))

        def psum(name, shape):
            return ctx.enter_context(nc.psum_tensor(name, shape, F32))

        def sem(name):
            return ctx.enter_context(nc.semaphore(name))

        col = sb("col", [P, 18])
        hcol = sb("hcol", [P, 8])
        row = sb("row", [1, 2 * HID + P])
        w_x = sb("w_x", [P, KT, 4 * HID])
        w_c = sb("w_c", [P, KT, 4 * HID])
        w_g = sb("w_g", [P, KT, HID])
        q_bias = sb("q_bias", [P, 2 * KT])
        qk_const = sb("qk_const", [1, 1])
        y_row = sb("y_row", [1, HID])
        y_bias = sb("y_bias", [P, HID])
        ident = sb("ident", [P, P])
        eps4 = sb("eps4", [P, B])
        mhalf = sb("mhalf", [P, B])
        minus1 = sb("minus1", [P, B])
        bias0 = sb("bias0", [P, 3 * KT])
        xin = sb("xin", [P, B, HID])
        nrm = sb("nrm", [P, B, HID])
        xr = sb("xr", [P, B, HID])
        n2T = sb("n2T", [P, KT, TOK])
        gt = sb("gt", [P, 3, KT * P])
        cc = sb("cc", [P, KT, P])
        hu = sb("hu", [P, HID])
        hh = sb("hh", [P, 2, 2 * HID])
        mx = sb("mx", [P, 2, 8])
        rq = sb("rq", [P, B])
        ln_x = LayerNorm(sb, sem, "ln_x")
        ln_o = LayerNorm(sb, sem, "ln_o")
        ln_2 = LayerNorm(sb, sem, "ln_2")
        ln_3 = LayerNorm(sb, sem, "ln_3")
        c_init = sb("c_init", [P, KT])
        w_qkvg = sb_a("w_qkvg", [P, KT, 4 * HID])
        w_beta = sb_a("w_beta", [P, KT, NH])
        xnT = sb_a("xnT", [P, KT, TOK])
        qk = sb_a("qk", [P, B, 2 * HID])
        sq = sb_a("sq", [P, 2, 2 * HID])
        ss = sb_a("ss", [P, B * 2 * NH])
        rn = sb_a("rn", [P, B * 2 * NH])
        bt = sb_a("bt", [P, B * NH])
        beta = sb_a("beta", [P, B * NH])
        kb = sb_a("kb", [P, B, HID])
        stage = sb_a("stage", [P, SLOTS, TOK])
        gate = sb_a("gate", [P, KT, TOK])
        lay = sb_a("lay", [P, 2, 4, D, HALF])
        dec = sb_a("dec", [P, 2, U, COL])
        st = sb_a("st", [P, 2, PAIRS, COL])
        ob = sb_a("ob", [P, 2, D, HALF])
        w_out = sb_a("w_out", [P, KT, HID])
        w_vo = sb_a("w_vo", [P, KT, HID])
        oH = sb_a("oH", [P, 2, KT, TOK])
        ogT = sb_a("ogT", [P, KT, TOK])
        gl = sb_a("gl", [P, KT, TOK])
        n3T = sb_a("n3T", [P, KT, TOK])
        w_raw = oH[:, :, :, :].rearrange("p a b c -> p (a b c)").rearrange("p (w k n) -> p w k n", w=4, k=KT)
        stage_a.close()
        keys_lo = sb("keys_lo", [P, KT, B, S], F32R)
        vals_lo = sb("vals_lo", [P, B, NC, HID], F32R)
        xq = sb("xq", [P, KT, TOK])
        keys_hi = sb("keys_hi", [P, KT, B, S], F32R)
        vals_hi = sb("vals_hi", [P, B, NC, HID], F32R)
        prob = sb("prob", [P, S])
        probT_hi = sb("probT_hi", [P, NC, P], F32R)
        probT_lo = sb("probT_lo", [P, NC, P], F32R)
        qT_hi = sb("qT_hi", [P, KT, TOK], F32R)
        qT_lo = sb("qT_lo", [P, KT, TOK], F32R)
        xa = xin

        PB = psum("PB", [P, 2, 512])
        QB = psum("QB", [P, 2, 512])
        FB = psum("FB", [P, 2, 512])
        JB = psum("JB", [P, 2, 512])

        first_loaded = sem("first_loaded")
        w_loaded = sem("w_loaded")
        const_set = sem("const_set")
        dve_const = sem("dve_const")
        x_loaded = sem("x_loaded")
        xT_done = sem("xT_done")
        xT_copied = sem("xT_copied")
        qk_mm = sem("qk_mm")
        sq_done = sem("sq_done")
        qk_copied = sem("qk_copied")
        ss_done = sem("ss_done")
        ssmax_done = sem("ssmax_done")
        norm_sqrt = sem("norm_sqrt")
        rn_done = sem("rn_done")
        n3T_free = sem("n3T_free")
        beta_mm = sem("beta_mm")
        bt_done = sem("bt_done")
        beta_done = sem("beta_done")
        v_mm = sem("v_mm")
        g_mm = sem("g_mm")
        tg_done = sem("tg_done")
        gate_done = sem("gate_done")
        gate_spilled = sem("gate_spilled")
        qkn_done = sem("qkn_done")
        kb_done = sem("kb_done")
        turn_done = sem("turn_done")
        staged = sem("staged")
        spilled = [sem(f"spilled{i}") for i in range(SLOTS)]
        lay_loaded = [sem(f"lay_loaded{i}") for i in range(2)]
        kk_done = sem("kk_done")
        dec_done = sem("dec_done")
        inp_done = sem("inp_done")
        mirror_done = sem("mirror_done")
        scan_done = sem("scan_done")
        carried = sem("carried")
        prod_done = sem("prod_done")
        sum_done = sem("sum_done")
        sum_copied = sem("sum_copied")
        ob_spilled = [sem(f"ob_spilled{i}") for i in range(2)]
        o_loaded = sem("o_loaded")
        gl_loaded = sem("gl_loaded")
        xr_loaded = sem("xr_loaded")
        osum_done = sem("osum_done")
        oT_done = sem("oT_done")
        onT_done = sem("onT_done")
        og_done = sem("og_done")
        gated = sem("gated")
        y_mm = sem("y_mm")
        x1_done = sem("x1_done")
        n2t_done = sem("n2t_done")
        n2T_copied = sem("n2T_copied")
        cell_mm = sem("cell_mm")
        cell_act = sem("cell_act")
        cell_h = sem("cell_h")
        c_done = sem("c_done")
        h_mm = sem("h_mm")
        u_mm = sem("u_mm")
        u_copied = sem("u_copied")
        h_sum = sem("h_sum")
        folded = sem("folded")
        vals_mm = sem("vals_mm")
        vals_copied = sem("vals_copied")
        vals_biased = sem("vals_biased")
        first_bias = sem("first_bias")
        y_row_done = sem("y_row_done")
        h_act = sem("h_act")
        x2_done = sem("x2_done")
        x2_stored = sem("x2_stored")
        v_stored = sem("v_stored")
        n3t_done = sem("n3t_done")
        n3T_copied = sem("n3T_copied")
        wb_mm = sem("wb_mm")
        wb_done = sem("wb_done")
        keys_loaded = [sem(f"keys_loaded{i}") for i in range(B)]
        vals_loaded = [sem(f"vals_loaded{i}") for i in range(B)]
        xq_loaded = sem("xq_loaded")
        xa_loaded = sem("xa_loaded")
        xa_copied = sem("xa_copied")
        q_mm = sem("q_mm")
        q_copied = sem("q_copied")
        rq_mm = sem("rq_mm")
        rq_done = sem("rq_done")
        score_mm = sem("score_mm")
        max_done = sem("max_done")
        bias_step = sem("bias_step")
        bias_done = sem("bias_done")
        exp_done = sem("exp_done")
        pt_mm = sem("pt_mm")
        pt_act = sem("pt_act")
        pt_lo = sem("pt_lo")
        q_lo = sem("q_lo")
        hi_done = sem("hi_done")
        split_done = sem("split_done")
        pv_mm = sem("pv_mm")
        recip_done = sem("recip_done")
        x3_done = sem("x3_done")

        def stages(i, steady=False):
            def stage(lag):
                def call(step, *args):
                    if steady or 0 <= i - lag < NC:
                        step(i - lag, *args)
                return call
            return stage(-1), stage(0), stage(1), stage(2)

        def mlp_before(c):
            return lambda step, *args: step(NC + c - 1, *args)

        def no_mlp(step, *args):
            pass

        def rounds(e, one):
            for i in (-1, 0, 1, 2):
                one(i, *stages(i))
            with e.Fori(3, NC - 1) as i:
                one(i, *stages(i, steady=True))
            for i in (NC - 1, NC, NC + 1):
                one(i, *stages(i))

        NW = 7

        block = ctx.enter_context(nc.Block())

        @block.sync
        def _(sp):
            def by_rows(w):
                return w.rearrange("(k p) n -> p k n", p=P)

            def load_first():
                sp.dma_start(xin[:, :, :], x_m[0]).then_inc(x_loaded, DMA)
                for dst, src in ((ident[:, :], ident_d), (w_qkvg[:, :, :], by_rows(wqkvg)), (w_beta[:, :, :], by_rows(wbeta))):
                    sp.dma_start(dst, src).then_inc(first_loaded, DMA)

            def load_weights():
                for dst, src in ((col[:, :], cols), (row[:, :], rows), (w_c[:, :, :], by_rows(wc)),
                                 (w_out[:, :, :], by_rows(wout)), (w_x[:, :, :], by_rows(wx))):
                    sp.dma_start(dst, src).then_inc(w_loaded, DMA)
                for k in range(KT):
                    sp.dma_start(w_raw[:, :, k, :], wattn.rearrange("w (k p) n -> k p w n", p=P)[k]).then_inc(w_loaded, DMA)

            def after(*waits):
                waits = [(w, n if isinstance(n, int) else sp.snap(n)) for w, n in waits]
                if not all(isinstance(n, int) for _, n in waits):
                    sp.wait_ge(w_loaded, NW * DMA)
                for w, n in waits:
                    wait(sp, w, n)

            def load_x(m):
                if isinstance(m, int) and m == 0:
                    return
                after((xT_done, 2 * m))
                sp.dma_start(xin[:, :, :], x_m[m]).then_inc(x_loaded, DMA)

            def spill_gate(m):
                for ft in range(KT):
                    after((gate_done, 2 * m + ft + 1))
                    sp.dma_start(gs_d[m, :, ft * TOK:(ft + 1) * TOK], gate[:, ft, :]).then_inc(gate_spilled, DMA)

            def spill_item(m, j):
                after((staged, NITEM * m + j + 1))
                for hf in range(2):
                    dst = rs_d[m, hf, j // 2].rearrange("b f t -> f b t")[(j % 2) * P:(j % 2 + 1) * P]
                    src = stage[:, j % SLOTS, :].rearrange("p (b s t) -> p s b t", b=B, s=2)[:, hf]
                    sp.dma_start(dst, src).then_inc(spilled[j % SLOTS], DMA)

            def load_lay(m, hf):
                after(*((sp_, 4 * DMA * (m + 1)) for sp_ in spilled))
                src = rs_d[m, hf].rearrange("w b (h i) t -> (b h) w (i t)", h=NH)
                dst = lay[:, hf].rearrange("p w i t -> p w (i t)")
                n = D * HALF
                sp.dma_start(dst[64:128, :, 0:n // 2], src[:, :, n // 2:n]).then_inc(lay_loaded[hf], DMA)
                sp.dma_start(dst[0:64], src).then_inc(lay_loaded[hf], DMA)
                sp.dma_start(dst[64:128, :, n // 2:n], src[:, :, 0:n // 2]).then_inc(lay_loaded[hf], DMA)

            def spill_sums(m, hf):
                after((sum_copied, NS * m + 2 * hf + 2))
                t = slice(hf * HALF, (hf + 1) * HALF)
                sp.dma_start(os_m[m, 0][:, :, t], ob[0:64, hf]).then_inc(ob_spilled[hf], DMA)
                sp.dma_start(os_m[m, 1][:, 8:16, t], ob[64:128, hf, 0:8]).then_inc(ob_spilled[hf], DMA)
                sp.dma_start(os_m[m, 1][:, 0:8, t], ob[64:128, hf, 8:16]).then_inc(ob_spilled[hf], DMA)

            def load_o(m):
                after(*((ob_spilled[hf], 3 * DMA * (m + 1)) for hf in range(2)))
                if isinstance(m, int) and m == 0:
                    sp.wait_ge(wb_mm, 6)
                for a in (1, 0):
                    for ft in range(KT):
                        sp.dma_start(oH[:, a, ft, :].rearrange("p (b t) -> p b t", b=B),
                                     os_f[m, a][ft * P:(ft + 1) * P]).then_inc(o_loaded, DMA)

            def load_gate(m):
                after((gate_spilled, 2 * DMA * (m + 1)))
                sp.dma_start(gl[:, :, :].rearrange("p k t -> p (k t)"), gs_d[m]).then_inc(gl_loaded, DMA)

            def load_xa(m):
                after((x2_stored, DMA * m))
                sp.dma_start(xr[:, :, :], x_m[m]).then_inc(xr_loaded, DMA)

            def store_xa(m):
                store_x(m, x2_m[m])

            def store_x(M, dst):
                after((x2_done, 2 * (M + 1)))
                sp.dma_start(dst, xr[:, :, :]).then_inc(x2_stored, DMA)

            def store_v(m):
                after((vals_biased, m + 1))
                sp.dma_start(vs_m[m], hh[:, :, :].rearrange("p j (b d) -> p (j b) d", b=2)).then_inc(v_stored, DMA)

            def store_k(m):
                for ft in range(KT):
                    after((n3T_copied, 2 * m + ft + 1))
                    sp.dma_start(ks_m[m, ft], n3T[:, ft, :].rearrange("p (b t) -> p b t", b=B)).then_inc(n3T_free, DMA)

            def load_keys(c0, c1):
                sp.wait_ge(n3T_free, 2 * DMA * (c1 + 1))
                sp.wait_ge(v_stored, DMA * c1)
                sp.wait_ge(prod_done, 2 * NS * NC)
                sp.wait_ge(sum_done, NS * NC)
                for b in range(B):
                    for k in range(KT):
                        sp.dma_start(keys_lo[:, k, b, c0 * P:c1 * P].bitcast(F32), ks_d[k, :, b, c0 * P:c1 * P]).then_inc(keys_loaded[b], DMA)
                    sp.dma_start(vals_lo[:, b, c0:c1].bitcast(F32), vs_d[b, c0 * P:c1 * P].rearrange("(j p) d -> p j d", p=P)).then_inc(vals_loaded[b], DMA)

            def load_queries(c):
                after((rq_mm, c))
                for k in range(KT):
                    sp.dma_start(xq[:, k, :].rearrange("p (b t) -> p b t", b=B), ks_m[c, k]).then_inc(xq_loaded, DMA)

            def one(i, pre, main, post, keys_):
                main(spill_item, 5)
                main(spill_item, 6)
                main(spill_item, 7)
                pre(load_x)
                post(spill_sums, 0)
                main(load_lay, 0)
                keys_(store_xa)
                post(spill_sums, 1)
                keys_(store_k)
                post(load_gate)
                post(load_o)
                main(load_lay, 1)
                pre(spill_item, 0)
                post(load_xa)
                pre(spill_item, 1)
                pre(spill_gate)
                pre(spill_item, 2)
                pre(spill_item, 3)
                keys_(store_v)
                pre(spill_item, 4)
                if isinstance(i, int) and i == NC:
                    load_keys(0, NC - 2)
                    load_queries(0)

            def load_x2(c):
                first = isinstance(c, int) and c == 0
                after((ln_2.norm_done, 0 if first else 4 * (NC + c)), (xa_copied, c))
                sp.dma_start(xa[:, :, :], x2_m[c]).then_inc(xa_loaded, DMA)

            def store_out(c):
                store_x(NC + c, out_m[c])

            load_first()
            load_weights()
            rounds(sp, one)
            load_keys(NC - 2, NC)
            load_x2(0)
            load_queries(1)
            with sp.Fori(1, NC - 1) as c:
                load_x2(c)
                load_queries(c + 1)
                store_out(c - 1)
            load_x2(NC - 1)
            store_out(NC - 2)
            store_out(NC - 1)
            sp.wait_ge(x2_stored, 2 * DMA * NC)

        @block.gpsimd
        def _(gp):
            def consts():
                gp.memset(eps4[:, :], EPS).then_inc(const_set, 1)
                gp.memset(mhalf[:, :], -0.5).then_inc(const_set, 1)
                gp.memset(minus1[:, :], -1.0).then_inc(const_set, 1)
                gp.memset(dec[:, :, :, 0:1], 0.0).then_inc(const_set, 1)
                gp.memset(st[:, 0, :, 0:1], 0.0).then_inc(const_set, 1)
                gp.memset(ob[:, :, D - 1, :], 0.0).then_inc(const_set, 1)
                gp.memset(n3T[:, :, 0:1], 0.0).then_inc(n3T_free, 2 * DMA)
                gp.wait_ge(const_set, 6)

            def rstd(L, M):
                gp.wait_ge(L.mv_done, 4 * (M + 1))
                gp.tensor_tensor(L.rs[:, :], L.mv[:, :, 1], eps4[:, :], ALU.add).then_inc(L.var_done, 1)
                gp.tensor_tensor(L.shift[:, :], L.mv[:, :, 0], minus1[:, :], ALU.mult).then_inc(L.neg_done, 1)
                gp.wait_ge(L.var_done, M + 1)
                gp.tensor_tensor(L.rs[:, :], L.rs[:, :], mhalf[:, :], ALU.pow).then_inc(L.rstd_done, 1)
                gp.wait_ge(L.neg_done, M + 1)
                gp.wait_ge(L.rstd_done, M + 1)
                gp.tensor_tensor(L.shift[:, :], L.shift[:, :], L.rs[:, :], ALU.mult).then_inc(L.shift_done, 1)

            def kk(m, s):
                hf, par, t = s // 2, s % 2, (s % 2) * SUB
                gp.wait_ge(lay_loaded[hf], 3 * DMA * (m + 1))
                wait(gp, scan_done, 2 * NS * m + 2 * s - 2)
                a, b_ = pair_views(lay, hf, K_, t), shifted_views(lay, hf, KB_, t)
                gp.tensor_tensor(pairs_out(dec, par, 0, ND), a(0, ND), b_(0, ND), ALU.mult).then_inc(kk_done, 1)

            def fold(m, s):
                n, par = NS * m + s, s % 2
                gp.wait_ge(prod_done, 2 * n + 1)
                near, far = pairs_out(st, par, NI, 4), pairs_out(st, par, 5 * NI, 4)
                gp.tensor_tensor(near, near, far, ALU.add).then_inc(folded, 1)
                gp.wait_ge(folded, 2 * n + 1)
                near, far = pairs_out(st, par, NI, 2), pairs_out(st, par, 3 * NI, 2)
                gp.tensor_tensor(near, near, far, ALU.add).then_inc(folded, 1)

            def bias_vals(m):
                gp.wait_ge(vals_copied, 2 * (m + 1))
                if isinstance(m, int) and m == 0:
                    gp.wait_ge(wb_done, 5)
                v = hh[:, :, :].rearrange("p j (b d) -> p (j b) d", b=2)
                gp.tensor_tensor(v, v, y_bias[:, :].unsqueeze(1).broadcast_to([P, B, HID]),
                                 ALU.add).then_inc(vals_biased, 1)

            def scale_kb(m):
                gp.wait_ge(qkn_done, m + 1)
                gp.wait_ge(beta_done, m + 1)
                wait(gp, turn_done, 6 * m)
                gp.tensor_tensor(kb[:, :, :].rearrange("p b (h i) -> p b h i", i=D),
                                 qk[:, :, HID:2 * HID].rearrange("p b (h i) -> p b h i", i=D),
                                 beta[:, :].rearrange("p (b h) -> p b h", b=B).unsqueeze(3).broadcast_to([P, B, NH, D]),
                                 ALU.mult).then_inc(kb_done, 1)

            def mirror_inputs(m, s):
                hf, t = s // 2, (s % 2) * SUB
                gp.wait_ge(lay_loaded[hf], 3 * DMA * (m + 1))
                wait(gp, sum_done, NS * m + s - 1)
                v_sh, b_ = shifted_views(lay, hf, V_, t), pair_views(lay, hf, KB_, t)
                gp.tensor_tensor(pairs_out(st, s % 2, U, ND - 2), v_sh(1, ND - 1), b_(1, ND - 1),
                                 ALU.mult).then_inc(mirror_done, 1)

            def add_halves(m):
                gp.wait_ge(o_loaded, 4 * DMA * (m + 1))
                gp.tensor_tensor(oH[:, 0], oH[:, 0], oH[:, 1], ALU.add).then_inc(osum_done, 1)

            def gating(m):
                gp.wait_ge(gl_loaded, DMA * (m + 1))
                for ft in range(KT):
                    gp.wait_ge(og_done, 2 * m + ft + 1)
                    gp.tensor_tensor(ogT[:, ft], ogT[:, ft], gl[:, ft], ALU.mult).then_inc(gated, 1)

            def add_mlp(M):
                for j in range(2):
                    gp.wait_ge(h_act, 2 * M + j + 1)
                    v = xr[:, 2 * j:2 * j + 2, :].rearrange("p b d -> p (b d)")
                    gp.tensor_tensor(v, v, hh[:, j, :], ALU.add).then_inc(x2_done, 1)

            def norm_x(m):
                rstd(ln_x, m)

            def norm_o(m):
                rstd(ln_o, m)

            def norm_2(M):
                rstd(ln_2, M)

            def norm_3(m):
                rstd(ln_3, m)

            def chunk_b(c):
                rstd(ln_2, NC + c)
                gp.wait_ge(xa_copied, c + 1)
                add_mlp(NC + c)

            def one(i, pre, main, post, keys_):
                post(mirror_inputs, 3)
                post(fold, 2)
                pre(norm_x)
                main(kk, 0)
                post(fold, 3)
                keys_(add_mlp)
                keys_(norm_3)
                main(mirror_inputs, 0)
                main(kk, 1)
                keys_(bias_vals)
                post(add_halves)
                main(mirror_inputs, 1)
                post(norm_o)
                main(fold, 0)
                post(gating)
                main(kk, 2)
                pre(scale_kb)
                post(norm_2)
                main(mirror_inputs, 2)
                main(fold, 1)
                main(kk, 3)

            consts()
            rounds(gp, one)
            chunk_b(0)
            with gp.Fori(1, NC) as c:
                chunk_b(c)

        @block.scalar
        def _(act):
            def copy(dst, src, scale=1.0, bias=0.0):
                return act.activation(dst, src, ACT.Identity, scale=scale, bias=bias)

            def norm_apply(L, M, src, dst):
                act.wait_ge(L.shift_done, M + 1)
                for b in range(B):
                    copy(dst(b), src(b), scale=L.rs[:, b:b + 1], bias=L.shift[:, b:b + 1]).then_inc(L.norm_done, 1)

            def tile(t):
                return lambda b: t[:, b, :]

            def o_tile(b):
                return QB[:, b // 2, (b % 2) * HID:(b % 2 + 1) * HID]

            def x_norm(m):
                norm_apply(ln_x, m, tile(xin), tile(xin))

            def o_norm(m):
                wait(act, n3t_done, 2 * m)
                norm_apply(ln_o, m, o_tile, tile(nrm))

            def n2_norm(m):
                act.wait_ge(onT_done, 2 * (m + 1))
                norm_apply(ln_2, m, tile(xr), tile(nrm))

            def n3_norm(m):
                act.wait_ge(n2t_done, 2 * (m + 1))
                norm_apply(ln_3, m, tile(xr), tile(nrm))

            def xa_norm(M):
                act.wait_ge(n2t_done, 2 * M)
                if isinstance(M, int) and M == NC:
                    act.wait_ge(n3t_done, 2 * NC)
                norm_apply(ln_2, M, tile(xa), tile(nrm))

            def copy_xT(m):
                for ft in range(KT):
                    act.wait_ge(xT_done, 2 * m + ft + 1)
                    wait(act, g_mm, 2 * m)
                    copy(xnT[:, ft, :], PB[:, ft, :]).then_inc(xT_copied, 1)

            def copy_qk(m, b):
                act.wait_ge(qk_mm, 4 * m + b + 1)
                wait(act, ss_done, 4 * m + b - 1)
                act.activation(sq[:, b % 2, :], PB[:, b % 2, :], ACT.Square).then_inc(sq_done, 1)
                wait(act, turn_done, 6 * m)
                copy(qk[:, b, :], PB[:, b % 2, :]).then_inc(qk_copied, 1)

            def beta_tanh(m):
                act.wait_ge(beta_mm, m + 1)
                wait(act, beta_done, m)
                act.activation(bt[:, :], PB[:, 0, 0:B * NH], ACT.Tanh, scale=0.5).then_inc(bt_done, 1)

            def copy_v(m, ft):
                act.wait_ge(v_mm, 2 * m + ft + 1)
                to_stage(m, ft, PB[:, 1 - ft, :])

            def gate_tanh(m, ft):
                act.wait_ge(g_mm, 2 * m + ft + 1)
                wait(act, gate_spilled, 2 * DMA * m)
                act.activation(gate[:, ft, :], PB[:, 1 - ft, :], ACT.Tanh, scale=0.5).then_inc(tg_done, 1)

            def head_norms(m):
                act.wait_ge(ssmax_done, m + 1)
                act.activation(rn[:, :], rn[:, :], ACT.Sqrt).then_inc(norm_sqrt, 1)

            def copy_turned(m, j):
                act.wait_ge(turn_done, 6 * m + j + 1)
                to_stage(m, 2 + j, PB[:, (j + 1) % 2, :])

            def to_stage(m, j, src):
                wait(act, spilled[j % SLOTS], 4 * DMA * m + 2 * DMA * (j // SLOTS))
                copy(stage[:, j % SLOTS, :], src).then_inc(staged, 1)

            def decay(m, s):
                act.wait_ge(kk_done, NS * m + s + 1)
                v = dec[:, s % 2, :, 1:COL]
                copy(v, v, scale=-1.0, bias=1.0).then_inc(dec_done, 1)

            def sums(m, s):
                act.wait_ge(sum_done, NS * m + s + 1)
                hf, t = s // 2, (s % 2) * SUB
                wait(act, ob_spilled[hf], 3 * DMA * m)
                copy(ob[:, hf, 0:D - 1, t:t + SUB],
                     JB[:, s % 2, 0:(D - 1) * SUB].rearrange("p (i t) -> p i t", t=SUB)).then_inc(sum_copied, 1)

            def scale_o(m):
                for ft in range(KT):
                    act.wait_ge(onT_done, 2 * m + ft + 1)
                    wait(act, y_mm, 2 * m)
                    copy(ogT[:, ft, :], QB[:, ft, :], scale=hcol[:, ft:ft + 1],
                         bias=hcol[:, 2 + ft:3 + ft]).then_inc(og_done, 1)

            def copy_n2T(M):
                for ft in range(KT):
                    act.wait_ge(n2t_done, 2 * M + ft + 1)
                    wait(act, h_mm, 2 * M)
                    copy(n2T[:, ft, :], QB[:, ft, :]).then_inc(n2T_copied, 1)

            def round_keys(b, c0, c1):
                act.wait_ge(keys_loaded[b], 2 * DMA if c0 == 0 else 4 * DMA)
                t = slice(c0 * P, c1 * P)
                copy(keys_hi[:, :, b, t], keys_lo[:, :, b, t].bitcast(F32)).then_inc(hi_done, 1)
                act.wait_ge(vals_loaded[b], DMA if c0 == 0 else 2 * DMA)
                copy(vals_hi[:, b, c0:c1], vals_lo[:, b, c0:c1].bitcast(F32)).then_inc(hi_done, 1)

            def cell(M, b):
                wait(act, c_done, 4 * M + b)
                if b == 0 and isinstance(M, int) and M == 0:
                    act.wait_ge(first_bias, 2)
                for g in range(3):
                    if g != 1:
                        act.wait_ge(cell_mm, 8 * M + 2 * b + (g // 2) + 1)
                    for mt in range(KT):
                        n = g * KT + mt
                        if b == 0:
                            bias = bias0[:, n:n + 1]
                        else:
                            bias = hcol[:, 4 + n:5 + n] if g < 2 else col[:, BC + mt:BC + mt + 1]
                        act.activation(gt[:, g, mt * P:(mt + 1) * P], FB[:, n // 4, (n % 4) * P:(n % 4 + 1) * P],
                                       ACT.Tanh, scale=0.5 if g < 2 else 1.0, bias=bias).then_inc(cell_act, 1)
                if isinstance(M, int) and M == NC - 1:
                    round_keys(b, 0, NC - 2)

            def copy_u(M):
                act.wait_ge(u_mm, M + 1)
                wait(act, h_sum, 2 * M)
                copy(hu[:, :], FB[:, 1, HID:2 * HID]).then_inc(u_copied, 1)

            def h_tanh(M):
                for j in range(2):
                    act.wait_ge(h_sum, 2 * M + j + 1)
                    act.activation(hh[:, j, :], hh[:, j, :], ACT.Tanh).then_inc(h_act, 1)

            def keys_out(m):
                for ft in range(KT):
                    act.wait_ge(n3t_done, 2 * m + ft + 1)
                    act.wait_ge(n3T_free, 2 * DMA * (m + 1))
                    copy(n3T[:, ft, :], QB[:, ft, :]).then_inc(n3T_copied, 1)

            def copy_vals(m):
                for j in range(2):
                    act.wait_ge(vals_mm, 2 * m + j + 1)
                    copy(hh[:, j, :], QB[:, j, :]).then_inc(vals_copied, 1)

            def attn_weights():
                act.wait_ge(dve_const, 4)
                act.wait_ge(wb_mm, 6)
                act.wait_ge(first_bias, 1)
                copy(w_g[:, :, :], JB[:, 0, :].rearrange("p (k n) -> p k n", k=KT)).then_inc(wb_done, 1)
                copy(w_vo[:, :, :], JB[:, 1, :].rearrange("p (k n) -> p k n", k=KT)).then_inc(wb_done, 1)
                copy(q_bias[:, :], QB[:, 0, 0:2 * KT]).then_inc(wb_done, 1)
                copy(qk_const[:, :], QB[0:1, 0, 16:17]).then_inc(wb_done, 1)
                act.wait_ge(wb_mm, 7)
                copy(y_bias[:, :], QB[:, 1, HID:2 * HID]).then_inc(wb_done, 1)
                act.wait_ge(wb_done, 5)

            def one(i, pre, main, post, keys_):
                post(decay, 3)
                keys_(cell, 2)
                pre(x_norm)
                keys_(cell, 3)
                main(decay, 0)
                keys_(copy_u)
                keys_(h_tanh)
                post(sums, 2)
                pre(copy_xT)
                post(sums, 3)
                keys_(n3_norm)
                pre(copy_qk, 0)
                keys_(keys_out)
                keys_(copy_vals)
                pre(copy_qk, 1)
                main(decay, 1)
                pre(copy_qk, 2)
                pre(copy_qk, 3)
                pre(beta_tanh)
                pre(head_norms)
                pre(copy_v, 0)
                pre(copy_v, 1)
                post(o_norm)
                post(scale_o)
                pre(gate_tanh, 0)
                pre(gate_tanh, 1)
                main(decay, 2)
                pre(copy_turned, 0)
                pre(copy_turned, 1)
                pre(copy_turned, 2)
                pre(copy_turned, 3)
                post(n2_norm)
                post(copy_n2T)
                main(sums, 0)
                pre(copy_turned, 4)
                pre(copy_turned, 5)
                post(cell, 0)
                main(sums, 1)
                post(cell, 1)
                if isinstance(i, int) and i == -1:
                    attn_weights()

            def softmax(c, b):
                n = 4 * c + b
                act.wait_ge(bias_done, n + 1)
                wait(act, pt_mm, 2 * n)
                act.activation(prob[:, :], JB[:, :, :].rearrange("p a n -> p (a n)"), ACT.Exp, scale=SCALE,
                               bias=mx[:, b % 2, 2:3], accum_out=mx[:, b % 2, 3:4]).then_inc(exp_done, 1)

            def copy_prob(c, b):
                n = 4 * c + b
                for j in range(2):
                    act.wait_ge(pt_mm, 2 * n + j + 1)
                    wait(act, pv_mm, n)
                    copy(probT_hi[:, 4 * j:4 * j + 4, :],
                         PB[:, j, :].rearrange("p (j q) -> p j q", j=4)).then_inc(pt_act, 1)

            def copy_q(c):
                for et in range(KT):
                    act.wait_ge(q_mm, 2 * c + et + 1)
                    wait(act, score_mm, 4 * c)
                    copy(qT_hi[:, et, :], PB[:, et, :], bias=q_bias[:, et:et + 1]).then_inc(q_copied, 1)

            def copy_xa(M):
                act.wait_ge(x3_done, 4 * (M - NC + 1))
                act.wait_ge(x2_stored, DMA * M)
                copy(xr[:, :, :], xa[:, :, :]).then_inc(xa_copied, 1)

            def chunk_b(c, mlp_of, last=False):
                copy_prob(c, 0)
                mlp_of(xa_norm)
                softmax(c, 1)
                mlp_of(copy_xa)
                copy_prob(c, 1)
                mlp_of(copy_n2T)
                softmax(c, 2)
                copy_prob(c, 2)
                mlp_of(cell, 0)
                mlp_of(cell, 1)
                softmax(c, 3)
                mlp_of(cell, 2)
                copy_prob(c, 3)
                if not last:
                    copy_q(c + 1)
                mlp_of(cell, 3)
                if not last:
                    softmax(c + 1, 0)
                mlp_of(copy_u)
                mlp_of(h_tanh)

            rounds(act, one)
            copy_q(0)
            for b in range(B):
                round_keys(b, NC - 2, NC)
                if b == 0:
                    softmax(0, 0)
            chunk_b(0, no_mlp)
            with act.Fori(1, NC - 1) as c:
                chunk_b(c, mlp_before(c))
            chunk_b(NC - 1, mlp_before(NC - 1), last=True)
            xa_norm(2 * NC - 1)
            copy_xa(2 * NC - 1)
            copy_n2T(2 * NC - 1)
            for b in range(B):
                cell(2 * NC - 1, b)
            copy_u(2 * NC - 1)
            h_tanh(2 * NC - 1)

        @block.tensor
        def _(pe):
            def mm(dst, lhsT, rhs, start, stop):
                return pe.matmul(dst, lhsT, rhs, start=start, stop=stop, skip_group_check=True)

            def turn_tiles(bank, src, ft):
                for b in range(B):
                    i = pe.transpose(bank[:, b * P:(b + 1) * P], src[:, b, ft * P:(ft + 1) * P], ident[:, :])
                return i

            def turn_x(m):
                pe.wait_ge(ln_x.norm_done, 4 * (m + 1))
                for ft in range(KT):
                    wait(pe, staged, NITEM * m - ft)
                    turn_tiles(PB[:, ft, :], xin, ft).then_inc(xT_done, 1)

            def project_qk(m, b):
                pe.wait_ge(xT_copied, 2 * (m + 1))
                if b >= 2:
                    pe.wait_ge(qk_copied, 4 * m + b - 1)
                for k in range(KT):
                    i = mm(PB[:, b % 2, :], xnT[:, k, b * P:(b + 1) * P], w_qkvg[:, k, 0:2 * HID],
                           k == 0, k == KT - 1)
                i.then_inc(qk_mm, 1)

            def project_beta(m):
                pe.wait_ge(qk_copied, 4 * m + 3)
                for b in range(B):
                    for k in range(KT):
                        i = mm(PB[:, 0, b * NH:(b + 1) * NH], xnT[:, k, b * P:(b + 1) * P], w_beta[:, k, :],
                               b == 0 and k == 0, k == KT - 1)
                i.then_inc(beta_mm, 1)

            def project_t(m, n, ft, done):
                if n == 2 and ft == 0:
                    pe.wait_ge(qk_copied, 4 * m + 4)
                elif n == 2:
                    pe.wait_ge(bt_done, m + 1)
                else:
                    pe.wait_ge(staged, NITEM * m + ft + 1)
                for k in range(KT):
                    w = w_qkvg[:, k, n * HID + ft * P:n * HID + (ft + 1) * P]
                    i = mm(PB[:, 1 - ft, :], w, xnT[:, k, :], k == 0, k == KT - 1)
                i.then_inc(done, 1)

            def project_v(m, ft):
                project_t(m, 2, ft, v_mm)

            def project_g(m, ft):
                project_t(m, 3, ft, g_mm)

            def turn_qk(m, j):
                if j < 2:
                    pe.wait_ge(qkn_done, m + 1)
                    pe.wait_ge(gate_done, 2 * m + j + 1)
                else:
                    pe.wait_ge(staged, NITEM * m + j + 1)
                if j == 4:
                    pe.wait_ge(kb_done, m + 1)
                src = (qk[:, :, 0:HID], qk[:, :, HID:2 * HID], kb[:, :, :])[j // 2]
                turn_tiles(PB[:, (j + 1) % 2, :], src, j % 2).then_inc(turn_done, 1)

            def attn_weights():
                pe.wait_ge(w_loaded, NW * DMA)
                pe.wait_ge(dve_const, 4)
                for d in range(KT):
                    for k in range(KT):
                        i = mm(JB[:, 0, d * HID:(d + 1) * HID], w_raw[:, 0, k, d * P:(d + 1) * P], w_raw[:, 1, k, :],
                               d == 0 and k == 0, k == KT - 1)
                i.then_inc(wb_mm, 1)
                for d in range(KT):
                    for k in range(KT):
                        i = mm(JB[:, 1, d * HID:(d + 1) * HID], w_raw[:, 2, k, d * P:(d + 1) * P], w_raw[:, 3, k, :],
                               d == 0 and k == 0, k == KT - 1)
                i.then_inc(wb_mm, 1)
                for w, bias, at in ((1, BQ, 0), (0, BK, 2)):
                    for d in range(KT):
                        for k in range(KT):
                            i = mm(QB[:, 0, at + d:at + d + 1], w_raw[:, w, k, d * P:(d + 1) * P],
                                   col[:, bias + k:bias + k + 1], at + d + k == 0, k == KT - 1)
                i.then_inc(wb_mm, 1)
                for k in range(KT):
                    i = mm(QB[0:1, 0, 16:17], col[:, BQ + k:BQ + k + 1], col[:, BK + k:BK + k + 1], False, k == KT - 1)
                i.then_inc(wb_mm, 1)
                for k in range(KT):
                    i = mm(QB[0:1, 1, 0:HID], col[:, BV + k:BV + k + 1], w_raw[:, 3, k, :], k == 0, k == KT - 1)
                i.then_inc(wb_mm, 1)
                for n in range(3 * KT):
                    for k in range(KT):
                        i = mm(QB[:, 0, 32 + n:33 + n], w_c[:, k, n * P:(n + 1) * P], c_init[:, k:k + 1],
                               False, k == KT - 1)
                i.then_inc(wb_mm, 1)
                pe.wait_ge(y_row_done, 1)
                mm(QB[:, 1, HID:2 * HID], row[:, 2 * HID:2 * HID + P], y_row[:, :], True, True).then_inc(wb_mm, 1)

            def sum_j(m, s, part):
                if part == 0:
                    pe.wait_ge(prod_done, 2 * NS * m + 2 * s + 2)
                    wait(pe, sum_copied, NS * m + s - 1)
                    if isinstance(m, int) and m == 0 and s < 2:
                        pe.wait_ge(wb_done, 5)
                if part == 3:
                    pe.wait_ge(folded, 2 * (NS * m + s + 1))
                par = s % 2
                order = [(0, 0)] + [(1, d) for d in range(ND - 2, 0, -1)] + [(0, 1), (0, 2)]
                for n in range(PARTS[part], PARTS[part + 1]):
                    mirror, d = order[n]
                    at = U + (d - 1) * NI if mirror else d * NI
                    lo = d if mirror else 0
                    i = mm(JB[:, par, lo * SUB:(lo + NI) * SUB], ident[:, :], st[:, par, at:at + NI, 1:COL],
                           n == 0, n == len(order) - 1)
                if part == 3:
                    i.then_inc(sum_done, 1)

            def turn_o(m):
                pe.wait_ge(osum_done, m + 1)
                if isinstance(m, int) and m == 0:
                    pe.wait_ge(wb_done, 5)
                    pe.wait_ge(first_bias, 1)
                for j in range(2):
                    wait(pe, vals_copied, 2 * m)
                    for b in (2 * j, 2 * j + 1):
                        for ft in range(KT):
                            i = pe.transpose(QB[:, j, (b % 2) * HID + ft * P:(b % 2) * HID + (ft + 1) * P],
                                             oH[:, 0, ft, b * P:(b + 1) * P], ident[:, :])
                    i.then_inc(oT_done, 1)

            def turn_on(m):
                pe.wait_ge(ln_o.norm_done, 4 * (m + 1))
                for ft in range(KT):
                    turn_tiles(QB[:, ft, :], nrm, ft).then_inc(onT_done, 1)

            def project_o(m):
                pe.wait_ge(gated, 2 * (m + 1))
                for j in range(2):
                    for b in (2 * j, 2 * j + 1):
                        for k in range(KT):
                            i = mm(QB[:, j, (b % 2) * HID:(b % 2 + 1) * HID], ogT[:, k, b * P:(b + 1) * P],
                                   w_out[:, k, :], b % 2 == 0 and k == 0, k == KT - 1)
                    i.then_inc(y_mm, 1)

            def turn_n2(M):
                pe.wait_ge(ln_2.norm_done, 4 * (M + 1))
                for ft in range(KT):
                    turn_tiles(QB[:, ft, :], nrm, ft).then_inc(n2t_done, 1)

            def cell_x(M, b):
                pe.wait_ge(n2T_copied, 2 * (M + 1))
                wait(pe, cell_act, 24 * M + 6 * b)
                if b == 0:
                    wait(pe, u_copied, M)
                for n in range(3 * KT):
                    for k in range(KT):
                        i = mm(FB[:, n // 4, (n % 4) * P:(n % 4 + 1) * P], w_x[:, k, n * P:(n + 1) * P],
                               n2T[:, k, b * P:(b + 1) * P], n % 4 == 0 and k == 0, b == 0 and k == KT - 1)
                    if b == 0 and n in (3, 5):
                        i.then_inc(cell_mm, 1)

            def cell_c(M, b):
                pe.wait_ge(c_done, 4 * M + b)
                for n in range(3 * KT):
                    for k in range(KT):
                        i = mm(FB[:, n // 4, (n % 4) * P:(n % 4 + 1) * P], w_c[:, k, n * P:(n + 1) * P],
                               cc[:, k, :], False, k == KT - 1)
                    if n in (3, 5):
                        i.then_inc(cell_mm, 1)

            def hidden_x(M, j):
                pe.wait_ge(n2T_copied, 2 * (M + 1))
                for b in (2 * j, 2 * j + 1):
                    for k in range(KT):
                        i = mm(QB[:, j, (b % 2) * HID:(b % 2 + 1) * HID], n2T[:, k, b * P:(b + 1) * P],
                               w_x[:, k, 3 * HID:4 * HID], b % 2 == 0 and k == 0, k == KT - 1)
                i.then_inc(h_mm, 1)

            def hidden_c(M):
                pe.wait_ge(c_done, 4 * (M + 1))
                for k in range(KT):
                    mm(FB[:, 1, HID:2 * HID], cc[:, k, :], w_c[:, k, 3 * HID:4 * HID], k == 0, False)
                mm(FB[:, 1, HID:2 * HID], row[:, 2 * HID:2 * HID + P], row[:, 0:HID], False, True).then_inc(u_mm, 1)

            def keys_out(m):
                pe.wait_ge(ln_3.norm_done, 4 * (m + 1))
                pe.wait_ge(h_sum, 2 * (m + 1))
                for ft in range(KT):
                    turn_tiles(QB[:, ft, :], nrm, ft).then_inc(n3t_done, 1)

            def project_vals(m):
                pe.wait_ge(n3T_copied, 2 * (m + 1))
                for j in range(2):
                    for b in (2 * j, 2 * j + 1):
                        for k in range(KT):
                            i = mm(QB[:, j, (b % 2) * HID:(b % 2 + 1) * HID], n3T[:, k, b * P:(b + 1) * P],
                                   w_vo[:, k, :], b % 2 == 0 and k == 0, k == KT - 1)
                    i.then_inc(vals_mm, 1)

            def one(i, pre, main, post, keys_):
                keys_(hidden_x, 1)
                keys_(hidden_c)
                post(sum_j, 2, 2)
                post(sum_j, 2, 3)
                pre(turn_x)
                post(sum_j, 3, 0)
                post(sum_j, 3, 1)
                post(sum_j, 3, 2)
                post(sum_j, 3, 3)
                pre(project_qk, 0)
                keys_(keys_out)
                keys_(project_vals)
                pre(project_qk, 1)
                pre(project_qk, 2)
                pre(project_qk, 3)
                pre(project_beta)
                post(turn_o)
                pre(project_v, 0)
                pre(project_v, 1)
                main(sum_j, 0, 0)
                pre(project_g, 0)
                post(turn_on)
                pre(project_g, 1)
                main(sum_j, 0, 1)
                post(project_o)
                main(sum_j, 0, 2)
                main(sum_j, 0, 3)
                pre(turn_qk, 0)
                pre(turn_qk, 1)
                pre(turn_qk, 2)
                pre(turn_qk, 3)
                main(sum_j, 1, 0)
                pre(turn_qk, 4)
                pre(turn_qk, 5)
                post(turn_n2)
                main(sum_j, 1, 1)
                main(sum_j, 1, 2)
                post(cell_x, 0)
                main(sum_j, 1, 3)
                post(cell_x, 1)
                post(cell_c, 1)
                main(sum_j, 2, 0)
                post(cell_x, 2)
                post(cell_c, 2)
                main(sum_j, 2, 1)
                post(cell_x, 3)
                post(cell_c, 3)
                post(hidden_x, 0)
                if isinstance(i, int) and i == -1:
                    attn_weights()

            def score(c, b):
                n = 4 * c + b
                wait(pe, exp_done, n)
                if isinstance(c, int) and c == 0:
                    pe.wait_ge(split_done, 2 * B + 2 * b + 1)
                if b == 0:
                    pe.wait_ge(q_lo, 2 * (c + 1))
                for j in range(2):
                    for n_, (q_, keys_) in enumerate(((qT_hi, keys_hi), (qT_lo, keys_hi), (qT_hi, keys_lo))):
                        for k in range(KT):
                            i = mm(JB[:, j, :], q_[:, k, b * P:(b + 1) * P], keys_[:, k, b, j * 512:(j + 1) * 512],
                                   n_ == 0 and k == 0, n_ == 2 and k == KT - 1)
                i.then_inc(score_mm, 1)

            def turn_prob(c, b):
                n = 4 * c + b
                pe.wait_ge(exp_done, n + 1)
                for j in range(2):
                    wait(pe, pt_lo, 2 * n + j - 1)
                    if b == 0:
                        pe.wait_ge(q_lo, 2 * (c + 1))
                        pe.wait_ge(rq_done, c + 1)
                    for t in range(4):
                        i = pe.transpose(PB[:, j, t * P:(t + 1) * P], prob[:, (4 * j + t) * P:(4 * j + t + 1) * P],
                                         ident[:, :])
                    i.then_inc(pt_mm, 1)

            def attend(c, b):
                n = 4 * c + b
                pe.wait_ge(pt_lo, 2 * n + 2)
                if isinstance(c, int) and c == 0:
                    pe.wait_ge(split_done, 2 * B + 2 * b + 2)
                wait(pe, x3_done, n - 1)
                if not (isinstance(c, int) and c == 0):
                    pe.wait_ge(h_sum if b < 2 else n2T_copied, 2 * (NC + c) - 3 + b)
                for t in range(NC):
                    for n_, (p_, vals_) in enumerate(((probT_hi, vals_hi), (probT_lo, vals_hi), (probT_hi, vals_lo))):
                        i = mm(QB[:, b % 2, 0:HID], p_[:, t, :], vals_[:, b, t, :], t + n_ == 0, t + n_ == NC + 1)
                i.then_inc(pv_mm, 1)

            def queries(c):
                pe.wait_ge(xq_loaded, 2 * DMA * (c + 1))
                wait(pe, pt_lo, 8 * c)
                for et in range(KT):
                    for k in range(KT):
                        i = mm(PB[:, et, :], w_g[:, k, et * P:(et + 1) * P], xq[:, k, :], k == 0, k == KT - 1)
                    i.then_inc(q_mm, 1)
                pe.wait_ge(q_lo, 2 * c + 1)
                for b in range(B):
                    for k in range(KT):
                        mm(PB[:, 0, b:b + 1], xq[:, k, b * P:(b + 1) * P], q_bias[:, 2 + k:3 + k], b == 0 and k == 0, False)
                    i = mm(PB[:, 0, b:b + 1], row[:, 2 * HID:2 * HID + P], qk_const[:, :], False, True)
                i.then_inc(rq_mm, 1)

            def free_banks(M):
                pe.wait_ge(x3_done, 4 * (M - NC) + 6)

            def free_bank(M, j):
                pe.wait_ge(x3_done, 4 * (M - NC) + 7 + j)

            def chunk_b(c, mlp_of, last=False):
                turn_prob(c, 0)
                score(c, 1)
                attend(c, 0)
                turn_prob(c, 1)
                score(c, 2)
                attend(c, 1)
                mlp_of(free_banks)
                mlp_of(turn_n2)
                mlp_of(cell_x, 0)
                turn_prob(c, 2)
                score(c, 3)
                mlp_of(cell_x, 1)
                mlp_of(cell_c, 1)
                attend(c, 2)
                mlp_of(cell_x, 2)
                mlp_of(cell_c, 2)
                turn_prob(c, 3)
                mlp_of(cell_x, 3)
                if not last:
                    queries(c + 1)
                mlp_of(cell_c, 3)
                if not last:
                    score(c + 1, 0)
                attend(c, 3)
                mlp_of(free_bank, 0)
                mlp_of(hidden_x, 0)
                mlp_of(free_bank, 1)
                mlp_of(hidden_x, 1)
                mlp_of(hidden_c)

            pe.wait_ge(first_loaded, 3 * DMA)
            rounds(pe, one)
            pe.wait_ge(staged, NITEM * NC)
            pe.wait_ge(sum_copied, NS * NC)
            pe.wait_ge(n3T_copied, 2 * NC)
            queries(0)
            score(0, 0)
            chunk_b(0, no_mlp)
            with pe.Fori(1, NC - 1) as c:
                chunk_b(c, mlp_before(c))
            chunk_b(NC - 1, mlp_before(NC - 1), last=True)
            pe.wait_ge(x3_done, 4 * NC)
            turn_n2(2 * NC - 1)
            cell_x(2 * NC - 1, 0)
            for b in range(1, B):
                cell_x(2 * NC - 1, b)
                if b < B - 1:
                    hidden_x(2 * NC - 1, b - 1)
                cell_c(2 * NC - 1, b)
            hidden_c(2 * NC - 1)

        @block.vector
        def _(dve):
            def norm_stats(L, M, src, ready, implied=False):
                if not implied:
                    wait(dve, L.norm_done, 4 * M)
                for b in range(B):
                    ready(b)
                    dve.bn_stats(L.stats[:, b, :], src(b)).then_inc(L.stat_done, 1)
                dve.wait_ge(L.stat_done, 4 * (M + 1))
                if not implied:
                    wait(dve, L.settled, M)
                dve.tensor_copy(L.last[:, :], L.stats[:, B - 1, 0:1]).then_inc(L.settled, 1)
                for b in range(B):
                    dve.bn_aggr(L.mv[:, b, :], L.stats[:, b, :]).then_inc(L.mv_done, 1)

            def tile(t):
                return lambda b: t[:, b, :]

            def consts():
                dve.wait_ge(w_loaded, NW * DMA)
                dve.tensor_scalar(hcol[:, 0:4], col[:, LNG:LNG + 4], 0.5, None, ALU.mult).then_inc(dve_const, 1)
                dve.tensor_scalar(hcol[:, 4:8], col[:, BF:BF + 4], 0.5, None, ALU.mult).then_inc(dve_const, 1)
                dve.tensor_scalar(w_c[:, :, :], w_c[:, :, :], 0.5, None, ALU.mult).then_inc(dve_const, 1)
                dve.tensor_scalar(c_init[:, :], col[:, INC:INC + 2], 2.0, None, ALU.mult).then_inc(dve_const, 1)

            def x_stats(m):
                norm_stats(ln_x, m, tile(xin), lambda b: dve.wait_ge(x_loaded, DMA * (m + 1)))

            def square_sums(m, b):
                dve.wait_ge(sq_done, 4 * m + b + 1)
                wait(dve, ssmax_done, m)
                dve.tensor_reduce(ss[:, b * 32:(b + 1) * 32], sq[:, b % 2, :].rearrange("p (h i) -> p h i", i=D),
                                  AX.X, ALU.add).then_inc(ss_done, 1)

            def head_guard(m):
                dve.wait_ge(ss_done, 4 * (m + 1))
                wait(dve, qkn_done, m)
                dve.tensor_scalar(rn[:, :], ss[:, :], 1e-24, None, ALU.max).then_inc(ssmax_done, 1)

            def make_beta(m):
                dve.wait_ge(bt_done, m + 1)
                wait(dve, kb_done, m)
                dve.tensor_scalar(beta[:, :], bt[:, :], 0.5, 0.5, ALU.mult, ALU.add).then_inc(beta_done, 1)

            def make_gate(m, ft):
                dve.wait_ge(tg_done, 2 * m + ft + 1)
                dve.scalar_tensor_tensor(out=gate[:, ft, :], in0=gate[:, ft, :], scalar=1.0, in1=PB[:, 1 - ft, :],
                                         op0=ALU.add, op1=ALU.mult).then_inc(gate_done, 1)

            def head_recip(m):
                dve.wait_ge(norm_sqrt, m + 1)
                dve.reciprocal(rn[:, :], rn[:, :]).then_inc(rn_done, 1)

            def scale_qk(m):
                dve.wait_ge(rn_done, m + 1)
                dve.wait_ge(qk_copied, 4 * (m + 1))
                v = qk[:, :, :].rearrange("p b (h i) -> p (b h) i", i=D)
                dve.tensor_tensor(v, v, rn[:, :].unsqueeze(2).broadcast_to([P, B * 2 * NH, D]),
                                  ALU.mult).then_inc(qkn_done, 1)

            def views(w, s):
                return pair_views(lay, s // 2, w, (s % 2) * SUB), shifted_views(lay, s // 2, w, (s % 2) * SUB)

            def inputs(m, s):
                v, _ = views(V_, s)
                _, b_sh = views(KB_, s)
                dve.wait_ge(lay_loaded[s // 2], 3 * DMA * (m + 1))
                wait(dve, sum_done, NS * m + s - 1)
                dve.tensor_tensor(pairs_out(st, s % 2, 0, ND), v(0, ND), b_sh(0, ND), ALU.mult).then_inc(inp_done, 1)

            def scan(m, s, mirror):
                n, par = NS * m + s, s % 2
                if not mirror:
                    dve.wait_ge(dec_done, n + 1)
                    dve.wait_ge(inp_done, n + 1)
                    wait(dve, carried, n)
                else:
                    dve.wait_ge(mirror_done, n + 1)
                a = dec[:, par, NI:NI + MIR, :] if mirror else dec[:, par, :, :]
                v = st[:, par, U:PAIRS, :] if mirror else st[:, par, 0:U, :]
                a, v = a.rearrange("p r t -> p (r t)"), v.rearrange("p r t -> p (r t)")
                dve.tensor_tensor_scan(v, a, v, 0.0, ALU.mult, ALU.add).then_inc(scan_done, 1)

            def carry(m, s):
                n, par = NS * m + s, s % 2
                dve.wait_ge(scan_done, 2 * n + 2)
                dve.tensor_copy(st[:, 1 - par, :, 0:1], st[:, par, :, SUB:COL]).then_inc(carried, 1)

            def outputs(m, s, mirror):
                q, q_sh = views(Q_, s)
                if not mirror:
                    dve.wait_ge(carried, NS * m + s + 1)
                    v = pairs_out(st, s % 2, 0, ND)
                    dve.tensor_tensor(v, v, q_sh(0, ND), ALU.mult).then_inc(prod_done, 1)
                else:
                    v = pairs_out(st, s % 2, U, ND - 2)
                    dve.tensor_tensor(v, v, q(1, ND - 1), ALU.mult).then_inc(prod_done, 1)

            def o_tile(b):
                return QB[:, b // 2, (b % 2) * HID:(b % 2 + 1) * HID]

            def o_stats(m):
                norm_stats(ln_o, m, o_tile, lambda b: dve.wait_ge(oT_done, 2 * m + b // 2 + 1))

            def add_y(m):
                dve.wait_ge(xr_loaded, DMA * (m + 1))
                for j in range(2):
                    dve.wait_ge(y_mm, 2 * m + j + 1)
                    v = xr[:, 2 * j:2 * j + 2, :].rearrange("p b d -> p (b d)")
                    dve.tensor_tensor(v, v, QB[:, j, :], ALU.add).then_inc(x1_done, 1)

            def n2_stats(m):
                norm_stats(ln_2, m, tile(xr), lambda b: dve.wait_ge(x1_done, 2 * m + b // 2 + 1))

            def rest_keys(b, c0, c1):
                n = 2 * b if c0 == 0 else 2 * B + 2 * b
                t = slice(c0 * P, c1 * P)
                dve.wait_ge(hi_done, n + 1)
                dve.tensor_tensor(keys_lo[:, :, b, t], keys_lo[:, :, b, t].bitcast(F32),
                                  keys_hi[:, :, b, t].bitcast(F32), ALU.subtract).then_inc(split_done, 1)
                dve.wait_ge(hi_done, n + 2)
                dve.tensor_tensor(vals_lo[:, b, c0:c1], vals_lo[:, b, c0:c1].bitcast(F32),
                                  vals_hi[:, b, c0:c1].bitcast(F32), ALU.subtract).then_inc(split_done, 1)

            def cell(M, b):
                dve.wait_ge(cell_act, 24 * M + 6 * b + 2)
                wait(dve, c_done, 4 * M + b)
                if b == 0:
                    before = c_init[:, :].unsqueeze(2).broadcast_to([P, KT, P])
                else:
                    before = cc[:, :, :]
                forget = gt[:, 0, :].rearrange("p (k t) -> p k t", k=KT)
                dve.scalar_tensor_tensor(out=forget, in0=forget, scalar=1.0, in1=before,
                                         op0=ALU.add, op1=ALU.mult).then_inc(cell_h, 1)
                dve.wait_ge(cell_act, 24 * M + 6 * b + 6)
                dve.scalar_tensor_tensor(out=gt[:, 1, :], in0=gt[:, 1, :], scalar=1.0, in1=gt[:, 2, :],
                                         op0=ALU.add, op1=ALU.mult).then_inc(cell_h, 1)
                dve.wait_ge(cell_h, 8 * M + 2 * b + 2)
                if b == 0:
                    wait(dve, u_mm, M)
                dve.scalar_tensor_tensor(out=cc[:, :, :].rearrange("p k t -> p (k t)"), in0=gt[:, 0, :], scalar=0.5,
                                         in1=gt[:, 1, :], op0=ALU.mult, op1=ALU.add).then_inc(c_done, 1)
                if b and isinstance(M, int) and M == NC - 1:
                    rest_keys(b - 1, 0, NC - 2)

            def hidden_sum(M):
                dve.wait_ge(u_copied, M + 1)
                wait(dve, x2_done, 2 * M)
                for j in range(2):
                    dve.wait_ge(h_mm, 2 * M + j + 1)
                    dve.tensor_tensor(hh[:, j, :].rearrange("p (b d) -> p b d", b=2),
                                      QB[:, j, :].rearrange("p (b d) -> p b d", b=2),
                                      hu[:, :].unsqueeze(1).broadcast_to([P, 2, HID]),
                                      ALU.add).then_inc(h_sum, 1)
                if isinstance(M, int) and M == NC - 1:
                    rest_keys(B - 1, 0, NC - 2)

            def hidden_sum_a(m):
                wait(dve, v_stored, DMA * m)
                hidden_sum(m)

            def n3_stats(m):
                norm_stats(ln_3, m, tile(xr), lambda b: dve.wait_ge(x2_done, 2 * m + b // 2 + 1), implied=True)

            def one(i, pre, main, post, keys_):
                post(inputs, 2)
                post(scan, 2, False)
                post(scan, 2, True)
                post(carry, 2)
                keys_(cell, 0)
                post(outputs, 2, False)
                post(outputs, 2, True)
                post(inputs, 3)
                keys_(cell, 1)
                post(scan, 3, False)
                pre(x_stats)
                keys_(cell, 2)
                post(scan, 3, True)
                post(carry, 3)
                post(outputs, 3, False)
                keys_(cell, 3)
                post(outputs, 3, True)
                keys_(hidden_sum_a)
                keys_(n3_stats)
                main(inputs, 0)
                main(scan, 0, False)
                main(scan, 0, True)
                main(carry, 0)
                pre(square_sums, 0)
                main(outputs, 0, False)
                main(outputs, 0, True)
                pre(square_sums, 1)
                main(inputs, 1)
                pre(square_sums, 2)
                pre(square_sums, 3)
                pre(head_guard)
                post(o_stats)
                main(scan, 1, False)
                main(scan, 1, True)
                pre(make_beta)
                main(carry, 1)
                pre(head_recip)
                main(outputs, 1, False)
                pre(make_gate, 0)
                pre(make_gate, 1)
                pre(scale_qk)
                post(add_y)
                post(n2_stats)
                main(outputs, 1, True)
                if isinstance(i, int) and i == -1:
                    consts()
                    dve.wait_ge(wb_mm, 5)
                    dve.tensor_tensor(y_row[:, :], row[:, HID:2 * HID], QB[0:1, 1, 0:HID], ALU.add).then_inc(y_row_done, 1)
                    dve.wait_ge(wb_mm, 6)
                    dve.tensor_tensor(bias0[:, :], col[:, BF:BF + 3 * KT], QB[:, 0, 32:32 + 3 * KT],
                                      ALU.add).then_inc(first_bias, 1)
                    dve.wait_ge(first_bias, 1)
                    dve.tensor_scalar(bias0[:, 0:2 * KT], bias0[:, 0:2 * KT], 0.5, None, ALU.mult).then_inc(first_bias, 1)

            def row_max(c, b):
                n = 4 * c + b
                m_ = mx[:, b % 2, :]
                dve.wait_ge(score_mm, n + 1)
                wait(dve, recip_done, n - 1)
                dve.tensor_reduce(m_[:, 0:1], JB[:, :, :], AX.XY, ALU.max).then_inc(max_done, 1)
                dve.wait_ge(max_done, n + 1)
                dve.tensor_tensor(m_[:, 1:2], m_[:, 0:1], rq[:, b:b + 1], ALU.add).then_inc(bias_step, 1)
                dve.wait_ge(bias_step, 2 * n + 1)
                dve.tensor_tensor(m_[:, 1:2], rq[:, b:b + 1], m_[:, 1:2], ALU.subtract).then_inc(bias_step, 1)
                dve.wait_ge(bias_step, 2 * n + 2)
                dve.tensor_scalar(m_[:, 2:3], m_[:, 1:2], SCALE, None, ALU.mult).then_inc(bias_done, 1)

            def rest_prob(c, b):
                n = 4 * c + b
                for j in range(2):
                    dve.wait_ge(pt_act, 2 * n + j + 1)
                    wait(dve, pv_mm, n)
                    dve.tensor_tensor(probT_lo[:, 4 * j:4 * j + 4, :], PB[:, j, :].rearrange("p (j q) -> p j q", j=4),
                                      probT_hi[:, 4 * j:4 * j + 4, :].bitcast(F32), ALU.subtract).then_inc(pt_lo, 1)

            def rest_q(c):
                for et in range(KT):
                    dve.wait_ge(q_copied, 2 * c + et + 1)
                    wait(dve, score_mm, 4 * c)
                    dve.scalar_tensor_tensor(out=qT_lo[:, et, :], in0=PB[:, et, :], scalar=q_bias[:, et:et + 1],
                                             in1=qT_hi[:, et, :].bitcast(F32), op0=ALU.add,
                                             op1=ALU.subtract).then_inc(q_lo, 1)

            def add_attended(c, b):
                n = 4 * c + b
                dve.wait_ge(exp_done, n + 1)
                dve.reciprocal(mx[:, b % 2, 4:5], mx[:, b % 2, 3:4]).then_inc(recip_done, 1)
                dve.wait_ge(recip_done, n + 1)
                dve.wait_ge(xa_loaded, DMA * (c + 1))
                dve.wait_ge(pv_mm, n + 1)
                dve.scalar_tensor_tensor(out=xa[:, b, :], in0=QB[:, b % 2, 0:HID], scalar=mx[:, b % 2, 4:5],
                                         in1=xa[:, b, :], op0=ALU.mult, op1=ALU.add).then_inc(x3_done, 1)

            def copy_rq(c):
                dve.wait_ge(rq_mm, c + 1)
                wait(dve, bias_done, 4 * c)
                dve.tensor_copy(rq[:, :], PB[:, 0, 0:B]).then_inc(rq_done, 1)
                dve.wait_ge(rq_done, c + 1)

            def xa_stats(M):
                norm_stats(ln_2, M, tile(xa), lambda b: dve.wait_ge(x3_done, 4 * (M - NC) + b + 1))

            def chunk_b(c, mlp_of, last=False):
                mlp_of(xa_stats)
                rest_prob(c, 0)
                row_max(c, 1)
                rest_prob(c, 1)
                add_attended(c, 0)
                add_attended(c, 1)
                row_max(c, 2)
                rest_prob(c, 2)
                mlp_of(cell, 0)
                row_max(c, 3)
                mlp_of(cell, 1)
                mlp_of(cell, 2)
                rest_prob(c, 3)
                add_attended(c, 2)
                if not last:
                    rest_q(c + 1)
                mlp_of(cell, 3)
                if not last:
                    copy_rq(c + 1)
                    row_max(c + 1, 0)
                add_attended(c, 3)
                mlp_of(hidden_sum)

            rounds(dve, one)
            rest_q(0)
            copy_rq(0)
            for b in range(B):
                rest_keys(b, NC - 2, NC)
                if b == 0:
                    row_max(0, 0)
            chunk_b(0, no_mlp)
            with dve.Fori(1, NC - 1) as c:
                chunk_b(c, mlp_before(c))
            chunk_b(NC - 1, mlp_before(NC - 1), last=True)
            xa_stats(2 * NC - 1)
            for b in range(B):
                cell(2 * NC - 1, b)
            hidden_sum(2 * NC - 1)


def _lay_view(lay, hf, w, t, pattern, first):
    base = lay[:, hf, w, first:first + 1, t:t + SUB]
    return bass.AP(base.tensor, base.offset, [list(base.ap[0])] + pattern)


def pair_views(lay, hf, w, t):
    return lambda d0, nd: _lay_view(lay, hf, w, t, [[0, nd if d0 == 0 else nd - d0], [HALF, NI], [1, SUB]], 0)


def shifted_views(lay, hf, w, t):
    return lambda d0, nd: _lay_view(lay, hf, w, t, [[HALF, nd if d0 == 0 else nd - d0], [HALF, NI], [1, SUB]], d0)


def pairs_out(buf, par, at, nd):
    return buf[:, par, at:at + nd * NI, 1:COL].rearrange("p (d i) t -> p d i t", i=NI)


def kernel(**inputs):
    import numpy as np
    import concourse.bacc as bacc
    from concourse.bass_utils import run_bass_kernel_spmd

    f = {k: np.asarray(v) for k, v in inputs.items()}
    a = lambda n: f["L0_attn_a_" + n]
    b = lambda n: f["L0_attn_b_" + n]
    w = lambda n: f["L0_ffn_" + n]
    cols = [a("ln_g"), a("ln_b"), w("bf"), w("bi"), w("bc"), w("in_c"), b("b_q"), b("b_k"), b("b_v")]
    arrays = {
        "x": a("x"),
        "wqkvg": np.concatenate([a("Wq"), a("Wk"), a("Wv"), a("Wg")], axis=1),
        "wbeta": a("Wbeta"),
        "wout": a("Wout"),
        "cols": np.concatenate([v.reshape(KT, P).T for v in cols], axis=1),
        "rows": np.concatenate([w("bo"), b("b_out"), np.ones(P, np.float32)])[None, :],
        "wx": np.concatenate([w("wf").T, w("wi").T, w("wc").T, w("wo").T], axis=1),
        "wc": np.concatenate([w("uf").T, w("ui").T, w("uc").T, w("uo").T], axis=1),
        "wattn": np.stack([b("w_q"), b("w_k"), b("w_v"), b("w_out").T]),
        "ident": np.eye(P, dtype=np.float32),
    }
    arrays = {k: np.ascontiguousarray(v) for k, v in arrays.items()}
    nc = bacc.Bacc("TRN2", target_bir_lowering=False, num_devices=1)
    args = [nc.dram_tensor("in_" + k, v.shape, mybir.dt.from_np(v.dtype), kind="ExternalInput").ap() for k, v in arrays.items()]
    out = nc.dram_tensor("out", (B, S, HID), F32, kind="ExternalOutput").ap()
    block_kernel(nc, *args, out)
    r = run_bass_kernel_spmd(nc, [{"in_" + k: v for k, v in arrays.items()}], core_ids=[0])
    return r.results[0]["out"]
```
